# Optimizing a Trainium2 kernel written in Bass

```python
import numpy as np
import jax
import jax.numpy as jnp

def _softmax(x, axis=-1):
    return jax.nn.softmax(x, axis=axis)
def _gelu(x):
    return jax.nn.gelu(x, approximate=True)
def _silu(x):
    return jax.nn.silu(x)
def _sigmoid(x):
    return jax.nn.sigmoid(x)
def _layernorm(x, axis=-1, eps=1e-5):
    m = jnp.mean(x, axis=axis, keepdims=True)
    v = jnp.var(x, axis=axis, keepdims=True)
    return (x - m) / jnp.sqrt(v + eps)
def _scatter_add(tgt, idx, src, axis=0):
    return tgt.at[idx].add(src)
def _segment_sum(src, seg, n):
    return jax.ops.segment_sum(src, seg, n)

kernel_name = 'mk_conv_preact_d4_conv_nhwc256_c3c472'

def setup_inputs(seed: int = 0):
    np.random.seed(seed)
    _w = jnp.asarray
    def _rec_inputs():
        import jax
        import jax.numpy as jnp
        _gk = jax.random.key(seed)
        x = -0.000929 + 1 * jax.random.normal(jax.random.fold_in(_gk, 1), (1, 64, 64, 256), jnp.float32)
        return x
    x = _rec_inputs()
    def _L0_conv_setup():
        import jax, jax.numpy as jnp
        import numpy as np
        from jax import lax
        B, H, W, C, NH = (1, 64, 64, 256, 8)
        DN = ('NCHW', 'OIHW', 'NCHW')

        def _conv(x, w, pad, groups=1):
            return lax.conv_general_dilated(x, w, window_strides=(1, 1), padding=[(pad, pad), (pad, pad)], dimension_numbers=DN, feature_group_count=groups)
        key = jax.random.key(seed)
        ks = jax.random.split(key, 7)
        s = 0.05
        return {'x': jax.random.normal(ks[0], (B, H, W, C), jnp.float32), 'W1': jax.random.normal(ks[1], (C, C, 1, 1), jnp.float32) * s, 'W3': jax.random.normal(ks[2], (C, C, 3, 3), jnp.float32) * s, 'W5': jax.random.normal(ks[3], (C, C, 5, 5), jnp.float32) * s, 'Wdw': jax.random.normal(ks[4], (3 * C, 1, 3, 3), jnp.float32) * s, 'Wproj': jax.random.normal(ks[5], (C, C, 1, 1), jnp.float32) * s, 'temperature': jnp.ones((NH, 1, 1), jnp.float32)}
    _L0_conv_all = _L0_conv_setup()
    _L0_conv_in = {k: v for k, v in _L0_conv_all.items() if k in ('W1', 'W3', 'W5', 'Wdw', 'Wproj', 'temperature', )}
    del _L0_conv_all

    def _L1_conv_setup():
        import jax, jax.numpy as jnp
        import numpy as np

        def encode(x, embeddings):
            xf = x.reshape(-1, x.shape[-1])
            dis = jnp.sum(xf * xf, axis=-1, keepdims=True) + jnp.sum(embeddings * embeddings, axis=0, keepdims=True) - 2.0 * jnp.matmul(xf, embeddings)
            indices = jnp.argmin(dis, axis=-1)
            return indices.reshape(x.shape[:-1])

        def decode(indices, embeddings):
            return jnp.take(embeddings.T, indices, axis=0)
        key = jax.random.key(seed)
        k1, k2 = jax.random.split(key)
        B, H, W, D, K = (16, 64, 64, 256, 1024)
        x = jax.random.normal(k1, (B, H, W, D), dtype=jnp.float32)
        limit = np.sqrt(3.0 / D).astype(np.float32)
        embeddings = jax.random.uniform(k2, (D, K), dtype=jnp.float32, minval=-limit, maxval=limit)
        return {'x': x, 'embeddings': embeddings}
    _L1_conv_all = _L1_conv_setup()
    _L1_conv_in = {k: v for k, v in _L1_conv_all.items() if k in ('embeddings', )}
    del _L1_conv_all

    def _L2_conv_setup():
        import jax, jax.numpy as jnp
        import numpy as np
        DIM = 256
        HEADS = 8
        HD = DIM // HEADS
        WS = 8
        NEXP = 8
        HID = 128
        SCALE = HD ** (-0.5)

        def _window_partition(x, ws):
            B, H, W, C = x.shape
            x = x.reshape(B, H // ws, ws, W // ws, ws, C)
            return x.transpose(0, 1, 3, 2, 4, 5).reshape(-1, ws, ws, C)

        def _window_reverse(w, ws, B, H, W):
            C = w.shape[-1]
            x = w.reshape(B, H // ws, W // ws, ws, ws, C)
            return x.transpose(0, 1, 3, 2, 4, 5).reshape(B, H, W, C)

        def _rope2(x):
            B, Wh, Ww, d = x.shape
            d2 = d // 2

            def angles(L, dd):
                inv = 1.0 / 10000.0 ** (jnp.arange(0, dd, 2, dtype=jnp.float32) / dd)
                return jnp.arange(L, dtype=jnp.float32)[:, None] * inv[None, :]

            def rotate(v, ang, bshape):
                p = v.reshape(*v.shape[:-1], -1, 2)
                c = jnp.cos(ang).reshape(bshape)
                s = jnp.sin(ang).reshape(bshape)
                o0 = p[..., 0] * c - p[..., 1] * s
                o1 = p[..., 0] * s + p[..., 1] * c
                return jnp.stack([o0, o1], axis=-1).reshape(v.shape)
            ah = angles(Wh, d2)
            aw = angles(Ww, d2)
            xh = rotate(x[..., :d2], ah, (1, Wh, 1, d2 // 2))
            xw = rotate(x[..., d2:], aw, (1, 1, Ww, d2 // 2))
            return jnp.concatenate([xh, xw], axis=-1)

        def _moe_linear(xf, routes, w, b):
            out = jnp.zeros((xf.shape[0], w.shape[1]), xf.dtype)
            for i in range(w.shape[0]):
                y = xf @ w[i].T + b[i]
                out = jnp.where((routes == i)[:, None], y, out)
            return out
        key = jax.random.key(seed)
        ks = jax.random.split(key, 8)
        sc = 0.02
        return {'x': jax.random.normal(ks[0], (8, 64, 64, DIM), jnp.float32), 'router_w1': jax.random.normal(ks[1], (HID, DIM), jnp.float32) * sc, 'router_b1': jnp.zeros((HID,), jnp.float32), 'router_w2': jax.random.normal(ks[2], (NEXP, HID), jnp.float32) * sc, 'router_b2': jnp.zeros((NEXP,), jnp.float32), 'qkv_w': jax.random.normal(ks[3], (NEXP, 3 * DIM, DIM), jnp.float32) * sc, 'qkv_b': jnp.zeros((NEXP, 3 * DIM), jnp.float32), 'proj_w': jax.random.normal(ks[4], (NEXP, DIM, DIM), jnp.float32) * sc, 'proj_b': jnp.zeros((NEXP, DIM), jnp.float32)}
    _L2_conv_all = _L2_conv_setup()
    _L2_conv_in = {k: v for k, v in _L2_conv_all.items() if k in ('router_w1', 'router_b1', 'router_w2', 'router_b2', 'qkv_w', 'qkv_b', 'proj_w', 'proj_b', )}
    del _L2_conv_all

    def _L3_conv_setup():
        import jax, jax.numpy as jnp
        import numpy as np
        from jax import lax
        EXPAND = 64
        CHANNELS = 256

        def _conv(A, W, padding):
            return lax.conv_general_dilated(A, W, (1, 1), padding, dimension_numbers=('NHWC', 'HWIO', 'NHWC'))
        key = jax.random.key(seed)
        ks = jax.random.split(key, 7)
        x = jax.random.normal(ks[0], (16, 64, 64, 256), dtype=jnp.float32)
        s = 0.05
        w1 = jax.random.normal(ks[1], (1, 1, CHANNELS, EXPAND), dtype=jnp.float32) * s
        b1 = jax.random.normal(ks[2], (1, 1, 1, EXPAND), dtype=jnp.float32) * s
        w2 = jax.random.normal(ks[3], (3, 3, CHANNELS, EXPAND), dtype=jnp.float32) * s
        b2 = jax.random.normal(ks[4], (1, 1, 1, EXPAND), dtype=jnp.float32) * s
        w3 = jax.random.normal(ks[5], (1, 1, CHANNELS, 1), dtype=jnp.float32) * s
        b3 = jax.random.normal(ks[6], (1, 1, 1, 1), dtype=jnp.float32) * s
        return {'x': x, 'w1': w1, 'b1': b1, 'w2': w2, 'b2': b2, 'w3': w3, 'b3': b3}
    _L3_conv_all = _L3_conv_setup()
    _L3_conv_in = {k: v for k, v in _L3_conv_all.items() if k in ('w1', 'b1', 'w2', 'b2', 'w3', 'b3', )}
    del _L3_conv_all

    return {
        "x": x,
        "L0_conv_W1": _L0_conv_in["W1"],
        "L0_conv_W3": _L0_conv_in["W3"],
        "L0_conv_W5": _L0_conv_in["W5"],
        "L0_conv_Wdw": _L0_conv_in["Wdw"],
        "L0_conv_Wproj": _L0_conv_in["Wproj"],
        "L0_conv_temperature": _L0_conv_in["temperature"],
        "L1_conv_embeddings": _L1_conv_in["embeddings"],
        "L2_conv_router_w1": _L2_conv_in["router_w1"],
        "L2_conv_router_b1": _L2_conv_in["router_b1"],
        "L2_conv_router_w2": _L2_conv_in["router_w2"],
        "L2_conv_router_b2": _L2_conv_in["router_b2"],
        "L2_conv_qkv_w": _L2_conv_in["qkv_w"],
        "L2_conv_qkv_b": _L2_conv_in["qkv_b"],
        "L2_conv_proj_w": _L2_conv_in["proj_w"],
        "L2_conv_proj_b": _L2_conv_in["proj_b"],
        "L3_conv_w1": _L3_conv_in["w1"],
        "L3_conv_b1": _L3_conv_in["b1"],
        "L3_conv_w2": _L3_conv_in["w2"],
        "L3_conv_b2": _L3_conv_in["b2"],
        "L3_conv_w3": _L3_conv_in["w3"],
        "L3_conv_b3": _L3_conv_in["b3"],
    }

def reference(x, L0_conv_W1, L0_conv_W3, L0_conv_W5, L0_conv_Wdw, L0_conv_Wproj, L0_conv_temperature, L1_conv_embeddings, L2_conv_router_w1, L2_conv_router_b1, L2_conv_router_w2, L2_conv_router_b2, L2_conv_qkv_w, L2_conv_qkv_b, L2_conv_proj_w, L2_conv_proj_b, L3_conv_w1, L3_conv_b1, L3_conv_w2, L3_conv_b2, L3_conv_w3, L3_conv_b3):
    import jax
    import jax.numpy as jnp
    def _L0_conv_ref(x, W1, W3, W5, Wdw, Wproj, temperature):
        import jax, jax.numpy as jnp
        import numpy as np
        from jax import lax
        B, H, W, C, NH = (1, 64, 64, 256, 8)
        DN = ('NCHW', 'OIHW', 'NCHW')

        def _conv(x, w, pad, groups=1):
            return lax.conv_general_dilated(x, w, window_strides=(1, 1), padding=[(pad, pad), (pad, pad)], dimension_numbers=DN, feature_group_count=groups)
        b, h, w, c = x.shape
        xc = jnp.transpose(x, (0, 3, 1, 2))
        qkv = jnp.concatenate([_conv(xc, W1, 0), _conv(xc, W3, 1), _conv(xc, W5, 2)], axis=1)
        qkv = _conv(qkv, Wdw, 1, groups=3 * c)
        q, k, v = jnp.split(qkv, 3, axis=1)

        def heads(t):
            return jnp.transpose(t.reshape(b, NH, c // NH, h * w), (0, 1, 3, 2))
        q, k, v = (heads(q), heads(k), heads(v))

        def l2n(t):
            n = jnp.sqrt(jnp.sum(t * t, axis=-1, keepdims=True))
            return t / jnp.maximum(n, 1e-12)
        q, k = (l2n(q), l2n(k))
        attn = jnp.einsum('bhnc,bhmc->bhnm', q, k) * temperature
        attn = jax.nn.softmax(attn, axis=-1)
        o = jnp.einsum('bhnm,bhmc->bhnc', attn, v)
        o = jnp.transpose(o, (0, 1, 3, 2)).reshape(b, c, h, w)
        o = _conv(o, Wproj, 0)
        return jnp.transpose(o, (0, 2, 3, 1))

    def _L1_conv_ref(x, embeddings):
        import jax, jax.numpy as jnp
        import numpy as np

        def encode(x, embeddings):
            xf = x.reshape(-1, x.shape[-1])
            dis = jnp.sum(xf * xf, axis=-1, keepdims=True) + jnp.sum(embeddings * embeddings, axis=0, keepdims=True) - 2.0 * jnp.matmul(xf, embeddings)
            indices = jnp.argmin(dis, axis=-1)
            return indices.reshape(x.shape[:-1])

        def decode(indices, embeddings):
            return jnp.take(embeddings.T, indices, axis=0)
        indices = encode(x, embeddings)
        quantized = decode(indices, embeddings)
        return quantized

    def _L2_conv_ref(x, router_w1, router_b1, router_w2, router_b2, qkv_w, qkv_b, proj_w, proj_b):
        import jax, jax.numpy as jnp
        import numpy as np
        DIM = 256
        HEADS = 8
        HD = DIM // HEADS
        WS = 8
        NEXP = 8
        HID = 128
        SCALE = HD ** (-0.5)

        def _window_partition(x, ws):
            B, H, W, C = x.shape
            x = x.reshape(B, H // ws, ws, W // ws, ws, C)
            return x.transpose(0, 1, 3, 2, 4, 5).reshape(-1, ws, ws, C)

        def _window_reverse(w, ws, B, H, W):
            C = w.shape[-1]
            x = w.reshape(B, H // ws, W // ws, ws, ws, C)
            return x.transpose(0, 1, 3, 2, 4, 5).reshape(B, H, W, C)

        def _rope2(x):
            B, Wh, Ww, d = x.shape
            d2 = d // 2

            def angles(L, dd):
                inv = 1.0 / 10000.0 ** (jnp.arange(0, dd, 2, dtype=jnp.float32) / dd)
                return jnp.arange(L, dtype=jnp.float32)[:, None] * inv[None, :]

            def rotate(v, ang, bshape):
                p = v.reshape(*v.shape[:-1], -1, 2)
                c = jnp.cos(ang).reshape(bshape)
                s = jnp.sin(ang).reshape(bshape)
                o0 = p[..., 0] * c - p[..., 1] * s
                o1 = p[..., 0] * s + p[..., 1] * c
                return jnp.stack([o0, o1], axis=-1).reshape(v.shape)
            ah = angles(Wh, d2)
            aw = angles(Ww, d2)
            xh = rotate(x[..., :d2], ah, (1, Wh, 1, d2 // 2))
            xw = rotate(x[..., d2:], aw, (1, 1, Ww, d2 // 2))
            return jnp.concatenate([xh, xw], axis=-1)

        def _moe_linear(xf, routes, w, b):
            out = jnp.zeros((xf.shape[0], w.shape[1]), xf.dtype)
            for i in range(w.shape[0]):
                y = xf @ w[i].T + b[i]
                out = jnp.where((routes == i)[:, None], y, out)
            return out
        Bs, H, W, C = x.shape
        xf = x.reshape(-1, C)
        h = jax.nn.relu(xf @ router_w1.T + router_b1)
        router_logits = h @ router_w2.T + router_b2
        router_probs = jax.nn.softmax(router_logits, axis=-1)
        route_prob_max = jnp.max(router_probs, axis=-1)
        routes = jnp.argmax(router_probs, axis=-1)
        qkv = _moe_linear(xf, routes, qkv_w, qkv_b)
        qkv = qkv.reshape(Bs, H, W, 3 * C)
        qw = _window_partition(qkv, WS).reshape(-1, WS * WS, 3 * C)
        B_, N, _ = qw.shape
        qkv5 = qw.reshape(B_, N, 3, HEADS, HD).transpose(2, 0, 3, 1, 4)
        q, k, v = (qkv5[0], qkv5[1], qkv5[2])
        q = _rope2(q.reshape(-1, WS, WS, HD)).reshape(B_, HEADS, N, HD)
        k = _rope2(k.reshape(-1, WS, WS, HD)).reshape(B_, HEADS, N, HD)
        attn = jax.nn.softmax(q * SCALE @ k.swapaxes(-2, -1), axis=-1)
        out = (attn @ v).swapaxes(1, 2).reshape(B_, N, C)
        out = _window_reverse(out.reshape(-1, WS, WS, C), WS, Bs, H, W)
        of = _moe_linear(out.reshape(-1, C), routes, proj_w, proj_b)
        of = of * route_prob_max[:, None]
        return of.reshape(Bs, H, W, C)

    def _L3_conv_ref(x, w1, b1, w2, b2, w3, b3):
        import jax, jax.numpy as jnp
        import numpy as np
        from jax import lax
        EXPAND = 64
        CHANNELS = 256

        def _conv(A, W, padding):
            return lax.conv_general_dilated(A, W, (1, 1), padding, dimension_numbers=('NHWC', 'HWIO', 'NHWC'))
        depth_batch = CHANNELS // EXPAND

        def step1(A, i):
            Z = _conv(A, w1, 'VALID') + b1
            A = lax.dynamic_update_slice(A, Z, (0, 0, 0, i * EXPAND))
            return (A, None)

        def step2(A, i):
            Z = _conv(A, w2, 'SAME') + b2
            A = lax.dynamic_update_slice(A, Z, (0, 0, 0, i * EXPAND))
            return (A, None)

        def step3(A, i):
            Z = _conv(A, w3, 'VALID') + b3
            A = lax.dynamic_update_slice(A, Z, (0, 0, 0, i))
            return (A, None)
        A = x
        A, _ = lax.scan(step1, A, jnp.arange(depth_batch))
        A = jax.nn.relu(A)
        A, _ = lax.scan(step2, A, jnp.arange(depth_batch))
        A = jax.nn.relu(A)
        A, _ = lax.scan(step3, A, jnp.arange(CHANNELS))
        return A + x

    def _gn(v, G=32, eps=1e-5):
        B_, H_, W_, C_ = v.shape
        g = v.reshape(B_, H_, W_, G, C_ // G)
        m = jnp.mean(g, axis=(1, 2, 4), keepdims=True)
        s = jnp.var(g, axis=(1, 2, 4), keepdims=True)
        return ((g - m) / jnp.sqrt(s + eps)).reshape(v.shape)

    def _ln_c(v, eps=1e-6):
        m = jnp.mean(v, axis=-1, keepdims=True)
        s = jnp.var(v, axis=-1, keepdims=True)
        return (v - m) / jnp.sqrt(s + eps)

    def _ln_t(v, eps=1e-5):
        m = jnp.mean(v, axis=-1, keepdims=True)
        s = jnp.var(v, axis=-1, keepdims=True)
        return (v - m) / jnp.sqrt(s + eps)

    def _to_tokens(v):
        B_, H_, W_, C_ = v.shape
        return v.reshape(B_, H_ * W_, C_)
    def _from_tokens(t, like):
        return t.reshape(like.shape)

    x = x + _L0_conv_ref(_gn(x), L0_conv_W1, L0_conv_W3, L0_conv_W5, L0_conv_Wdw, L0_conv_Wproj, L0_conv_temperature)
    x = x + _L1_conv_ref(_gn(x), L1_conv_embeddings)
    x = x + _L2_conv_ref(_gn(x), L2_conv_router_w1, L2_conv_router_b1, L2_conv_router_w2, L2_conv_router_b2, L2_conv_qkv_w, L2_conv_qkv_b, L2_conv_proj_w, L2_conv_proj_b)
    x = x + _L3_conv_ref(_gn(x), L3_conv_w1, L3_conv_b1, L3_conv_w2, L3_conv_b2, L3_conv_w3, L3_conv_b3)
    return x


_drawn_inputs = setup_inputs


def setup_inputs(seed=0):
    import zlib

    import numpy as np

    out = dict(_drawn_inputs(seed))
    spreads = {'L0_conv_temperature': (1.0, 0.6),
     'L2_conv_router_b1': (0.0, 0.8),
     'L2_conv_router_b2': (0.0, 0.51),
     'L2_conv_qkv_b': (0.0, 0.8),
     'L2_conv_proj_b': (0.0, 0.574)}
    factors = {'L0_conv_W1': 8.0,
     'L0_conv_W3': 8.0,
     'L0_conv_W5': 4.156,
     'L0_conv_Wdw': 5.124,
     'L0_conv_Wproj': 4.984,
     'L2_conv_router_w1': 4.973,
     'L2_conv_router_w2': 4.533,
     'L2_conv_qkv_w': 8.0,
     'L2_conv_proj_w': 8.0,
     'L3_conv_b2': 3.61}
    for name, (base, spread) in spreads.items():
        noise = np.random.default_rng([zlib.crc32(name.encode()), seed]).standard_normal(out[name].shape)
        drawn = base * np.exp(spread * noise) if base else spread * noise
        out[name] = jnp.asarray(drawn.astype(out[name].dtype))
    for name, factor in factors.items():
        out[name] = (out[name] * factor).astype(out[name].dtype)
    return out
```

```python
from contextlib import ExitStack

import concourse.bass as bass
from concourse import mybir
from concourse.alu_op_type import AluOpType as ALU

ACT = mybir.ActivationFunctionType
AX_X = mybir.AxisListType.X
F32 = mybir.dt.float32
F16 = mybir.dt.float16
U32 = mybir.dt.uint32
I32 = mybir.dt.int32
ds = bass.ds

P = 128
H = W = 64
C = 256
CC = C // P
N = H * W
NT = 512
TILES = N // NT
TR = NT // W
HD = 32
HEADS = C // HD
GN_EPS = 1e-5


class Chain:

    def __init__(self, engine, sem):
        self.engine, self.sem, self.n = engine, sem, 0

    def done(self, ins):
        ins.then_inc(self.sem, 1)
        self.n += 1
        return ins

    def wait(self, back=0):
        self.engine.wait_ge(self.sem, self.n - back)


def group_norm_stats(nc, name, sem, X, stats, aggr, group_avg, ps_stat, cols, dve_wait=None):
    chan_ready = sem(name + "_channel_means")
    mean_ready = sem(name + "_group_means")
    dev_ready = sem(name + "_channel_vars")
    var_ready = sem(name + "_group_vars")
    std_ready = sem(name + "_group_std")
    dve_step = sem(name + "_dve_step")

    def vector(dve):
        chain = Chain(dve, dve_step)
        for c in range(CC):
            for t in range(TILES):
                chain.done(nc.vector.bn_stats(stats[:, c, t, :], X[:, c, t * NT:(t + 1) * NT]))
        chain.wait()
        for c in range(CC):
            chain.done(nc.vector.bn_aggr(aggr[:, c, 0:2], stats[:, c, :, :].rearrange("p t s -> p (t s)")))
        chain.wait()
        nc.vector.tensor_copy(cols[:, 2, :], aggr[:, :, 0]).then_inc(chan_ready, 1)
        dve.wait_ge(mean_ready, 1)
        chain.done(nc.vector.tensor_copy(cols[:, 3, :], ps_stat[:, 0:CC]))
        chain.wait()
        chain.done(nc.vector.tensor_tensor(cols[:, 4, :], aggr[:, :, 0], cols[:, 3, :], ALU.subtract))
        chain.wait()
        chain.done(nc.vector.tensor_tensor(cols[:, 5, :], cols[:, 4, :], cols[:, 4, :], ALU.mult))
        chain.wait()
        nc.vector.tensor_tensor(cols[:, 6, :], cols[:, 5, :], aggr[:, :, 1], ALU.add).then_inc(dev_ready, 1)
        dve.wait_ge(std_ready, 1)
        chain.done(nc.vector.reciprocal(cols[:, 0, :], cols[:, 7, :]))
        chain.wait()
        chain.done(nc.vector.scalar_tensor_tensor(out=cols[:, 1, :], in0=cols[:, 3, :], scalar=-1.0,
                                                  in1=cols[:, 0, :], op0=ALU.mult, op1=ALU.mult))
        chain.wait()
        assert chain.n == CC * TILES + 7

    def tensor(pe):
        pe.wait_ge(chan_ready, 1)
        nc.tensor.matmul(ps_stat[:, 0:CC], group_avg[:, :], cols[:, 2, :], start=True, stop=True).then_inc(mean_ready, 1)
        pe.wait_ge(dev_ready, 1)
        nc.tensor.matmul(ps_stat[:, CC:2 * CC], group_avg[:, :], cols[:, 6, :], start=True, stop=True).then_inc(var_ready, 1)

    def scalar(act, eps_col):
        act.wait_ge(var_ready, 1)
        nc.scalar.activation(cols[:, 7, :], ps_stat[:, CC:2 * CC], ACT.Sqrt, bias=eps_col).then_inc(std_ready, 1)

    def wait_ready(engine):
        engine.wait_ge(dve_step, CC * TILES + 7)

    return vector, tensor, scalar, wait_ready


def layer0_conv(nc, sem, X, x, w_convs, w_dw, temp, ones_head, group_avg, eps_col, Qhl, Khl, consts_ready):
    KS = (1, 3, 5)
    TAPS = [k * k for k in KS]
    TAP0 = [0, 1, 10]
    PW = W + 4
    QW = W + 2
    ORDER = [(0, 0), (1, 0), (0, 1), (1, 1), (2, 0), (2, 1)]
    NB = 4
    QTR = 4
    QR = H // QTR
    SPLIT = 256.0
    with ExitStack() as ctx:
        def sb(name, shape, dt):
            return ctx.enter_context(nc.sbuf_tensor(name, shape, dt))

        xpad = sb("xpad", [P, CC, PW, PW], F32)
        wc = sb("wc", [P, CC, sum(TAPS), C], F32)
        qpad = [sb(f"qpad{b}", [P, QW, QW], F32) for b in range(2)]
        sq = sb("sq", [P, N], F32)
        wd = sb("wd", [P, 3 * CC, 9], F32)
        tcol = sb("tcol", [P, CC], F32)
        stats = sb("stats0", [P, CC, TILES, 6], F32)
        aggr = sb("aggr0", [P, CC, 2], F32)
        cols = sb("cols0", [P, 8, 2], F32)
        nrm = sb("nrm", [P, 2, NT], F32)
        qn = sb("qn", [P, 2, NT], F32)
        hi = sb("hi", [P, 2, NT], F16)
        lo = sb("lo", [P, 2, NT], F16)
        psc = ctx.enter_context(nc.psum_tensor("psc", [P, NB, NT], F32))
        pss = ctx.enter_context(nc.psum_tensor("pss", [P, 3, NT], F32))
        ps_stat = ctx.enter_context(nc.psum_tensor("ps_stat0", [P, NT], F32))

        x_in = sem("l0_x_in")
        small_in = sem("l0_small_in")
        w_in = [sem(f"l0_w{k}_in") for k in KS]
        xpad_zero = sem("l0_xpad_zero")
        qpad_zero = sem("l0_qpad_zero")
        xpad_ready = sem("l0_xpad_ready")
        conv_done = sem("l0_conv_tiles")
        evac_done = sem("l0_conv_evacuated")
        dw_step = sem("l0_dw_steps")
        sq_done = sem("l0_squares")
        ss_done = sem("l0_square_sums")
        nrm_done = sem("l0_norms")
        post_step = sem("l0_post_steps")
        split_out = [sem(f"l0_split_out{b}") for b in range(2)]
        gn_vec, gn_pe, gn_act, gn_wait = group_norm_stats(nc, "gn0", sem, X, stats, aggr, group_avg, ps_stat, cols)
        DW = QTR * 9
        POST = 5
        QK = [i for i, (kind, _) in enumerate(ORDER) if kind < 2]

        block = ctx.enter_context(nc.Block())

        @block.sync
        def _(sp):
            for c in range(CC):
                sp.dma_start(X[:, c, :], x[c * P:(c + 1) * P, :]).then_inc(x_in, 16)
            sp.dma_start(wd[:, :, :], w_dw.rearrange("(c p) t -> p c t", p=P)).then_inc(small_in, 16)
            sp.dma_start(tcol[:, :], temp).then_inc(small_in, 16)
            for k in range(3):
                for c in range(CC):
                    sp.dma_start(wc[:, c, TAP0[k]:TAP0[k] + TAPS[k], :], w_convs[k][c * P:(c + 1) * P, :, :]).then_inc(w_in[k], 16)
            for n, i in enumerate(QK):
                kind, cc = ORDER[i]
                dst = (Qhl, Khl)[kind]
                with sp.Fori(0, TILES // 2) as t:
                    for b in range(2):
                        sp.wait_ge(post_step, t * (2 * POST) + ((b + 1 + n * TILES) * POST))
                        sp.dma_start(dst[0, cc * P:(cc + 1) * P, ds(t * (2 * NT) + b * NT, NT)], hi[:, b, :]).then_inc(split_out[b], 16)
                        sp.dma_start(dst[1, cc * P:(cc + 1) * P, ds(t * (2 * NT) + b * NT, NT)], lo[:, b, :]).then_inc(split_out[b], 16)
            for b in range(2):
                sp.wait_ge(split_out[b], 32 * (TILES // 2) * len(QK))

        @block.gpsimd
        def _(pool):
            nc.gpsimd.memset(xpad[:, :, :, :].rearrange("p c h w -> p (c h w)"), 0.0).then_inc(xpad_zero, 1)
            for b in range(2):
                nc.gpsimd.memset(qpad[b][:, :, :].rearrange("p h w -> p (h w)"), 0.0).then_inc(qpad_zero, 1)
            for n, i in enumerate(QK):
                pool.wait_ge(dw_step, (i + 1) * DW)
                if n:
                    pool.wait_ge(ss_done, n * TILES)
                for h in range(2):
                    part = X[:, i % 2, h * (N // 2):(h + 1) * (N // 2)]
                    nc.gpsimd.tensor_tensor(sq[:, h * (N // 2):(h + 1) * (N // 2)], part, part, ALU.mult).then_inc(sq_done, 1)

        @block.tensor
        def _(pe):
            pe.wait_ge(consts_ready, 16)
            gn_pe(pe)
            pe.wait_ge(xpad_ready, CC)

            def conv_tile(kind, cc, t, b):
                k = KS[kind]
                off = 2 - (k - 1) // 2
                n = 0
                for c in range(CC):
                    for dy in range(k):
                        for dx in range(k):
                            last = nc.tensor.matmul(
                                psc[:, b, :], wc[:, c, TAP0[kind] + dy * k + dx, cc * P:(cc + 1) * P],
                                xpad[:, c, ds(t * TR + off + dy, TR), off + dx:off + dx + W],
                                start=(n == 0), stop=(n == CC * k * k - 1))
                            n += 1
                last.then_inc(conv_done, 1)

            def conv_chunk(i):
                kind, cc = ORDER[i]
                pe.wait_ge(w_in[kind], 16 * CC)
                if i == 0:
                    for t in range(TILES):
                        if t >= NB:
                            pe.wait_ge(evac_done, t - NB + 1)
                        conv_tile(kind, cc, t, t % NB)
                else:
                    with pe.Fori(0, TILES // NB) as t:
                        for b in range(NB):
                            pe.wait_ge(evac_done, t * NB + (i * TILES + b - NB + 1))
                            conv_tile(kind, cc, t * NB + b, b)

            def square_sums(n):
                pe.wait_ge(sq_done, 2 * (n + 1))
                for t in range(TILES):
                    m = n * TILES + t
                    if m >= 3:
                        pe.wait_ge(nrm_done, m - 2)
                    nc.tensor.matmul(pss[:, m % 3, :], ones_head[:, :], sq[:, t * NT:(t + 1) * NT],
                                     start=True, stop=True).then_inc(ss_done, 1)

            conv_chunk(0)
            conv_chunk(1)
            square_sums(0)
            conv_chunk(2)
            conv_chunk(3)
            square_sums(1)
            conv_chunk(4)
            square_sums(2)
            square_sums(3)
            conv_chunk(5)

        @block.scalar
        def _(act):
            gn_act(act, eps_col)

            def evacuate(i):
                if i < 2:
                    act.wait_ge(qpad_zero, i + 1)
                else:
                    act.wait_ge(dw_step, (i - 1) * DW)
                with act.Fori(0, TILES // NB) as t:
                    for b in range(NB):
                        act.wait_ge(conv_done, t * NB + (i * TILES + b + 1))
                        nc.scalar.activation(qpad[i % 2][:, ds(t * (NB * TR) + (b * TR + 1), TR), 1:1 + W],
                                             psc[:, b, :].rearrange("p (h w) -> p h w", h=TR), ACT.Copy).then_inc(evac_done, 1)

            def norms(n):
                for t in range(TILES):
                    m = n * TILES + t
                    act.wait_ge(ss_done, m + 1)
                    if m >= 2:
                        act.wait_ge(post_step, (m - 2) * POST + 3)
                    nc.scalar.activation(nrm[:, m % 2, :], pss[:, m % 3, :], ACT.Sqrt).then_inc(nrm_done, 1)

            evacuate(0)
            evacuate(1)
            norms(0)
            evacuate(2)
            evacuate(3)
            norms(1)
            evacuate(4)
            norms(2)
            norms(3)
            evacuate(5)

        @block.vector
        def _(dve):
            dve.wait_ge(x_in, 16 * CC)
            gn_vec(dve)
            dve.wait_ge(xpad_zero, 1)
            for c in range(CC):
                nc.vector.tensor_scalar(out=xpad[:, c, 2:2 + H, 2:2 + W], in0=X[:, c, :].rearrange("p (h w) -> p h w", h=H),
                                        scalar1=cols[:, 0, c:c + 1], scalar2=cols[:, 1, c:c + 1],
                                        op0=ALU.mult, op1=ALU.add).then_inc(xpad_ready, 1)
            dve.wait_ge(small_in, 32)
            dve.wait_ge(xpad_ready, CC)

            def taps(i, q, base):
                kind, cc = ORDER[i]
                out = X[:, i % 2, ds(q * (QR * W), QR * W)].rearrange("p (h w) -> p h w", h=QR)
                for tap in range(9):
                    dy, dx = divmod(tap, 3)
                    src = qpad[i % 2][:, ds(q * QR + dy, QR), dx:dx + W]
                    col = wd[:, kind * CC + cc, tap:tap + 1]
                    if tap == 0:
                        ins = nc.vector.tensor_scalar(out=out, in0=src, scalar1=col, scalar2=None, op0=ALU.mult)
                    else:
                        dve.wait_ge(dw_step, base + tap)
                        ins = nc.vector.scalar_tensor_tensor(out=out, in0=src, scalar=col, in1=out, op0=ALU.mult, op1=ALU.add)
                    ins.then_inc(dw_step, 1)

            def depthwise(i):
                per = TILES // QTR
                with dve.Fori(0, QTR - 1) as q:
                    dve.wait_ge(evac_done, q * per + (i * TILES + per + 1))
                    taps(i, q, q * 9 + i * DW)
                dve.wait_ge(evac_done, (i + 1) * TILES)
                taps(i, QTR - 1, (QTR - 1) * 9 + i * DW)

            def normalise(n):
                i = QK[n]
                kind, cc = ORDER[i]
                for t in range(TILES):
                    m = n * TILES + t
                    b = m % 2
                    base = m * POST
                    dve.wait_ge(nrm_done, m + 1)
                    nc.vector.tensor_scalar(out=nrm[:, b, :], in0=nrm[:, b, :], scalar1=1e-12, scalar2=1.0 / SPLIT,
                                            op0=ALU.max, op1=ALU.mult).then_inc(post_step, 1)
                    dve.wait_ge(post_step, base + 1)
                    nc.vector.reciprocal(nrm[:, b, :], nrm[:, b, :]).then_inc(post_step, 1)
                    dve.wait_ge(post_step, base + 2)
                    D = X[:, i % 2, t * NT:(t + 1) * NT]
                    if kind == 0:
                        ins = nc.vector.scalar_tensor_tensor(out=qn[:, b, :], in0=D, scalar=tcol[:, cc:cc + 1],
                                                             in1=nrm[:, b, :], op0=ALU.mult, op1=ALU.mult)
                    else:
                        ins = nc.vector.tensor_tensor(qn[:, b, :], D, nrm[:, b, :], ALU.mult)
                    ins.then_inc(post_step, 1)
                    dve.wait_ge(post_step, base + 3)
                    if m >= 2:
                        dve.wait_ge(split_out[b], 32 * (m // 2))
                    nc.vector.tensor_copy(hi[:, b, :], qn[:, b, :]).then_inc(post_step, 1)
                    dve.wait_ge(post_step, base + 4)
                    nc.vector.tensor_tensor(lo[:, b, :], qn[:, b, :], hi[:, b, :], ALU.subtract).then_inc(post_step, 1)

            depthwise(0)
            depthwise(1)
            normalise(0)
            depthwise(2)
            normalise(1)
            depthwise(3)
            normalise(2)
            normalise(3)
            depthwise(4)
            depthwise(5)


def layer0_attention(nc, sem, X, x, Qhl, Khl, w_proj, ident):
    SPLIT2 = 1.0 / (256.0 * 256.0)
    HG = 4
    GROUPS = HEADS // HG
    MT = N // P
    UN = 2 * MT
    UI = GROUPS * UN
    RING = 3
    PRING = 4
    AHEAD = 3
    POOL_M = [3, 4, 8, 12, 16, 20, 24, 27]
    PE_M = [29, 31]
    DVE_M = [m for m in range(MT) if m not in POOL_M and m not in PE_M]
    ND, NPOOL = 2 * (len(DVE_M) - 1), 2 * (len(POOL_M) - 1)
    PIECES = 4
    PW = NT // PIECES
    PIECE_M = POOL_M[1:1 + PIECES]
    assert UI % PRING == 0 and DVE_M[1] == DVE_M[0] + 1 and POOL_M[1] == POOL_M[0] + 1
    with ExitStack() as ctx:
        def sb(name, shape, dt):
            return ctx.enter_context(nc.sbuf_tensor(name, shape, dt))

        Kst = sb("Kst", [P, HEADS, N], F16)
        Qst = sb("Qst", [P, GROUPS, HG, NT], F16)
        V = sb("V", [P, MT, C], F32)
        O = sb("O", [P, CC, N], F32)
        prob = sb("prob", [P, PRING, 2, NT], F32)
        acc = sb("acc", [P, HG, NT], F32)
        accp = sb("accp", [P, HG, NT], F32)
        ones = sb("ones32", [P, HD], F32)
        rsum = sb("rsum", [P, NT], F32)
        wp = sb("wp", [P, CC, C], F32)
        S = ctx.enter_context(nc.psum_tensor("S", [P, RING, 2, NT], F32))
        PO = ctx.enter_context(nc.psum_tensor("PO", [P, NT], F32))
        PS = ctx.enter_context(nc.psum_tensor("PS", [P, NT], F32))

        k_in = sem("l0_k_in")
        q_in = [sem(f"l0_q_in{g}") for g in range(GROUPS)]
        w_in = sem("l0_wproj_in")
        x_in = sem("l0_x_again")
        ones_ready = sem("l0_ones")
        vt_done = sem("l0_v_transposed")
        v_ready = sem("l0_v_ready")
        qk_done = sem("l0_scores")
        exp_done = sem("l0_exp")
        pv_done = sem("l0_pv")
        dve_add = sem("l0_dve_add")
        pool_add = sem("l0_pool_add")
        group_done = sem("l0_group")
        po_free = sem("l0_po_free")
        ps_free = sem("l0_ps_free")
        o_ready = sem("l0_o_ready")
        proj_done = sem("l0_proj")
        x_ready = sem("l0_x_ready")
        block = ctx.enter_context(nc.Block())

        def dve_adds(n, g, m, pair):
            j = DVE_M.index(m)
            return n * (GROUPS * ND) + (g * ND + 2 * (max(j, 1) - 1) + pair + 1)

        def pool_adds(n, g, m, pair):
            return n * (GROUPS * NPOOL) + (g * NPOOL + 2 * (max(POOL_M.index(m), 1) - 1) + pair + 1)

        @block.sync
        def _(sp):
            def load_q(g, off):
                for r in range(4):
                    sp.dma_start(Qst[r * HD:(r + 1) * HD, g, :, :],
                                 Qhl[r // 2, g * P:(g + 1) * P, ds(off, NT)].rearrange("(h d) n -> d h n", d=HD)).then_inc(q_in[g], 16)

            for g in range(GROUPS):
                for r in range(4):
                    sp.dma_start(Kst[r * HD:(r + 1) * HD, g * HG:(g + 1) * HG, :],
                                 Khl[r % 2, g * P:(g + 1) * P, :].rearrange("(h d) n -> d h n", d=HD)).then_inc(k_in, 16)
                load_q(g, 0)
            sp.dma_start(wp[:, :, :], w_proj.rearrange("(c p) n -> p c n", p=P)).then_inc(w_in, 16)
            sp.wait_ge(v_ready, MT // 2)
            for c in range(CC):
                sp.dma_start(X[:, c, :], x[c * P:(c + 1) * P, :]).then_inc(x_in, 16)
            with sp.Fori(1, TILES) as n:
                for g in range(GROUPS):
                    sp.wait_ge(qk_done, n * UI + ((g + 1) * UN - UI))
                    load_q(g, n * NT)
            sp.wait_ge(qk_done, (TILES - 1) * UI + UN)
            load_q(0, (TILES - 1) * NT)

        @block.gpsimd
        def _(pool):
            nc.gpsimd.memset(ones[:, :], 1.0).then_inc(ones_ready, 1)

            def token_tile(n, first):
                for g in range(GROUPS):
                    for j, m in enumerate(POOL_M[1:]):
                        for pair in range(2):
                            u = g * UN + 2 * m + pair
                            dst = accp[:, 2 * pair:2 * pair + 2, :]
                            if j == 0 and pair == 0 and not (first and g == 0):
                                pool.wait_ge(group_done, n * GROUPS + g)
                            if j:
                                pool.wait_ge(pool_add, pool_adds(n, g, POOL_M[j], pair))
                            pool.wait_ge(exp_done, n * UI + (u + 1))
                            a = dst if j else prob[:, (u - 2) % PRING, :, :]
                            nc.gpsimd.tensor_tensor(dst, a, prob[:, u % PRING, :, :], ALU.add).then_inc(pool_add, 1)

            token_tile(0, True)
            with pool.Fori(1, TILES) as n:
                token_tile(n, False)

        @block.scalar
        def _(act):
            def wait_summed(n, k):
                g, m, pair = k // UN, k % UN // 2, k % 2
                if m in DVE_M:
                    act.wait_ge(dve_add, dve_adds(n, g, m, pair))
                elif m in POOL_M:
                    act.wait_ge(pool_add, pool_adds(n, g, m, pair))

            def token_tile(n, before):
                for k in range(UI):
                    act.wait_ge(qk_done, n * UI + (k + 1))
                    if k >= PRING:
                        act.wait_ge(pv_done, n * (UI // 2) + ((k - PRING) // 2 + 1))
                        wait_summed(n, k - PRING)
                    elif before is not None:
                        act.wait_ge(pv_done, n * (UI // 2) + (k - PRING) // 2 + 1)
                        wait_summed(before, k - PRING + UI)
                    nc.scalar.activation(prob[:, k % PRING, :, :], S[:, k % RING, :, :], ACT.Exp, scale=SPLIT2).then_inc(exp_done, 1)

            token_tile(0, None)
            with act.Fori(1, TILES) as n:
                token_tile(n, n - 1)

        @block.tensor
        def _(pe):
            for r in range(MT // 2):
                if r >= 2 * RING:
                    pe.wait_ge(v_ready, r - 2 * RING + 1)
                s = r % (2 * RING)
                for q in range(4):
                    j, c = 2 * r + q // 2, q % 2
                    last = nc.tensor.transpose(S[:, s // 2, s % 2, q * P:(q + 1) * P], X[:, c, j * P:(j + 1) * P], ident[:, :])
                last.then_inc(vt_done, 1)
            pe.wait_ge(v_ready, MT // 2)
            pe.wait_ge(ones_ready, 1)
            pe.wait_ge(k_in, 16 * 4 * GROUPS)

            def scores(n, k, first):
                g, m, pair = k // UN, k % UN // 2, k % 2
                if k % UN == 0:
                    pe.wait_ge(q_in[g], (n + 1) * 64)
                if k >= RING:
                    pe.wait_ge(exp_done, n * UI + (k - RING + 1))
                elif not first:
                    prev = max(u for u in range(UI - RING, UI) if u % RING == k)
                    pe.wait_ge(exp_done, n * UI + (prev + 1 - UI))
                for hh in range(2):
                    h = 2 * pair + hh
                    last = nc.tensor.matmul(S[:, k % RING, hh, :], Kst[:, g * HG + h, m * P:(m + 1) * P], Qst[:, g, h, :], start=True, stop=True)
                last.then_inc(qk_done, 1)

            def sums(src, start, stop):
                for h in range(HG):
                    last = nc.tensor.matmul(PS[h * HD:(h + 1) * HD, :], ones[:, :], src(h), start=start, stop=stop)
                return last

            def token_tile(n, first):
                for k in range(UI):
                    g, m, pair = k // UN, k % UN // 2, k % 2
                    ahead = k + AHEAD
                    if ahead < UI:
                        scores(n, ahead, first)
                    else:
                        scores(n + 1, ahead - UI, False)
                    if pair == 0:
                        continue
                    pe.wait_ge(exp_done, n * UI + (k + 1))
                    if m == 0 and not (first and g == 0):
                        pe.wait_ge(po_free, n * GROUPS + g)
                    for h in range(HG):
                        u = k - 1 + h // 2
                        last = nc.tensor.matmul(PO[h * HD:(h + 1) * HD, :], V[:, m, (g * HG + h) * HD:(g * HG + h + 1) * HD],
                                                prob[:, u % PRING, h % 2, :], start=(m == 0), stop=(m == MT - 1))
                    if m in PE_M:
                        if m == PE_M[0] and not (first and g == 0):
                            pe.wait_ge(ps_free, n * (GROUPS * PIECES) + g * PIECES)
                        last = sums(lambda h: prob[:, (k - 1 + h // 2) % PRING, h % 2, :], m == PE_M[0], False)
                    last.then_inc(pv_done, 1)
                    if m == MT - 1:
                        pe.wait_ge(pool_add, pool_adds(n, g, POOL_M[-1], 1))
                        sums(lambda h: accp[:, h, :], False, False)
                        pe.wait_ge(dve_add, dve_adds(n, g, DVE_M[-1], 1))
                        sums(lambda h: acc[:, h, :], False, True).then_inc(group_done, 1)

            for k in range(AHEAD):
                scores(0, k, True)
            token_tile(0, True)
            with pe.Fori(1, TILES) as n:
                token_tile(n, False)
            pe.wait_ge(w_in, 16)
            pe.wait_ge(o_ready, TILES * GROUPS * PIECES)
            pe.wait_ge(exp_done, TILES * UI)
            for t in range(TILES):
                for o in range(CC):
                    r = t * CC + o
                    s = r % 4
                    if r >= 4:
                        pe.wait_ge(x_ready, r - 3)
                    for c in range(CC):
                        last = nc.tensor.matmul(S[:, s // 2, s % 2, :], wp[:, c, o * P:(o + 1) * P], O[:, c, t * NT:(t + 1) * NT],
                                                start=(c == 0), stop=(c == CC - 1))
                    last.then_inc(proj_done, 1)

        @block.vector
        def _(dve):
            for r in range(MT // 2):
                dve.wait_ge(vt_done, r + 1)
                s = r % (2 * RING)
                nc.vector.tensor_copy(V[:, 2 * r:2 * r + 2, :].rearrange("p j c -> p (j c)"), S[:, s // 2, s % 2, :]).then_inc(v_ready, 1)

            def copy_values(n, g):
                dve.wait_ge(group_done, n * GROUPS + (g + 1))
                nc.vector.tensor_copy(O[:, g, ds(n * NT, NT)], PO[:, :]).then_inc(po_free, 1)

            def normalise_piece(n, g, j):
                dve.wait_ge(po_free, n * GROUPS + (g + 1))
                count = n * (GROUPS * PIECES) + (g * PIECES + j + 1)
                part = slice(j * PW, (j + 1) * PW)
                nc.vector.reciprocal(rsum[:, part], PS[:, part]).then_inc(ps_free, 1)
                dve.wait_ge(ps_free, count)
                out = O[:, g, ds(n * NT + j * PW, PW)]
                nc.vector.tensor_tensor(out, out, rsum[:, part], ALU.mult).then_inc(o_ready, 1)

            def token_tile(n, before):
                for g in range(GROUPS):
                    prev = (n, 0) if g else (before, 1)
                    for m in range(MT):
                        if m in PIECE_M and prev[0] is not None:
                            normalise_piece(*prev, PIECE_M.index(m))
                        if m == DVE_M[0] or m not in DVE_M:
                            continue
                        for pair in range(2):
                            u = g * UN + 2 * m + pair
                            dst = acc[:, 2 * pair:2 * pair + 2, :]
                            dve.wait_ge(exp_done, n * UI + (u + 1))
                            if m == DVE_M[1]:
                                a = prob[:, (u - 2) % PRING, :, :]
                            else:
                                a = dst
                                dve.wait_ge(dve_add, dve_adds(n, g, DVE_M[DVE_M.index(m) - 1], pair))
                            nc.vector.tensor_tensor(dst, a, prob[:, u % PRING, :, :], ALU.add).then_inc(dve_add, 1)
                    copy_values(n, g)

            token_tile(0, None)
            with dve.Fori(1, TILES) as n:
                token_tile(n, n - 1)
            for j in range(PIECES):
                normalise_piece(TILES - 1, GROUPS - 1, j)
            dve.wait_ge(x_in, 16 * CC)
            for t in range(TILES):
                for o in range(CC):
                    r = t * CC + o
                    s = r % 4
                    dve.wait_ge(proj_done, r + 1)
                    xt = X[:, o, t * NT:(t + 1) * NT]
                    nc.vector.tensor_tensor(xt, S[:, s // 2, s % 2, :], xt, ALU.add).then_inc(x_ready, 1)


def layer1_codebook(nc, sem, X, Xs, Os, codes, codes_t, ident, group_avg, eps_col):
    K = codes.shape[1]
    KB = K // NT
    MT = N // P
    RING = 4
    with ExitStack() as ctx:
        def sb(name, shape, dt):
            return ctx.enter_context(nc.sbuf_tensor(name, shape, dt))

        E2 = sb("E2", [P, CC, K], F32)
        Esq = sb("Esq", [P, CC, K], F32)
        nee = sb("nee", [1, K], F32)
        ones = sb("ones1", [P, P], F32)
        stats = sb("stats1", [P, CC, TILES, 6], F32)
        aggr = sb("aggr1", [P, CC, 2], F32)
        cols = sb("cols1", [P, 8, 2], F32)
        xt = sb("xt1", [P, RING, CC, P], F32)
        xsq = sb("xsq1", [P, RING, CC, P], F32)
        nxx = sb("nxx", [P, RING, 1], F32)
        nd = sb("nd", [P, RING, K], F32)
        best = sb("best", [P, RING, 8], F32)
        idx = sb("idx", [P, RING, 8], U32)
        quant = sb("quant", [P, RING, C], F32)
        zeros = sb("zeros1", [P, 2048], F32)
        D = ctx.enter_context(nc.psum_tensor("D1", [P, 2, KB, NT], F32))
        T = ctx.enter_context(nc.psum_tensor("T1", [P, 2, NT], F32))
        px = ctx.enter_context(nc.psum_tensor("px1", [P, 2, NT], F32))
        ps = px[:, 0, :]

        zeros_set = sem("l1_zeros_set")
        rows_zero = sem("l1_rows_zero")
        e_in = sem("l1_codes_in")
        ones_ready = sem("l1_ones")
        e_step = sem("l1_code_steps")
        ee_done = sem("l1_ee")
        nee_ready = sem("l1_nee")
        xt_ready = sem("l1_xt")
        sq_ready = sem("l1_xsq")
        d_done = sem("l1_products")
        nxx_ready = sem("l1_nxx")
        nd_ready = sem("l1_nd")
        best_ready = sem("l1_best")
        idx_ready = sem("l1_idx")
        q_in = [sem(f"l1_quant_in{b}") for b in range(RING)]
        qt_done = sem("l1_quant_t")
        x_done = sem("l1_x")
        gn_vec, gn_pe, gn_act, gn_wait = group_norm_stats(nc, "gn1", sem, X, stats, aggr, group_avg, ps, cols)
        block = ctx.enter_context(nc.Block())

        @block.sync
        def _(sp):
            sp.dma_start(E2[:, :, :], codes.rearrange("(c p) k -> p c k", p=P)).then_inc(e_in, 16)
            sp.wait_ge(zeros_set, 1)
            per = zeros.shape[1]
            count = 0
            for rows in (Xs, Os):
                flat = rows.rearrange("(p r) c -> p (r c)", p=P)
                for o in range(0, flat.shape[1], per):
                    sp.dma_start(flat[:, o:o + per], zeros[:, :]).then_inc(rows_zero, 16)
                    count += 16
            sp.wait_ge(rows_zero, count)

        @block.gpsimd
        def _(pool):
            nc.gpsimd.memset(ones[:, :], 1.0).then_inc(ones_ready, 1)
            nc.gpsimd.memset(zeros[:, :], 0.0).then_inc(zeros_set, 1)

            def square(i):
                b = i % RING
                pool.wait_ge(xt_ready, i + 1)
                nc.gpsimd.tensor_tensor(xsq[:, b, :, :], xt[:, b, :, :], xt[:, b, :, :], ALU.mult).then_inc(sq_ready, 1)

            square(0)
            square(1)
            for i in range(MT):
                if i + 2 < MT:
                    square(i + 2)
                if i >= RING:
                    pool.wait_ge(qt_done, i - RING + 1)
                pool.wait_ge(idx_ready, i + 1)
                nc.gpsimd.indirect_dma_start(out=quant[:, i % RING, :], out_offset=None, in_=codes_t,
                                             in_offset=bass.IndirectOffsetOnAxis(ap=idx[:, i % RING, 0:1], axis=0)).then_inc(q_in[i % RING], 16)

        @block.scalar
        def _(act):
            gn_act(act, eps_col)
            act.wait_ge(ee_done, KB)
            nc.scalar.activation(nee[0:1, :], D[0:1, 0, :, :].rearrange("p k n -> p (k n)"), ACT.Copy, scale=-1.0).then_inc(nee_ready, 1)
            gn_wait(act)

            def norm(r, b, first):
                i = r * RING + b
                if not first:
                    act.wait_ge(d_done, r * RING + (b - RING + 1))
                for c in range(CC):
                    ins = nc.scalar.activation(xt[:, b, c, :], X[:, c, ds(r * (RING * P) + b * P, P)], ACT.Identity,
                                               scale=cols[:, 0, c:c + 1], bias=cols[:, 1, c:c + 1])
                ins.then_inc(xt_ready, 1)

            def distances(r, b, first):
                act.wait_ge(d_done, r * RING + (b + 1))
                nc.scalar.activation(nxx[:, b, :], px[:, b % 2, 0:1], ACT.Copy, scale=-1.0).then_inc(nxx_ready, 1)
                act.wait_ge(nxx_ready, r * RING + (b + 1))
                if not first:
                    act.wait_ge(idx_ready, r * RING + (b - RING + 1))
                nc.scalar.activation(nd[:, b, :], D[:, b % 2, :, :].rearrange("p k n -> p (k n)"), ACT.Identity,
                                     bias=nxx[:, b, :]).then_inc(nd_ready, 1)

            for b in range(RING):
                norm(0, b, True)
            for b in range(RING):
                distances(0, b, True)
                norm(1, b, False)
            with act.Fori(1, MT // RING - 1) as r:
                for b in range(RING):
                    distances(r, b, False)
                    norm(r + 1, b, False)
            for b in range(RING):
                distances(MT // RING - 1, b, False)

        @block.tensor
        def _(pe):
            gn_pe(pe)
            pe.wait_ge(ones_ready, 1)
            pe.wait_ge(e_step, 1)
            for k in range(KB):
                for c in range(CC):
                    last = nc.tensor.matmul(D[0:1, 0, k, :], ones[:, 0:1], Esq[:, c, k * NT:(k + 1) * NT], start=(c == 0), stop=(c == CC - 1))
                last.then_inc(ee_done, 1)
            pe.wait_ge(nee_ready, 1)
            pe.wait_ge(e_step, 2)

            def products(r, b, early):
                pe.wait_ge(xt_ready, r * RING + (b + 1))
                pe.wait_ge(sq_ready, r * RING + (b + 1))
                if not early:
                    pe.wait_ge(nd_ready, r * RING + (b - 1))
                for c in range(CC):
                    nc.tensor.matmul(px[:, b % 2, 0:1], xsq[:, b, c, :], ones[:, 0:1], start=(c == 0), stop=(c == CC - 1))
                for k in range(KB):
                    part = slice(k * NT, (k + 1) * NT)
                    for c in range(CC):
                        nc.tensor.matmul(D[:, b % 2, k, :], xt[:, b, c, :], E2[:, c, part], start=(c == 0), stop=False)
                    last = nc.tensor.matmul(D[:, b % 2, k, :], ones[0:1, :], nee[0:1, part], start=False, stop=True)
                last.then_inc(d_done, 1)

            def transpose(r, b, early):
                pe.wait_ge(q_in[b], r * 16 + 16)
                if not early:
                    pe.wait_ge(x_done, r * RING + (b - 1))
                for c in range(CC):
                    last = nc.tensor.transpose(T[:, b % 2, c * P:(c + 1) * P], quant[:, b, c * P:(c + 1) * P], ident)
                last.then_inc(qt_done, 1)

            for b in range(RING):
                products(0, b, b < 2)
            for b in range(RING):
                products(1, b, False)
                transpose(0, b, b < 2)
            with pe.Fori(2, MT // RING) as r:
                for b in range(RING):
                    products(r, b, False)
                    transpose(r - 1, b, False)
            for b in range(RING):
                transpose(MT // RING - 1, b, False)

        @block.vector
        def _(dve):
            dve.wait_ge(e_in, 16)
            nc.vector.tensor_tensor(Esq[:, :, :], E2[:, :, :], E2[:, :, :], ALU.mult).then_inc(e_step, 1)
            dve.wait_ge(e_step, 1)
            nc.vector.tensor_scalar(out=E2[:, :, :], in0=E2[:, :, :], scalar1=2.0, scalar2=None, op0=ALU.mult).then_inc(e_step, 1)
            gn_vec(dve)

            def add_codes(i):
                xi = X[:, :, i * P:(i + 1) * P]
                dve.wait_ge(qt_done, i + 1)
                nc.vector.tensor_tensor(xi, T[:, i % 2, 0:C].rearrange("p (c n) -> p c n", c=CC), xi, ALU.add).then_inc(x_done, 1)

            for i in range(MT):
                b = i % RING
                dve.wait_ge(nd_ready, i + 1)
                nc.vector.max(best[:, b, :], nd[:, b, :]).then_inc(best_ready, 1)
                if i >= RING:
                    dve.wait_ge(q_in[b], 16 * (i // RING))
                dve.wait_ge(best_ready, i + 1)
                nc.vector.max_index(idx[:, b, :], best[:, b, :], nd[:, b, :]).then_inc(idx_ready, 1)
                if i >= RING:
                    add_codes(i - RING)
            for i in range(MT - RING, MT):
                add_codes(i)


EXPERTS = 8
SLOTS = N // P + EXPERTS
WIN = 8
PAIRS = N // P


def by_window(ap):
    return ap.rearrange("p (r w c) -> p w r c", r=WIN, c=WIN)


def layer2_route(nc, sem, X, rw1, rb1, rw2, rb2, consts2, ident, group_avg, eps_col, pos, pmax, expert, Xs):
    HID = rw1.shape[1]
    with ExitStack() as ctx:
        def sb(name, shape, dt):
            return ctx.enter_context(nc.sbuf_tensor(name, shape, dt))

        xw = sb("xw", [P, CC, N], F32)
        XT = sb("XT", [P, PAIRS, C], F32)
        w1 = sb("rw1", [P, CC, HID], F32)
        b1 = sb("rb1", [P, 1], F32)
        w2 = sb("rw2", [P, EXPERTS], F32)
        b2 = sb("rb2", [1, EXPERTS], F32)
        cst = sb("cst2", [P, 2, P], F32)
        iota = sb("iota8", [P, PAIRS, EXPERTS], F32)
        tilec = sb("tilec", [P, SLOTS, EXPERTS], F32)
        hid = sb("hid", [P, 2, NT], F32)
        stats = sb("stats2", [P, CC, TILES, 6], F32)
        aggr = sb("aggr2", [P, CC, 2], F32)
        cols = sb("cols2", [P, 8, 2], F32)
        te = [sb(f"te{k}", [P, PAIRS, EXPERTS], F32) for k in range(4)]
        et = [sb(f"et{k}", [P, EXPERTS, PAIRS], F32) for k in range(3)]
        tk = [sb(f"tk{k}", [P, PAIRS], F32) for k in range(4)]
        ex = [sb(f"ex{k}", [P, EXPERTS], F32) for k in range(4)]
        exi = sb("exi", [P, 2, EXPERTS], I32)
        ones = sb("ones2", [P, PAIRS], F32)
        tcmp = sb("tcmp", [P, SLOTS, EXPERTS], F32)
        tsum = sb("tsum", [P, SLOTS], F32)
        psh = ctx.enter_context(nc.psum_tensor("psh", [P, 2, NT], F32))
        psl = ctx.enter_context(nc.psum_tensor("psl", [P, NT], F32))
        psx = ctx.enter_context(nc.psum_tensor("psx", [P, 3, NT], F32))
        psc = ctx.enter_context(nc.psum_tensor("psc2", [P, NT], F32))
        ps = ctx.enter_context(nc.psum_tensor("ps2", [P, NT], F32))

        w_in = sem("l2_w_in")
        xw_ready = sem("l2_xw")
        hid_done = sem("l2_hid")
        relu_done = sem("l2_relu")
        logits_done = sem("l2_logits")
        xt_done = sem("l2_xt")
        xt_ready = sem("l2_xt_ready")
        shift_ready = sem("l2_shift")
        exp_done = sem("l2_exp")
        onehot_ready = sem("l2_onehot")
        count_done = sem("l2_count")
        pos_ready = sem("l2_pos")
        chain_sem = sem("l2_chain")
        scattered = sem("l2_scattered")
        gn_vec, gn_pe, gn_act, gn_wait = group_norm_stats(nc, "gn2", sem, X, stats, aggr, group_avg, ps, cols)
        block = ctx.enter_context(nc.Block())
        LOADS = 7

        @block.sync
        def _(sp):
            loads = [(w1[:, :, :], rw1.rearrange("(c p) m -> p c m", p=P)), (b1[:, :], rb1), (w2[:, :], rw2), (b2[:, :], rb2),
                     (cst[:, :, :], consts2["tri"]), (iota[:, :, :], consts2["iota"]), (tilec[:, :, :], consts2["tile"])]
            assert len(loads) == LOADS
            for dst, src in loads:
                sp.dma_start(dst, src).then_inc(w_in, 16)

        @block.gpsimd
        def _(pool):
            pool.wait_ge(xt_ready, PAIRS // 2)
            pool.wait_ge(pos_ready, 1)
            for i in range(PAIRS):
                nc.gpsimd.indirect_dma_start(out=Xs, out_offset=bass.IndirectOffsetOnAxis(ap=pos[:, i:i + 1], axis=0),
                                             in_=XT[:, i, :], in_offset=None).then_inc(scattered, 16)
            pool.wait_ge(scattered, 16 * PAIRS)

        @block.scalar
        def _(act):
            gn_act(act, eps_col)
            act.wait_ge(w_in, 16 * LOADS)

            def transposed(r):
                act.wait_ge(xt_done, r + 1)
                nc.scalar.activation(XT[:, 2 * r:2 * r + 2, :].rearrange("p j c -> p (j c)"), psx[:, r % 3, :], ACT.Copy).then_inc(xt_ready, 1)

            for t in range(TILES):
                act.wait_ge(hid_done, t + 1)
                if t >= 2:
                    act.wait_ge(logits_done, t - 1)
                nc.scalar.activation(hid[:, t % 2, :], psh[:, t % 2, :], ACT.Relu, bias=b1[:, 0:1]).then_inc(relu_done, 1)
                transposed(2 * t)
                transposed(2 * t + 1)
            act.wait_ge(shift_ready, 1)
            nc.scalar.activation(te[1][:, :, :], te[0][:, :, :], ACT.Exp).then_inc(exp_done, 1)

        @block.tensor
        def _(pe):
            gn_pe(pe)
            pe.wait_ge(w_in, 16 * LOADS)

            def hidden(t):
                pe.wait_ge(xw_ready, CC * (t + 1))
                if t >= 2:
                    pe.wait_ge(relu_done, t - 1)
                for c in range(CC):
                    last = nc.tensor.matmul(psh[:, t % 2, :], w1[:, c, :], xw[:, c, t * NT:(t + 1) * NT], start=(c == 0), stop=(c == CC - 1))
                last.then_inc(hid_done, 1)

            hidden(0)
            for t in range(TILES):
                if t + 1 < TILES:
                    hidden(t + 1)
                for r in (2 * t, 2 * t + 1):
                    if r >= 3:
                        pe.wait_ge(xt_ready, r - 2)
                    for q in range(4):
                        i, c = 2 * r + q // 2, q % 2
                        last = nc.tensor.transpose(psx[:, r % 3, q * P:(q + 1) * P], xw[:, c, i * P:(i + 1) * P], ident)
                    last.then_inc(xt_done, 1)
                pe.wait_ge(relu_done, t + 1)
                for q in range(NT // P):
                    i = t * (NT // P) + q
                    o = psl[:, i * EXPERTS:(i + 1) * EXPERTS]
                    nc.tensor.matmul(o, hid[:, t % 2, q * P:(q + 1) * P], w2[:, :], start=True, stop=False)
                    last = nc.tensor.matmul(o, cst[0:1, 1, :], b2[0:1, :], start=False, stop=True)
                last.then_inc(logits_done, 1)
            pe.wait_ge(onehot_ready, 1)
            half = PAIRS * EXPERTS
            rhs = te[3][:, :, :].rearrange("p i e -> p (i e)")
            for k in range(2):
                last = nc.tensor.matmul(psc[:, k * half:(k + 1) * half], cst[:, k, :], rhs, start=True, stop=True)
            last.then_inc(count_done, 1)

        @block.vector
        def _(dve):
            gn_vec(dve)
            for t in range(TILES):
                for c in range(CC):
                    nc.vector.tensor_scalar(out=xw[:, c, t * NT:(t + 1) * NT].rearrange("p (w r c) -> p w r c", r=WIN, c=WIN),
                                            in0=by_window(X[:, c, t * NT:(t + 1) * NT]),
                                            scalar1=cols[:, 0, c:c + 1], scalar2=cols[:, 1, c:c + 1],
                                            op0=ALU.mult, op1=ALU.add).then_inc(xw_ready, 1)
            chain = Chain(dve, chain_sem)

            def step(ins):
                chain.done(ins)
                chain.wait()

            def each(ap):
                return ap.unsqueeze(2).to_broadcast([P, PAIRS, EXPERTS])

            V = nc.vector
            dve.wait_ge(logits_done, TILES)
            logits = psl[:, 0:PAIRS * EXPERTS].rearrange("p (i e) -> p i e", e=EXPERTS)
            step(V.tensor_reduce(out=tk[0][:, :], in_=logits, axis=AX_X, op=ALU.max))
            V.tensor_tensor(te[0][:, :, :], logits, each(tk[0][:, :]), ALU.subtract).then_inc(shift_ready, 1)
            dve.wait_ge(exp_done, 1)
            step(V.tensor_reduce(out=tk[1][:, :], in_=te[1][:, :, :], axis=AX_X, op=ALU.add))
            step(V.reciprocal(tk[1][:, :], tk[1][:, :]))
            step(V.tensor_tensor(te[2][:, :, :], te[1][:, :, :], each(tk[1][:, :]), ALU.mult))
            step(V.tensor_reduce(out=pmax[:, :], in_=te[2][:, :, :], axis=AX_X, op=ALU.max))
            dve.wait_ge(w_in, 16 * LOADS)
            step(V.tensor_tensor(te[0][:, :, :], te[2][:, :, :], each(pmax[:, :]), ALU.is_equal))
            step(V.scalar_tensor_tensor(out=te[1][:, :, :].rearrange("p i e -> p (i e)"), in0=te[0][:, :, :].rearrange("p i e -> p (i e)"),
                                        scalar=-float(EXPERTS), in1=iota[:, :, :].rearrange("p i e -> p (i e)"), op0=ALU.mult, op1=ALU.add))
            step(V.tensor_reduce(out=tk[2][:, :], in_=te[1][:, :, :], axis=AX_X, op=ALU.min))
            V.tensor_tensor(te[3][:, :, :], te[1][:, :, :], each(tk[2][:, :]), ALU.is_equal).then_inc(onehot_ready, 1)
            step(V.memset(ones[:, :], 1.0))
            dve.wait_ge(count_done, 1)
            half = PAIRS * EXPERTS
            step(V.tensor_copy(et[0][:, :, :], psc[:, half:2 * half].rearrange("p (i e) -> p e i", e=EXPERTS)))
            for e in range(EXPERTS):
                chain.done(V.tensor_tensor_scan(out=et[1][:, e, :], data0=ones[:, 0:PAIRS], data1=et[0][:, e, :], initial=0.0,
                                                op0=ALU.mult, op1=ALU.add))
            chain.wait()
            step(V.tensor_tensor(et[2][:, :, :], et[1][:, :, :], et[0][:, :, :], ALU.subtract))
            step(V.tensor_scalar(out=exi[:, 0, :], in0=et[1][:, :, PAIRS - 1], scalar1=float(P - 1), scalar2=None, op0=ALU.add))
            step(V.tensor_scalar(out=exi[:, 1, :], in0=exi[:, 0, :], scalar1=P.bit_length() - 1, scalar2=None, op0=ALU.arith_shift_right))
            step(V.tensor_copy(ex[0][:, :], exi[:, 1, :]))
            step(V.tensor_tensor_scan(out=ex[1][:, :], data0=ones[:, 0:EXPERTS], data1=ex[0][:, :], initial=0.0, op0=ALU.mult, op1=ALU.add))
            step(V.tensor_tensor(ex[2][:, :], ex[1][:, :], ex[0][:, :], ALU.subtract))
            step(V.tensor_scalar(out=ex[3][:, :], in0=ex[2][:, :], scalar1=float(P), scalar2=-1.0, op0=ALU.mult, op1=ALU.add))
            step(V.tensor_tensor(et[0][:, :, :], et[2][:, :, :], ex[3][:, :].unsqueeze(2).to_broadcast([P, EXPERTS, PAIRS]), ALU.add))
            step(V.tensor_tensor(te[0][:, :, :], psc[:, 0:half].rearrange("p (i e) -> p i e", e=EXPERTS),
                                 et[0][:, :, :].rearrange("p e i -> p i e"), ALU.add))
            step(V.tensor_tensor(te[1][:, :, :], te[0][:, :, :], te[3][:, :, :], ALU.mult))
            step(V.tensor_reduce(out=tk[3][:, :], in_=te[1][:, :, :], axis=AX_X, op=ALU.add))
            V.tensor_copy(pos[:, :], tk[3][:, :]).then_inc(pos_ready, 1)
            step(V.tensor_tensor(tcmp[:, :, :], tilec[:, :, :], ex[1][:, :].unsqueeze(1).to_broadcast([P, SLOTS, EXPERTS]), ALU.is_ge))
            step(V.tensor_reduce(out=tsum[:, :], in_=tcmp[:, :, :], axis=AX_X, op=ALU.add))
            step(V.tensor_copy(expert[:, :], tsum[:, :]))


def layer2_sorted_linear(nc, sem, tag, src, dst, w, bias, expert, ident):
    M = dst.shape[1]
    HALVES = [(o, min(NT, M - o)) for o in range(0, M, NT)]
    BUF = 2
    with ExitStack() as ctx:
        def sb(name, shape, dt):
            return ctx.enter_context(nc.sbuf_tensor(tag + name, shape, dt))

        wsb = sb("w", [P, CC, EXPERTS * M], F32)
        bsb = sb("b", [P, EXPERTS * M], F32)
        xs = sb("xs", [P, BUF, C], F32)
        xsT = sb("xsT", [P, BUF, CC, P], F32)
        y = sb("y", [P, BUF, M], F32)
        psT = ctx.enter_context(nc.psum_tensor(tag + "psT", [P, BUF, NT], F32))
        psY = ctx.enter_context(nc.psum_tensor(tag + "psY", [P, BUF, 2 * NT], F32))

        w_in = sem(tag + "_w_in")
        x_in = [sem(tag + f"_x_in{b}") for b in range(BUF)]
        t_done = sem(tag + "_t")
        t_ready = sem(tag + "_t_ready")
        y_done = sem(tag + "_y")
        y_ready = sem(tag + "_y_ready")
        stored = [sem(tag + f"_stored{b}") for b in range(BUF)]
        block = ctx.enter_context(nc.Block())
        ROUNDS = SLOTS // BUF

        def rounds(engine, body):
            for b in range(BUF):
                body(0, b, b, True)
            with engine.Fori(1, ROUNDS) as r:
                for b in range(BUF):
                    body(r, b, r * BUF + b, False)

        @block.sync
        def _(sp):
            def load(b, row):
                sp.dma_start(xs[:, b, :], src[ds(row, P), :]).then_inc(x_in[b], 16)

            def store(r, b, j):
                sp.wait_ge(y_ready, j + 1)
                sp.dma_start(dst[ds(j * P, P), :], y[:, b, :]).then_inc(stored[b], 16)

            for b in range(BUF):
                load(b, b * P)
            for c in range(CC):
                sp.dma_start(wsb[:, c, :], w[c * P:(c + 1) * P, :]).then_inc(w_in, 16)
            sp.dma_start(bsb[:, :], bias.partition_broadcast(P)).then_inc(w_in, 16)
            with sp.Fori(0, ROUNDS - 1) as r:
                for b in range(BUF):
                    sp.wait_ge(t_done, r * BUF + (b + 1))
                    load(b, r * (BUF * P) + (BUF + b) * P)
                    store(r, b, r * BUF + b)
            for b in range(BUF):
                store(ROUNDS - 1, b, SLOTS - BUF + b)
            for b in range(BUF):
                sp.wait_ge(stored[b], 16 * ROUNDS)

        @block.scalar
        def _(act):
            def body(r, b, j, first):
                act.wait_ge(t_done, j + 1)
                if not first:
                    act.wait_ge(y_done, j - (BUF - 1))
                nc.scalar.activation(xsT[:, b, :, :].rearrange("p c n -> p (c n)"), psT[:, b, 0:C], ACT.Copy).then_inc(t_ready, 1)
            rounds(act, body)

        @block.tensor
        def _(pe):
            def transpose(r, b, j, first):
                pe.wait_ge(x_in[b], r * 16 + 16)
                if not first:
                    pe.wait_ge(t_ready, j - (BUF - 1))
                for c in range(CC):
                    last = nc.tensor.transpose(psT[:, b, c * P:(c + 1) * P], xs[:, b, c * P:(c + 1) * P], ident)
                last.then_inc(t_done, 1)

            def multiply(r, b, j, first):
                off = nc.tensor.value_load(expert[0:1, ds(j, 1)], min_val=0, max_val=EXPERTS - 1) * M
                pe.wait_ge(t_ready, j + 1)
                if not first:
                    pe.wait_ge(y_ready, j - (BUF - 1))
                for o, n in HALVES:
                    for c in range(CC):
                        last = nc.tensor.matmul(psY[:, b, o:o + n], xsT[:, b, c, :], wsb[:, c, ds(off + o, n)],
                                                start=(c == 0), stop=(c == CC - 1))
                last.then_inc(y_done, 1)

            for b in range(BUF):
                transpose(0, b, b, True)
            pe.wait_ge(w_in, 16 * (CC + 1))
            for b in range(BUF):
                multiply(0, b, b, True)
                transpose(1, b, BUF + b, False)
            with pe.Fori(1, ROUNDS - 1) as r:
                for b in range(BUF):
                    multiply(r, b, r * BUF + b, False)
                    transpose(r + 1, b, r * BUF + (BUF + b), False)
            for b in range(BUF):
                multiply(ROUNDS - 1, b, SLOTS - BUF + b, False)

        @block.vector
        def _(dve):
            dve.wait_ge(w_in, 16 * (CC + 1))

            def body(r, b, j, first):
                off = nc.vector.value_load(expert[0:1, ds(j, 1)], min_val=0, max_val=EXPERTS - 1) * M
                if not first:
                    dve.wait_ge(stored[b], r * 16)
                dve.wait_ge(y_done, j + 1)
                nc.vector.tensor_tensor(y[:, b, :], psY[:, b, 0:M], bsb[:, ds(off, M)], ALU.add).then_inc(y_ready, 1)
            rounds(dve, body)


def layer2_windows(nc, sem, pos, QKVs, Os, rope, ident):
    SCALE = float(HD) ** -0.5
    HG = 4
    G = HEADS // HG
    WT = WIN * WIN
    VW = HD + 1
    RING = 4
    LAG = 3
    with ExitStack() as ctx:
        def sb(name, shape, dt):
            return ctx.enter_context(nc.sbuf_tensor(name, shape, dt))

        qkv = sb("qkv2", [P, RING, 3 * C], F32)
        tab = sb("tab2", [P, 2, 2 * C], F32)
        t1 = sb("t1", [P, 2, 2 * C], F32)
        t2 = sb("t2", [P, 2, 2 * C], F32)
        rqk = sb("rqk", [P, 2, 2 * C], F32)
        vx = sb("vx", [P, RING, HEADS, VW], F32)
        qT = sb("qT", [P, 2, G, P], F32)
        kT = sb("kT", [P, 2, G, HG, P], F32)
        mx = sb("mx", [P, 2, HEADS], F32)
        sh = sb("sh", [P, 2, HEADS, WT], F32)
        pb = sb("pb", [P, 2, HEADS, P], F32)
        pT = sb("pT", [P, 2, HEADS, P], F32)
        rs = sb("rs", [P, 2, HEADS], F32)
        ob = sb("ob", [P, RING, HEADS, HD], F32)
        psA = ctx.enter_context(nc.psum_tensor("psA", [P, NT], F32))
        psS = ctx.enter_context(nc.psum_tensor("psS", [P, 2, NT], F32))
        psP = ctx.enter_context(nc.psum_tensor("psP", [P, 2, 2, NT], F32))
        psO = ctx.enter_context(nc.psum_tensor("psO", [P, NT], F32))

        tab_in = sem("w2_tab_in")
        zeroed = sem("w2_zeroed")
        g_in = [sem(f"w2_gather{b}") for b in range(RING)]
        t1_done = sem("w2_t1")
        t2_done = sem("w2_t2")
        vx_ready = sem("w2_vx")
        r_ready = sem("w2_r")
        a_done = sem("w2_a")
        a_ready = sem("w2_a_ready")
        s_done = sem("w2_s")
        mx_done = sem("w2_mx")
        sh_ready = sem("w2_sh")
        e_ready = sem("w2_e")
        p_done = sem("w2_p")
        p_ready = [sem("w2_p_ready_act"), sem("w2_p_ready_dve")]
        o_done = sem("w2_o")
        rs_done = sem("w2_rs")
        o_ready = sem("w2_o_ready")
        out_done = [sem(f"w2_out{b}") for b in range(RING)]
        block = ctx.enter_context(nc.Block())
        SLOT0, SLOT1 = RING, PAIRS

        def slots(engine, body):
            def fixed(s):
                def tile(k):
                    i = s - k
                    return (i, i % RING, i // RING) if 0 <= i < PAIRS else None
                return tile
            for s in range(SLOT0):
                body(fixed(s))
            with engine.Fori(0, (SLOT1 - SLOT0) // RING) as r:
                for b in range(RING):
                    body(lambda k: (r * RING + (SLOT0 + b - k), (b - k) % RING, r + (SLOT0 // RING + (b - k) // RING)))
            for s in range(SLOT1, PAIRS + LAG):
                body(fixed(s))

        def again(i, n):
            return not isinstance(i, int) or i >= n

        @block.sync
        def _(sp):
            sp.dma_start(tab[:, :, :], rope).then_inc(tab_in, 16)

        @block.gpsimd
        def _(pool):
            nc.gpsimd.memset(pb[:, :, :, :].rearrange("p b h n -> p (b h n)"), 0.0).then_inc(zeroed, 1)
            nc.gpsimd.memset(kT[:, :, :, :, :].rearrange("p b g h n -> p (b g h n)"), 0.0).then_inc(zeroed, 1)
            nc.gpsimd.memset(vx[:, :, :, HD:VW].rearrange("p b h o -> p (b h o)"), 1.0).then_inc(zeroed, 1)
            pool.wait_ge(tab_in, 16)

            def gather(i):
                if i >= RING:
                    pool.wait_ge(t1_done, i - RING + 1)
                    pool.wait_ge(vx_ready, i - RING + 1)
                nc.gpsimd.indirect_dma_start(out=qkv[:, i % RING, :], out_offset=None, in_=QKVs,
                                             in_offset=bass.IndirectOffsetOnAxis(ap=pos[:, i:i + 1], axis=0)).then_inc(g_in[i % RING], 16)

            def scatter(i):
                pool.wait_ge(o_ready, i + 1)
                nc.gpsimd.indirect_dma_start(out=Os, out_offset=bass.IndirectOffsetOnAxis(ap=pos[:, i:i + 1], axis=0),
                                             in_=ob[:, i % RING, :, :].rearrange("p h d -> p (h d)"), in_offset=None).then_inc(out_done[i % RING], 16)

            def rotate(i):
                pool.wait_ge(g_in[i % RING], 16 * (i // RING + 1))
                if i >= 2:
                    pool.wait_ge(r_ready, i - 1)
                x = qkv[:, i % RING, 0:2 * C].rearrange("p (n two) -> p n two", two=2)
                s = tab[:, 1, :].rearrange("p (n two) -> p n two", two=2)
                o = t2[:, i % 2, :].rearrange("p (n two) -> p n two", two=2)
                nc.gpsimd.tensor_tensor(o[:, :, 0], x[:, :, 1], s[:, :, 0], ALU.mult).then_inc(t2_done, 1)
                nc.gpsimd.tensor_tensor(o[:, :, 1], x[:, :, 0], s[:, :, 1], ALU.mult).then_inc(t2_done, 1)
                if i >= RING:
                    pool.wait_ge(o_done, i - RING + 1)
                nc.gpsimd.tensor_copy(vx[:, i % RING, :, 0:HD], qkv[:, i % RING, 2 * C:3 * C].rearrange("p (h d) -> p h d", d=HD)).then_inc(vx_ready, 1)

            for i in range(RING - 1):
                gather(i)
            for i in range(PAIRS + LAG + 1):
                if i < PAIRS:
                    rotate(i)
                if RING - 1 <= i + RING - 1 < PAIRS:
                    gather(i + RING - 1)
                if 0 <= i - LAG - 1 < PAIRS:
                    scatter(i - LAG - 1)
            for b in range(RING):
                pool.wait_ge(out_done[b], 16 * (PAIRS // RING))

        @block.vector
        def _(dve):
            def rope1(i, b, r):
                dve.wait_ge(g_in[b], r * 16 + 16)
                nc.vector.tensor_tensor(t1[:, b % 2, :], qkv[:, b, 0:2 * C], tab[:, 0, :], ALU.mult).then_inc(t1_done, 1)

            def rope2(i, b, r):
                dve.wait_ge(t1_done, i + 1)
                if again(i, 2):
                    dve.wait_ge(a_done, i - 1)
                dve.wait_ge(t2_done, i * 2 + 2)
                nc.vector.tensor_tensor(rqk[:, b % 2, :], t1[:, b % 2, :], t2[:, b % 2, :], ALU.add).then_inc(r_ready, 1)

            def shift(i, b, r):
                S = psS[:, b % 2, :].rearrange("p (h m) -> p h m", m=WT)
                dve.wait_ge(s_done, i + 1)
                nc.vector.tensor_reduce(out=mx[:, b % 2, :], in_=S, axis=AX_X, op=ALU.max).then_inc(mx_done, 1)
                if again(i, 2):
                    dve.wait_ge(e_ready, i - 1)
                dve.wait_ge(mx_done, i + 1)
                nc.vector.tensor_tensor(sh[:, b % 2, :, :], S, mx[:, b % 2, :].unsqueeze(2).to_broadcast([P, HEADS, WT]), ALU.subtract).then_inc(sh_ready, 1)

            def evacuate(i, b, r):
                if again(i, 2):
                    dve.wait_ge(o_done, i - 1)
                dve.wait_ge(p_done, i + 1)
                nc.vector.tensor_copy(pT[:, b % 2, HG:, :].rearrange("p h n -> p (h n)"), psP[:, b % 2, 1, :]).then_inc(p_ready[1], 1)

            def normalise(i, b, r):
                O = psO[:, 0:HEADS * VW].rearrange("p (h d) -> p h d", d=VW)
                dve.wait_ge(o_done, i + 1)
                nc.vector.reciprocal(rs[:, b % 2, :], O[:, :, HD]).then_inc(rs_done, 1)
                if again(i, RING):
                    dve.wait_ge(out_done[b], r * 16)
                dve.wait_ge(rs_done, i + 1)
                nc.vector.tensor_tensor(ob[:, b, :, :], O[:, :, 0:HD], rs[:, b % 2, :].unsqueeze(2).to_broadcast([P, HEADS, HD]), ALU.mult).then_inc(o_ready, 1)

            dve.wait_ge(tab_in, 16)

            def body(tile):
                for k, stages in ((0, (rope1, rope2)), (1, (shift,)), (2, (evacuate,)), (3, (normalise,))):
                    at = tile(k)
                    if at is not None:
                        for stage in stages:
                            stage(*at)
            slots(dve, body)

        @block.scalar
        def _(act):
            def spread(i, b, r):
                act.wait_ge(a_done, i + 1)
                if again(i, 2):
                    act.wait_ge(s_done, i - 1)
                A = psA[:, :].rearrange("p (s n) -> p s n", n=P)
                nc.scalar.activation(qT[:, b % 2, :, :], A[:, 0:G, :], ACT.Copy)
                for h in range(HG):
                    on = slice(h * HD, (h + 1) * HD)
                    last = nc.scalar.activation(kT[on, b % 2, :, h, :], A[on, G:2 * G, :], ACT.Copy)
                last.then_inc(a_ready, 1)

            def exponent(i, b, r):
                act.wait_ge(sh_ready, i + 1)
                if again(i, 2):
                    act.wait_ge(p_done, i - 1)
                for w in range(2):
                    on = slice(w * WT, (w + 1) * WT)
                    last = nc.scalar.activation(pb[on, b % 2, :, w * WT:(w + 1) * WT], sh[on, b % 2, :, :], ACT.Exp, scale=SCALE)
                last.then_inc(e_ready, 1)

            def evacuate(i, b, r):
                if again(i, 2):
                    act.wait_ge(o_done, i - 1)
                act.wait_ge(p_done, i + 1)
                nc.scalar.activation(pT[:, b % 2, 0:HG, :].rearrange("p h n -> p (h n)"), psP[:, b % 2, 0, :], ACT.Copy).then_inc(p_ready[0], 1)

            act.wait_ge(zeroed, 3)

            def body(tile):
                for k, stage in ((0, spread), (1, exponent), (2, evacuate)):
                    if tile(k) is not None:
                        stage(*tile(k))
            slots(act, body)

        @block.tensor
        def _(pe):
            def transpose_qk(i, b, r):
                pe.wait_ge(r_ready, i + 1)
                if again(i, 1):
                    pe.wait_ge(a_ready, i)
                for q in range(2 * G):
                    last = nc.tensor.transpose(psA[:, q * P:(q + 1) * P], rqk[:, b % 2, q * P:(q + 1) * P], ident)
                last.then_inc(a_done, 1)

            def scores(i, b, r):
                pe.wait_ge(a_ready, i + 1)
                if again(i, 2):
                    pe.wait_ge(sh_ready, i - 1)
                for g in range(G):
                    for w in range(2):
                        on = slice(w * WT, (w + 1) * WT)
                        last = nc.tensor.matmul(psS[on, b % 2, g * HG * WT:(g + 1) * HG * WT], qT[:, b % 2, g, on], kT[:, b % 2, g, :, on],
                                                start=True, stop=True)
                last.then_inc(s_done, 1)

            def transpose_p(i, b, r):
                pe.wait_ge(e_ready, i + 1)
                if again(i, 2):
                    pe.wait_ge(p_ready[0], i - 1)
                    pe.wait_ge(p_ready[1], i - 1)
                for h in range(HEADS):
                    last = nc.tensor.transpose(psP[:, b % 2, h // HG, h % HG * P:(h % HG + 1) * P], pb[:, b % 2, h, :], ident)
                last.then_inc(p_done, 1)

            def values(i, b, r):
                pe.wait_ge(p_ready[0], i + 1)
                pe.wait_ge(p_ready[1], i + 1)
                pe.wait_ge(vx_ready, i + 1)
                if again(i, 1):
                    pe.wait_ge(o_ready, i)
                for h in range(HEADS):
                    last = nc.tensor.matmul(psO[:, h * VW:(h + 1) * VW], pT[:, b % 2, h, :], vx[:, b, h, :], start=True, stop=True)
                last.then_inc(o_done, 1)

            pe.wait_ge(zeroed, 3)

            def body(tile):
                for k, stage in ((0, transpose_qk), (1, scores), (2, transpose_p), (3, values)):
                    if tile(k) is not None:
                        stage(*tile(k))
            slots(pe, body)


def layer2_combine(nc, sem, X, pos, pmax, Ps, ident):
    RING = 4
    with ExitStack() as ctx:
        g = ctx.enter_context(nc.sbuf_tensor("g2", [P, RING, C], F32))
        gs = ctx.enter_context(nc.sbuf_tensor("gs2", [P, RING, C], F32))
        ps = ctx.enter_context(nc.psum_tensor("psg", [P, RING, NT], F32))
        g_in = [sem(f"c2_in{b}") for b in range(RING)]
        s_ready = sem("c2_scaled")
        t_done = sem("c2_t")
        x_done = sem("c2_x")
        block = ctx.enter_context(nc.Block())

        @block.gpsimd
        def _(pool):
            for i in range(PAIRS):
                if i >= RING:
                    pool.wait_ge(s_ready, i - RING + 1)
                nc.gpsimd.indirect_dma_start(out=g[:, i % RING, :], out_offset=None, in_=Ps,
                                             in_offset=bass.IndirectOffsetOnAxis(ap=pos[:, i:i + 1], axis=0)).then_inc(g_in[i % RING], 16)

        @block.scalar
        def _(act):
            for i in range(PAIRS):
                act.wait_ge(g_in[i % RING], 16 * (i // RING + 1))
                if i >= RING:
                    act.wait_ge(t_done, i - RING + 1)
                nc.scalar.activation(gs[:, i % RING, :], g[:, i % RING, :], ACT.Copy, scale=pmax[:, i:i + 1]).then_inc(s_ready, 1)

        @block.tensor
        def _(pe):
            for i in range(PAIRS):
                pe.wait_ge(s_ready, i + 1)
                if i >= RING:
                    pe.wait_ge(x_done, CC * (i - RING + 1))
                for c in range(CC):
                    last = nc.tensor.transpose(ps[:, i % RING, c * P:(c + 1) * P], gs[:, i % RING, c * P:(c + 1) * P], ident)
                last.then_inc(t_done, 1)

        @block.vector
        def _(dve):
            per = NT // P
            for i in range(PAIRS):
                dve.wait_ge(t_done, i + 1)
                for c in range(CC):
                    x = by_window(X[:, c, i // per * NT:(i // per + 1) * NT])[:, 2 * (i % per):2 * (i % per) + 2, :, :]
                    nc.vector.tensor_tensor(x, ps[:, i % RING, c * P:(c + 1) * P].rearrange("p (w r c) -> p w r c", r=WIN, c=WIN), x,
                                            ALU.add).then_inc(x_done, 1)


def layer3_chain(nc, sem, X, w1, b1, w2, b2, w3row, w3col, b3, ident, group_avg, eps_col, out):
    EX = w1.shape[1]
    ROUNDS = C // EX
    PW = W + 2
    HALF = TILES // 2
    with ExitStack() as ctx:
        def sb(name, shape, dt):
            return ctx.enter_context(nc.sbuf_tensor(name, shape, dt))

        xn = sb("xn3", [P, CC, N], F32)
        A = sb("A3", [P, CC, N], F32)
        B0 = sb("B0", [P, PW, PW], F32)
        B1 = sb("B1", [P, PW, PW], F32)
        B2 = sb("B2", [P, PW, PW], F32)
        S2 = sb("S2", [P, HALF, NT], F32)
        U = sb("U3", [P, HALF, NT], F32)
        w1s = sb("w1s", [P, CC, EX], F32)
        w2s = sb("w2s", [P, CC, 9, EX], F32)
        b12 = sb("b12", [P, 2], F32)
        w3r = sb("w3r", [P, C], F32)
        w3c = sb("w3c", [P, CC], F32)
        b3c = sb("b3c", [P, 1], F32)
        grow = sb("grow", [P, C], F32)
        step = sb("step3", [P, CC + 1, C], F32)
        MT3 = sb("MT3", [P, CC + 1, C], F32)
        ccol = sb("ccol", [P, CC], F32)
        one = sb("one3", [1, 1], F32)
        stats = sb("stats3", [P, CC, TILES, 6], F32)
        aggr = sb("aggr3", [P, CC, 2], F32)
        cols = sb("cols3", [P, 8, 2], F32)
        banks = [ctx.enter_context(nc.psum_tensor(f"bank3_{i}", [P, NT], F32)) for i in range(7)]
        ps = ctx.enter_context(nc.psum_tensor("ps3", [P, NT], F32))

        w_in = sem("l3_w_in")
        pads_zero = sem("l3_pads")
        xn_ready = sem("l3_xn")
        a0_ready = sem("l3_a0")
        y_ready = sem("l3_y")
        pair_done = sem("l3_pairs")
        a_ready = sem("l3_a")
        relu_done = sem("l3_relu")
        z_ready = sem("l3_z")
        u_ready = sem("l3_u")
        z_copied = sem("l3_z_copied")
        mat_step = sem("l3_mat")
        col_done = sem("l3_col")
        ccol_ready = sem("l3_ccol")
        last_relu = sem("l3_last_relu")
        m_done = sem("l3_m")
        o_ready = sem("l3_out_ready")
        x_out = sem("l3_x_out")
        gn_vec, gn_pe, gn_act, gn_wait = group_norm_stats(nc, "gn3", sem, X, stats, aggr, group_avg, ps, cols)
        block = ctx.enter_context(nc.Block())
        LOADS = 10
        MAT_STEPS = 11
        STAGES = [(B2, 1), (B0, 0), (B1, 0), (B0, 0), (B2, 1)]

        def lanes(h):
            return slice(h * EX, (h + 1) * EX)

        def rows(B, half, t):
            return B[lanes(half), 1 + t * TR:1 + (t + 1) * TR, 1:1 + W]

        def as_rows(ap):
            return ap.rearrange("p (h w) -> p h w", w=W)

        def pairs(stage, j):
            return (ROUNDS + stage) * HALF + j + 1

        @block.sync
        def _(sp):
            loads = [(w1s[:, :, :], w1.rearrange("(c p) m -> p c m", p=P))]
            loads += [(w2s[:, c, :, :], w2[:, c * P:(c + 1) * P, :].rearrange("t p m -> p t m")) for c in range(CC)]
            for h in range(2):
                loads += [(b12[lanes(h), 0:1], b1), (b12[lanes(h), 1:2], b2)]
            loads += [(w3r[:, :], w3row), (w3c[:, :], w3col), (b3c[:, :], b3)]
            assert len(loads) == LOADS
            for dst, src in loads:
                sp.dma_start(dst, src).then_inc(w_in, 16)
            for t in range(TILES):
                sp.wait_ge(o_ready, (t + 1) * CC)
                for c in range(CC):
                    sp.dma_start(out[c * P:(c + 1) * P, t * NT:(t + 1) * NT], X[:, c, t * NT:(t + 1) * NT]).then_inc(x_out, 16)
            sp.wait_ge(x_out, 16 * CC * TILES)

        @block.gpsimd
        def _(pool):
            for B in (B0, B1, B2):
                nc.gpsimd.memset(B[:, :, :].rearrange("p h w -> p (h w)"), 0.0).then_inc(pads_zero, 1)
            nc.gpsimd.memset(one[:, :], 1.0).then_inc(pads_zero, 1)
            for c in range(CC):
                for h in range(2):
                    part = slice(h * (N // 2), (h + 1) * (N // 2))
                    pool.wait_ge(xn_ready, CC * c + h + 1)
                    if c == 0 and h == 0:
                        pool.wait_ge(a0_ready, CC)
                    nc.gpsimd.tensor_tensor(X[:, c, part], X[:, c, part], xn[:, c, part], ALU.add).then_inc(y_ready, 1)
            for t in range(TILES):
                pool.wait_ge(z_ready, TILES + t + 1)
                pool.wait_ge(pair_done, pairs(1, min((t + 1) // 2, HALF - 1)))
                nc.gpsimd.tensor_copy(rows(B0, 0, t), rows(B1, 0, t)).then_inc(z_copied, 1)

        @block.scalar
        def _(act):
            gn_act(act, eps_col)
            gn_wait(act)
            act.wait_ge(w_in, 16 * LOADS)
            for c in range(CC):
                for h in range(2):
                    part = slice(h * (N // 2), (h + 1) * (N // 2))
                    nc.scalar.activation(xn[:, c, part], X[:, c, part], ACT.Identity, scale=cols[:, 0, c:c + 1],
                                         bias=cols[:, 1, c:c + 1]).then_inc(xn_ready, 1)
            for i in range(ROUNDS):
                for j in range(HALF):
                    act.wait_ge(pair_done, i * HALF + j + 1)
                    for h in range(2):
                        t = 2 * j + h
                        nc.scalar.activation(A[lanes(i % 2), i // 2, t * NT:(t + 1) * NT], banks[j][lanes(h), :], ACT.Identity,
                                             bias=b12[lanes(h), 0:1]).then_inc(a_ready, 1)
            for t in range(TILES):
                part = slice(t * NT, (t + 1) * NT)
                act.wait_ge(z_ready, 3 * TILES + t + 1)
                act.wait_ge(z_copied, t + 1)
                nc.scalar.activation(as_rows(A[:, 0, part]), B0[:, 1 + t * TR:1 + (t + 1) * TR, 1:1 + W], ACT.Relu).then_inc(last_relu, 1)
                nc.scalar.activation(as_rows(A[lanes(0), 1, part]), rows(B2, 0, t), ACT.Relu).then_inc(last_relu, 1)
            for t in range(TILES):
                part = slice(t * NT, (t + 1) * NT)
                act.wait_ge(z_ready, 4 * TILES + t + 1)
                nc.scalar.activation(A[lanes(1), 1, part], A[lanes(1), 1, part], ACT.Relu).then_inc(last_relu, 1)

        @block.tensor
        def _(pe):
            gn_pe(pe)
            pe.wait_ge(w_in, 16 * LOADS)
            pe.wait_ge(a0_ready, CC)
            for i in range(ROUNDS):
                for j in range(HALF):
                    if i:
                        pe.wait_ge(a_ready, (i - 1) * TILES + 2 * j + 2)
                    for c in range(CC):
                        for h in range(2):
                            t = 2 * j + h
                            last = nc.tensor.matmul(banks[j][lanes(h), :], w1s[:, c, :], A[:, c, t * NT:(t + 1) * NT],
                                                    start=(c == 0), stop=(c == CC - 1))
                    last.then_inc(pair_done, 1)
            pe.wait_ge(mat_step, MAT_STEPS)
            pe.wait_ge(pads_zero, 4)
            for c in range(CC):
                last = nc.tensor.matmul(ps[:, c:c + 1], MT3[0:1, CC, c * P:(c + 1) * P], one[0:1, 0:1], start=True, stop=True)
            last.then_inc(col_done, 1)
            pe.wait_ge(a_ready, ROUNDS * TILES)
            for s, (B, c) in enumerate(STAGES):
                for j in range(HALF):
                    reads = min(2 * j + 3, TILES)
                    if s < 2:
                        pe.wait_ge(relu_done, 3 * reads)
                    if s > 0:
                        pe.wait_ge(z_ready, (s - 1) * TILES + (reads if s > 1 else 2 * j + 2))
                    if s == 3:
                        pe.wait_ge(z_copied, reads)
                    for tap in range(9):
                        dy, dx = divmod(tap, 3)
                        for h in range(2):
                            t = 2 * j + h
                            last = nc.tensor.matmul(banks[j][lanes(h), :], w2s[:, c, tap, :],
                                                    B[:, t * TR + dy:t * TR + dy + TR, dx:dx + W],
                                                    start=(tap == 0), stop=(tap == 8))
                    last.then_inc(pair_done, 1)
            for t in range(TILES):
                pe.wait_ge(last_relu, 2 * TILES + t + 1)
                for o in range(CC):
                    r = t * CC + o
                    if r >= 3:
                        pe.wait_ge(o_ready, r - 2)
                    for c in range(CC):
                        last = nc.tensor.matmul(banks[4 + r % 3][:, :], MT3[:, c, o * P:(o + 1) * P], A[:, c, t * NT:(t + 1) * NT],
                                                start=(c == 0), stop=(c == CC - 1))
                    last.then_inc(m_done, 1)

        @block.vector
        def _(dve):
            gn_vec(dve)
            for c in range(CC):
                nc.vector.tensor_scalar(out=A[:, c, :], in0=X[:, c, :], scalar1=cols[:, 0, c:c + 1], scalar2=cols[:, 1, c:c + 1],
                                        op0=ALU.mult, op1=ALU.add).then_inc(a0_ready, 1)
            dve.wait_ge(w_in, 16 * LOADS)
            chain = Chain(dve, mat_step)
            chain.done(nc.vector.tensor_scalar(out=grow[:, :], in0=w3r[:, :], scalar1=1.0, scalar2=None, op0=ALU.add))
            chain.done(nc.vector.memset(step[:, :, :], 0.0))
            chain.wait()
            for c in range(CC):
                part = slice(c * P, (c + 1) * P)
                chain.done(nc.vector.scalar_tensor_tensor(out=step[:, c, part], in0=ident, scalar=-1.0, in1=w3r[:, part],
                                                          op0=ALU.mult, op1=ALU.mult))
            chain.done(nc.vector.tensor_scalar(out=step[:, CC, :], in0=w3r[:, :], scalar1=b3c[:, 0:1], scalar2=None, op0=ALU.mult))
            chain.done(nc.vector.tensor_copy(MT3[:, 0:CC, 0], w3c[:, :]))
            chain.done(nc.vector.memset(MT3[:, CC, 0:1], 0.0))
            chain.wait()
            for c in range(CC + 1):
                chain.done(nc.vector.tensor_tensor_scan(out=MT3[:, c, 1:C], data0=grow[:, 0:C - 1], data1=step[:, c, 0:C - 1],
                                                        initial=w3c[:, c:c + 1] if c < CC else 0.0, op0=ALU.mult, op1=ALU.add))
            chain.wait()
            chain.done(nc.vector.tensor_scalar(out=MT3[:, CC, :], in0=MT3[:, CC, :], scalar1=b3c[:, 0:1], scalar2=None, op0=ALU.add))
            assert chain.n == MAT_STEPS
            dve.wait_ge(pads_zero, 3)
            for t in range(TILES):
                part = slice(t * NT, (t + 1) * NT)
                dve.wait_ge(a_ready, (ROUNDS - 1) * TILES + t + 1)
                for dst, src in ((B0[:, 1 + t * TR:1 + (t + 1) * TR, 1:1 + W], A[:, 0, part]),
                                 (B2[:, 1 + t * TR:1 + (t + 1) * TR, 1:1 + W], A[:, 1, part]),
                                 (rows(B1, 1, t), A[lanes(1), 0, part])):
                    nc.vector.tensor_scalar(out=dst, in0=as_rows(src), scalar1=0.0, scalar2=None, op0=ALU.max).then_inc(relu_done, 1)
            dve.wait_ge(col_done, 1)
            nc.vector.tensor_copy(ccol[:, :], ps[:, 0:CC]).then_inc(ccol_ready, 1)

            def biased(dst, t, share):
                j, h = divmod(t, 2)
                nc.vector.scalar_tensor_tensor(out=dst, in0=as_rows(banks[j][lanes(h), :]), scalar=b12[lanes(h), 1:2],
                                               in1=as_rows(share[lanes(h), j, :]), op0=ALU.add, op1=ALU.add).then_inc(z_ready, 1)

            for s in range(len(STAGES)):
                for t in range(TILES):
                    j, h = divmod(t, 2)
                    dve.wait_ge(pair_done, pairs(s, j))
                    if s == 0:
                        nc.vector.tensor_copy(S2[lanes(h), j, :], banks[j][lanes(h), :]).then_inc(z_ready, 1)
                    elif s == 1:
                        dve.wait_ge(z_ready, t + 1)
                        biased(rows(B1, 0, t), t, S2)
                    elif s == 2:
                        biased(rows(B0, 1, t), t, S2)
                    elif s == 3:
                        nc.vector.tensor_copy(U[lanes(h), j, :], banks[j][lanes(h), :]).then_inc(u_ready, 1)
                        biased(rows(B2, 0, t), t, S2)
                    else:
                        dve.wait_ge(u_ready, t + 1)
                        biased(as_rows(A[lanes(1), 1, t * NT:(t + 1) * NT]), t, U)
            dve.wait_ge(y_ready, 2 * CC)
            dve.wait_ge(ccol_ready, 1)
            for t in range(TILES):
                for o in range(CC):
                    r = t * CC + o
                    xt = X[:, o, t * NT:(t + 1) * NT]
                    dve.wait_ge(m_done, r + 1)
                    nc.vector.scalar_tensor_tensor(out=xt, in0=banks[4 + r % 3][:, :], scalar=ccol[:, o:o + 1], in1=xt,
                                                   op0=ALU.add, op1=ALU.add).then_inc(o_ready, 1)


def build(nc, a, out):
    with ExitStack() as ctx:
        def sem(name):
            return nc.alloc_semaphore(name=name)

        X = ctx.enter_context(nc.sbuf_tensor("X", [P, CC, N], F32))
        consts = ctx.enter_context(nc.sbuf_tensor("consts", [P, 3, P], F32))
        pos = ctx.enter_context(nc.sbuf_tensor("pos", [P, PAIRS], U32))
        pmax = ctx.enter_context(nc.sbuf_tensor("pmax", [P, PAIRS], F32))
        expert = ctx.enter_context(nc.sbuf_tensor("expert", [P, SLOTS], U32))
        eps = ctx.enter_context(nc.sbuf_tensor("eps", [P, 1], F32))
        Qhl = nc.dram_tensor("q_parts", [2, C, N], F16).ap()
        Xs = nc.dram_tensor("tokens_by_expert", [SLOTS * P, C], F32).ap()
        QKVs = nc.dram_tensor("qkv_by_expert", [SLOTS * P, 3 * C], F32).ap()
        Os = nc.dram_tensor("attended_by_expert", [SLOTS * P, C], F32).ap()
        Ps = nc.dram_tensor("projected_by_expert", [SLOTS * P, C], F32).ap()
        Khl = nc.dram_tensor("k_parts", [2, C, N], F16).ap()
        consts_in = sem("consts_in")
        eps_set = sem("eps_set")
        with nc.Block() as block:
            @block.sync
            def _(sp):
                sp.dma_start(consts[:, :, :], a["consts"]).then_inc(consts_in, 16)
                sp.wait_ge(consts_in, 16)

            @block.vector
            def _(dve):
                nc.vector.memset(eps[:, :], GN_EPS).then_inc(eps_set, 1)
                dve.wait_ge(eps_set, 1)
        ident, ones_head, group_avg = consts[:, 0, :], consts[:, 1, :], consts[:, 2, :]
        with nc.cleanup_on_exit():
            layer0_conv(nc, sem, X, a["x"], (a["L0_conv_W1"], a["L0_conv_W3"], a["L0_conv_W5"]), a["L0_conv_Wdw"],
                        a["temp"], ones_head, group_avg, eps[:, 0:1], Qhl, Khl, consts_in)
        with nc.cleanup_on_exit():
            layer0_attention(nc, sem, X, a["x"], Qhl, Khl, a["L0_conv_Wproj"], ident)
        with nc.cleanup_on_exit():
            layer1_codebook(nc, sem, X, Xs, Os, a["codes"], a["codes_t"], ident, group_avg, eps[:, 0:1])
        with nc.cleanup_on_exit():
            layer2_route(nc, sem, X, a["rw1"], a["rb1"], a["rw2"], a["rb2"], a, ident, group_avg, eps[:, 0:1], pos, pmax, expert, Xs)
            layer2_sorted_linear(nc, sem, "qkv", Xs, QKVs, a["qkv_w"], a["qkv_b"], expert, ident)
        with nc.cleanup_on_exit():
            layer2_windows(nc, sem, pos, QKVs, Os, a["rope"], ident)
            layer2_sorted_linear(nc, sem, "proj", Os, Ps, a["proj_w"], a["proj_b"], expert, ident)
        with nc.cleanup_on_exit():
            layer2_combine(nc, sem, X, pos, pmax, Ps, ident)
            layer3_chain(nc, sem, X, a["w1"], a["b1"], a["w2"], a["b2"], a["w3row"], a["w3col"], a["b3"], ident, group_avg, eps[:, 0:1], out)


def kernel(**inputs):
    import numpy as np
    import concourse.bacc as bacc
    from concourse.bass_utils import run_bass_kernel_spmd

    a = {name: np.asarray(value) for name, value in inputs.items()}
    arrays = {
        "x": a["x"].reshape(N, C).T,
        "L0_conv_W1": a["L0_conv_W1"].reshape(C, C, 1).transpose(1, 2, 0),
        "L0_conv_W3": a["L0_conv_W3"].reshape(C, C, 9).transpose(1, 2, 0),
        "L0_conv_W5": a["L0_conv_W5"].reshape(C, C, 25).transpose(1, 2, 0),
        "L0_conv_Wdw": a["L0_conv_Wdw"].reshape(3 * C, 9),
        "L0_conv_Wproj": a["L0_conv_Wproj"].reshape(C, C).T,
        "temp": np.repeat(a["L0_conv_temperature"].reshape(HEADS), HD).reshape(CC, P).T,
        "rw1": a["L2_conv_router_w1"].T,
        "rb1": a["L2_conv_router_b1"].reshape(-1, 1),
        "rw2": a["L2_conv_router_w2"].T,
        "rb2": a["L2_conv_router_b2"].reshape(1, -1),
        "qkv_w": a["L2_conv_qkv_w"].reshape(EXPERTS * 3 * C, C).T,
        "qkv_b": a["L2_conv_qkv_b"].reshape(-1),
        "proj_w": a["L2_conv_proj_w"].reshape(EXPERTS * C, C).T,
        "proj_b": a["L2_conv_proj_b"].reshape(-1),
        "w1": a["L3_conv_w1"].reshape(C, -1),
        "b1": a["L3_conv_b1"].reshape(-1, 1),
        "w2": a["L3_conv_w2"].reshape(9, C, -1),
        "b2": a["L3_conv_b2"].reshape(-1, 1),
        "w3row": np.broadcast_to(a["L3_conv_w3"].reshape(1, C), (P, C)),
        "w3col": a["L3_conv_w3"].reshape(CC, P).T,
        "b3": np.broadcast_to(a["L3_conv_b3"].reshape(1, 1), (P, 1)),
        "codes": a["L1_conv_embeddings"],
        "codes_t": a["L1_conv_embeddings"].T,
    }
    p = np.arange(P)
    same = lambda w: (p[:, None] // w == p[None, :] // w)
    arrays["consts"] = np.stack([np.eye(P), same(HD), same(C // 32) / (C // 32)], axis=1).astype(np.float32)
    arrays["tri"] = np.stack([p[:, None] <= p[None, :], np.ones((P, P))], axis=1).astype(np.float32)
    arrays["iota"] = np.broadcast_to(np.arange(EXPERTS, dtype=np.float32) + EXPERTS, (P, PAIRS, EXPERTS))
    tile = np.where(np.arange(EXPERTS) < EXPERTS - 1, np.arange(SLOTS)[:, None], -1)
    arrays["tile"] = np.broadcast_to(tile.astype(np.float32), (P, SLOTS, EXPERTS))
    half = HD // 2
    inv = (1.0 / 10000.0 ** (np.arange(0, half, 2, dtype=np.float32) / np.float32(half))).astype(np.float32)
    row, col = p // WIN % WIN, p % WIN
    ang = np.concatenate([row[:, None].astype(np.float32) * inv, col[:, None].astype(np.float32) * inv], axis=1)
    cos = np.repeat(np.cos(ang), 2, axis=1)
    sin = np.repeat(np.sin(ang), 2, axis=1) * np.where(np.arange(HD) % 2, 1, -1)
    arrays["rope"] = np.stack([np.tile(cos, 2 * HEADS), np.tile(sin, 2 * HEADS)], axis=1).astype(np.float32)
    arrays = {name: np.ascontiguousarray(value) for name, value in arrays.items()}
    nc = bacc.Bacc("TRN2", target_bir_lowering=False, num_devices=1)
    args = {name: nc.dram_tensor(name + "_dram", v.shape, mybir.dt.from_np(v.dtype), kind="ExternalInput").ap()
            for name, v in arrays.items()}
    out = nc.dram_tensor("out_dram", (C, N), F32, kind="ExternalOutput").ap()
    build(nc, args, out)
    r = run_bass_kernel_spmd(nc, [{name + "_dram": v for name, v in arrays.items()}], core_ids=[0])
    return r.results[0]["out_dram"].T.reshape(1, H, W, C)
```

```python
from contextlib import ExitStack

import concourse.bass as bass
from concourse import mybir
from concourse.alu_op_type import AluOpType as ALU

ACT = mybir.ActivationFunctionType
AX_X = mybir.AxisListType.X
F32 = mybir.dt.float32
F16 = mybir.dt.float16
U32 = mybir.dt.uint32
I32 = mybir.dt.int32
ds = bass.ds

P = 128
H = W = 64
C = 256
CC = C // P
N = H * W
NT = 512
TILES = N // NT
TR = NT // W
HD = 32
HEADS = C // HD
GN_EPS = 1e-5


class Chain:

    def __init__(self, engine, sem):
        self.engine, self.sem, self.n = engine, sem, 0

    def done(self, ins):
        ins.then_inc(self.sem, 1)
        self.n += 1
        return ins

    def wait(self, back=0):
        self.engine.wait_ge(self.sem, self.n - back)


def group_norm_stats(nc, name, sem, X, stats, aggr, group_avg, ps_stat, cols, dve_wait=None):
    chan_ready = sem(name + "_channel_means")
    mean_ready = sem(name + "_group_means")
    dev_ready = sem(name + "_channel_vars")
    var_ready = sem(name + "_group_vars")
    std_ready = sem(name + "_group_std")
    dve_step = sem(name + "_dve_step")

    def vector(dve):
        chain = Chain(dve, dve_step)
        for c in range(CC):
            for t in range(TILES):
                chain.done(nc.vector.bn_stats(stats[:, c, t, :], X[:, c, t * NT:(t + 1) * NT]))
        chain.wait()
        for c in range(CC):
            chain.done(nc.vector.bn_aggr(aggr[:, c, 0:2], stats[:, c, :, :].rearrange("p t s -> p (t s)")))
        chain.wait()
        nc.vector.tensor_copy(cols[:, 2, :], aggr[:, :, 0]).then_inc(chan_ready, 1)
        dve.wait_ge(mean_ready, 1)
        chain.done(nc.vector.tensor_copy(cols[:, 3, :], ps_stat[:, 0:CC]))
        chain.wait()
        chain.done(nc.vector.tensor_tensor(cols[:, 4, :], aggr[:, :, 0], cols[:, 3, :], ALU.subtract))
        chain.wait()
        chain.done(nc.vector.tensor_tensor(cols[:, 5, :], cols[:, 4, :], cols[:, 4, :], ALU.mult))
        chain.wait()
        nc.vector.tensor_tensor(cols[:, 6, :], cols[:, 5, :], aggr[:, :, 1], ALU.add).then_inc(dev_ready, 1)
        dve.wait_ge(std_ready, 1)
        chain.done(nc.vector.reciprocal(cols[:, 0, :], cols[:, 7, :]))
        chain.wait()
        chain.done(nc.vector.scalar_tensor_tensor(out=cols[:, 1, :], in0=cols[:, 3, :], scalar=-1.0,
                                                  in1=cols[:, 0, :], op0=ALU.mult, op1=ALU.mult))
        chain.wait()
        assert chain.n == CC * TILES + 7

    def tensor(pe):
        pe.wait_ge(chan_ready, 1)
        nc.tensor.matmul(ps_stat[:, 0:CC], group_avg[:, :], cols[:, 2, :], start=True, stop=True).then_inc(mean_ready, 1)
        pe.wait_ge(dev_ready, 1)
        nc.tensor.matmul(ps_stat[:, CC:2 * CC], group_avg[:, :], cols[:, 6, :], start=True, stop=True).then_inc(var_ready, 1)

    def scalar(act, eps_col):
        act.wait_ge(var_ready, 1)
        nc.scalar.activation(cols[:, 7, :], ps_stat[:, CC:2 * CC], ACT.Sqrt, bias=eps_col).then_inc(std_ready, 1)

    def wait_ready(engine):
        engine.wait_ge(dve_step, CC * TILES + 7)

    return vector, tensor, scalar, wait_ready


def layer0_conv(nc, sem, X, x, w_convs, w_dw, temp, ones_head, group_avg, eps_col, Qhl, Khl, consts_ready):
    KS = (1, 3, 5)
    TAPS = [k * k for k in KS]
    UNIT0 = [0, CC * TAPS[0], CC * (TAPS[0] + TAPS[1])]
    UNITS = CC * sum(TAPS)
    G = 4
    PIECES = [[(UNIT0[k] + o, min(G, CC * TAPS[k] - o)) for o in range(0, CC * TAPS[k], G)] for k in range(3)]
    PIECE0 = [0, len(PIECES[0]), len(PIECES[0]) + len(PIECES[1]), sum(len(p) for p in PIECES)]
    PW = W + 4
    QW = W + 2
    ORDER = [(0, 0, 0), (1, 0, 1), (2, 0, 0), (0, 1, 1), (1, 1, 1), (2, 1, 1)]
    NB = 2
    QTR = 4
    QR = H // QTR
    SPLIT = 256.0
    XSCALE = 128.0
    WSCALE = 32768.0
    TMP = 8
    with ExitStack() as ctx:
        def sb(name, shape, dt):
            return ctx.enter_context(nc.sbuf_tensor(name, shape, dt))

        xh = sb("xh", [P, CC, PW, PW], F16)
        xl = sb("xl", [P, CC, PW, PW], F16)
        wraw = sb("wraw", [P, G + UNITS, C], F32)
        wparts = wraw[:, :, :].bitcast(F16)
        qpad = [sb(f"qpad{b}", [P, QW, QW], F32) for b in range(2)]
        sq = sb("sq", [P, N], F32)
        ones = sb("ones0", [P, P], F32)
        wd = sb("wd", [P, 3 * CC, 9], F32)
        tcol = sb("tcol", [P, CC], F32)
        stats = sb("stats0", [P, CC, TILES, 6], F32)
        aggr = sb("aggr0", [P, CC, 2], F32)
        cols = sb("cols0", [P, 8, 2], F32)
        xcols = sb("xcols0", [P, 2, 2], F32)
        wss = sb("wss", [P, PIECE0[3]], F32)
        wsum = sb("wsum", [P, 3], F32)
        wroot = sb("wroot", [P, 3], F32)
        wcols = sb("wcols", [P, 4, 3], F32)
        nrm = sb("nrm", [P, 2, NT], F32)
        qn = sb("qn", [P, 2, NT], F32)
        hi = sb("hi", [P, 2, NT], F16)
        lo = sb("lo", [P, 2, NT], F16)
        psc = ctx.enter_context(nc.psum_tensor("psc", [P, NB, NT], F32))
        pss = ctx.enter_context(nc.psum_tensor("pss", [P, 3, NT], F32))
        ps_stat = ctx.enter_context(nc.psum_tensor("ps_stat0", [P, NT], F32))

        x_in = sem("l0_x_in")
        small_in = sem("l0_small_in")
        w_in = [sem(f"l0_w{k}_in") for k in KS]
        ones_set = sem("l0_ones_set")
        xpad_zero = sem("l0_xpad_zero")
        qpad_zero = sem("l0_qpad_zero")
        xcols_ready = sem("l0_xcols")
        xn_ready = sem("l0_xn")
        xh_ready = sem("l0_xh")
        xl_ready = sem("l0_xl")
        wss_ready = sem("l0_wss")
        wsum_ready = sem("l0_wsum")
        wall_ready = sem("l0_wall")
        wroot_ready = sem("l0_wroot")
        wcols_step = sem("l0_wcols")
        wh_ready = sem("l0_wh")
        wl_ready = sem("l0_wl")
        conv_done = sem("l0_conv_tiles")
        evac_done = sem("l0_conv_evacuated")
        dw_step = sem("l0_dw_steps")
        sq_done = sem("l0_squares")
        ss_done = sem("l0_square_sums")
        nrm_done = sem("l0_norms")
        post_step = sem("l0_post_steps")
        split_out = [sem(f"l0_split_out{b}") for b in range(2)]
        gn_vec, gn_pe, gn_act, gn_wait = group_norm_stats(nc, "gn0", sem, X, stats, aggr, group_avg, ps_stat, cols)
        DW = QTR * 9
        POST = 5
        WSTEPS = 4
        SETS = ((0, 2), (2, 3))
        QK = [i for i, (kind, _, _) in enumerate(ORDER) if kind < 2]

        block = ctx.enter_context(nc.Block())

        @block.sync
        def _(sp):
            for c in range(CC):
                sp.dma_start(X[:, c, :], x[c * P:(c + 1) * P, :]).then_inc(x_in, 16)
            for k in range(3):
                for c in range(CC):
                    u = G + UNIT0[k] + c * TAPS[k]
                    sp.dma_start(wraw[:, u:u + TAPS[k], :], w_convs[k][c * P:(c + 1) * P, :, :]).then_inc(w_in[k], 16)
            sp.dma_start(wd[:, :, :], w_dw.rearrange("(c p) t -> p c t", p=P)).then_inc(small_in, 16)
            sp.dma_start(tcol[:, :], temp).then_inc(small_in, 16)
            for n, i in enumerate(QK):
                kind, cc, _ = ORDER[i]
                dst = (Qhl, Khl)[kind]
                with sp.Fori(0, TILES // 2) as t:
                    for b in range(2):
                        sp.wait_ge(post_step, t * (2 * POST) + ((b + 1 + n * TILES) * POST))
                        sp.dma_start(dst[0, cc * P:(cc + 1) * P, ds(t * (2 * NT) + b * NT, NT)], hi[:, b, :]).then_inc(split_out[b], 16)
                        sp.dma_start(dst[1, cc * P:(cc + 1) * P, ds(t * (2 * NT) + b * NT, NT)], lo[:, b, :]).then_inc(split_out[b], 16)
            for b in range(2):
                sp.wait_ge(split_out[b], 32 * (TILES // 2) * len(QK))

        @block.gpsimd
        def _(pool):
            nc.gpsimd.memset(ones[:, :], 1.0).then_inc(ones_set, 1)
            for part in (xh, xl):
                nc.gpsimd.memset(part[:, :, :, :].bitcast(F32).rearrange("p c h w -> p (c h w)"), 0.0).then_inc(xpad_zero, 1)
            for b in range(2):
                nc.gpsimd.memset(qpad[b][:, :, :].rearrange("p h w -> p (h w)"), 0.0).then_inc(qpad_zero, 1)
            pool.wait_ge(xpad_zero, 2)
            for t in range(TILES):
                for c in range(CC):
                    j = t * CC + c
                    pool.wait_ge(xn_ready, j + 1)
                    tmp = sq[:, j % TMP * NT:(j % TMP + 1) * NT].rearrange("p (h w) -> p h w", h=TR)
                    nc.gpsimd.tensor_copy(xh[:, c, 2 + t * TR:2 + (t + 1) * TR, 2:2 + W], tmp).then_inc(xh_ready, 1)
            pool.wait_ge(xl_ready, TILES * CC)
            for n, i in enumerate(QK):
                slot = ORDER[i][2]
                pool.wait_ge(dw_step, (i + 1) * DW)
                if n:
                    pool.wait_ge(ss_done, n * TILES)
                for h in range(2):
                    part = X[:, slot, h * (N // 2):(h + 1) * (N // 2)]
                    nc.gpsimd.tensor_tensor(sq[:, h * (N // 2):(h + 1) * (N // 2)], part, part, ALU.mult).then_inc(sq_done, 1)

        @block.tensor
        def _(pe):
            def weight_sums(s):
                a, b = SETS[s]
                pe.wait_ge(ones_set, 1)
                pe.wait_ge(wsum_ready, b)
                nc.tensor.matmul(ps_stat[:, 8 + a:8 + b], ones[:, :], wsum[:, a:b], start=True, stop=True).then_inc(wall_ready, 1)

            pe.wait_ge(consts_ready, 16)
            gn_pe(pe)
            weight_sums(0)

            def conv_tile(kind, cc, t, b):
                k = KS[kind]
                off = 2 - (k - 1) // 2
                n, total = 0, 3 * CC * k * k
                for c in range(CC):
                    for dy in range(k):
                        for dx in range(k):
                            u = UNIT0[kind] + c * TAPS[kind] + dy * k + dx
                            at = (slice(None), c, ds(t * TR + off + dy, TR), slice(off + dx, off + dx + W))
                            wh = wparts[:, u, cc * P:(cc + 1) * P]
                            wl = wparts[:, u, C + cc * P:C + (cc + 1) * P]
                            for weights, image in ((wh, xh), (wh, xl), (wl, xh)):
                                last = nc.tensor.matmul(psc[:, b, :], weights, image[at], start=(n == 0), stop=(n == total - 1))
                                n += 1
                last.then_inc(conv_done, 1)

            def conv_chunk(i, first=0, last=TILES):
                kind, cc, _ = ORDER[i]
                pe.wait_ge(wl_ready, PIECE0[kind + 1])
                with pe.Fori(first // NB, last // NB) as t:
                    for b in range(NB):
                        pe.wait_ge(evac_done, t * NB + (i * TILES + b - NB + 1))
                        conv_tile(kind, cc, t * NB + b, b)

            def square_sums(n):
                pe.wait_ge(sq_done, 2 * (n + 1))
                for t in range(TILES):
                    m = n * TILES + t
                    if m >= 3:
                        pe.wait_ge(nrm_done, m - 2)
                    nc.tensor.matmul(pss[:, m % 3, :], ones_head[:, :], sq[:, t * NT:(t + 1) * NT],
                                     start=True, stop=True).then_inc(ss_done, 1)

            pe.wait_ge(wl_ready, PIECE0[1])
            for t in range(TILES):
                pe.wait_ge(xl_ready, (t + 1) * CC)
                if t >= NB:
                    pe.wait_ge(evac_done, t - NB + 1)
                conv_tile(0, 0, t, t % NB)
            conv_chunk(1, 0, 6)
            weight_sums(1)
            conv_chunk(1, 6, TILES)
            square_sums(0)
            conv_chunk(2, 0, 4)
            square_sums(1)
            conv_chunk(2, 4, TILES)
            conv_chunk(3)
            conv_chunk(4)
            square_sums(2)
            conv_chunk(5, 0, 4)
            square_sums(3)
            conv_chunk(5, 4, TILES)

        @block.scalar
        def _(act):
            gn_act(act, eps_col)

            squares = pss[:, :, :].rearrange("p b n -> p (b n)")

            def sum_squares(s):
                for k in range(*SETS[s]):
                    act.wait_ge(w_in[k], 16 * CC)
                    for p, (u, n) in enumerate(PIECES[k]):
                        q = PIECE0[k] + p
                        if q:
                            act.wait_ge(wss_ready, q)
                        nc.scalar.activation(squares[:, 0:n * C], wraw[:, G + u:G + u + n, :].rearrange("p u c -> p (u c)"), ACT.Square,
                                             accum_out=wss[:, q:q + 1]).then_inc(wss_ready, 1)

            def root(s):
                a, b = SETS[s]
                act.wait_ge(wall_ready, s + 1)
                nc.scalar.activation(wroot[:, a:b], ps_stat[:, 8 + a:8 + b], ACT.Sqrt).then_inc(wroot_ready, 1)

            def high_parts(s):
                act.wait_ge(wcols_step, WSTEPS * (s + 1))
                for k in range(*SETS[s]):
                    for p, (u, n) in enumerate(PIECES[k]):
                        q = PIECE0[k] + p
                        if q:
                            act.wait_ge(wl_ready, q)
                        nc.scalar.activation(wparts[:, u:u + n, 0:C], wraw[:, G + u:G + u + n, :], ACT.Copy,
                                             scale=wcols[:, 2, k:k + 1]).then_inc(wh_ready, 1)

            def evacuate_tile(i, t, b):
                kind = ORDER[i][0]
                act.wait_ge(conv_done, t + (i * TILES + 1))
                nc.scalar.activation(qpad[i % 2][:, ds(t * TR + 1, TR), 1:1 + W], psc[:, b, :].rearrange("p (h w) -> p h w", h=TR),
                                     ACT.Copy, scale=wcols[:, 3, kind:kind + 1]).then_inc(evac_done, 1)

            def wait_qpad(i):
                if i < 2:
                    act.wait_ge(qpad_zero, i + 1)
                else:
                    act.wait_ge(dw_step, (i - 1) * DW)

            def evacuate(i, first=0, last=TILES):
                if first == 0:
                    wait_qpad(i)
                with act.Fori(first // NB, last // NB) as t:
                    for b in range(NB):
                        evacuate_tile(i, t * NB + b, b)

            def norms(n):
                for t in range(TILES):
                    m = n * TILES + t
                    act.wait_ge(ss_done, m + 1)
                    if m >= 2:
                        act.wait_ge(post_step, (m - 2) * POST + 3)
                    nc.scalar.activation(nrm[:, m % 2, :], pss[:, m % 3, :], ACT.Sqrt).then_inc(nrm_done, 1)

            sum_squares(0)
            root(0)
            act.wait_ge(xcols_ready, 1)
            for t in range(TILES):
                for c in range(CC):
                    j = t * CC + c
                    if j >= TMP:
                        act.wait_ge(xl_ready, j - TMP + 1)
                    nc.scalar.activation(sq[:, j % TMP * NT:(j % TMP + 1) * NT], X[:, c, t * NT:(t + 1) * NT], ACT.Identity,
                                         scale=xcols[:, 0, c:c + 1], bias=xcols[:, 1, c:c + 1]).then_inc(xn_ready, 1)
                if t == 0:
                    high_parts(0)
            wait_qpad(0)
            for t in range(TILES):
                evacuate_tile(0, t, t % NB)
            evacuate(1, 0, 4)
            sum_squares(1)
            evacuate(1, 4, 6)
            root(1)
            high_parts(1)
            evacuate(1, 6, TILES)
            norms(0)
            evacuate(2, 0, 4)
            norms(1)
            evacuate(2, 4, TILES)
            evacuate(3)
            evacuate(4)
            norms(2)
            evacuate(5, 0, 4)
            norms(3)
            evacuate(5, 4, TILES)

        @block.vector
        def _(dve):
            def sum_weights(s):
                a, b = SETS[s]
                dve.wait_ge(wss_ready, PIECE0[b])
                for k in range(a, b):
                    ins = nc.vector.tensor_reduce(out=wsum[:, k:k + 1], in_=wss[:, PIECE0[k]:PIECE0[k + 1]], axis=AX_X, op=ALU.add)
                    ins.then_inc(wsum_ready, 1)

            def weight_cols(s):
                a, b = SETS[s]
                base = WSTEPS * s
                dve.wait_ge(wroot_ready, s + 1)
                nc.vector.tensor_scalar(out=wcols[:, 0, a:b], in0=wroot[:, a:b], scalar1=1e-15, scalar2=None, op0=ALU.max).then_inc(wcols_step, 1)
                dve.wait_ge(wcols_step, base + 1)
                nc.vector.reciprocal(wcols[:, 1, a:b], wcols[:, 0, a:b]).then_inc(wcols_step, 1)
                dve.wait_ge(wcols_step, base + 2)
                nc.vector.tensor_scalar(out=wcols[:, 2, a:b], in0=wcols[:, 1, a:b], scalar1=WSCALE, scalar2=None, op0=ALU.mult).then_inc(wcols_step, 1)
                nc.vector.tensor_scalar(out=wcols[:, 3, a:b], in0=wcols[:, 0, a:b], scalar1=1.0 / (WSCALE * XSCALE), scalar2=None,
                                        op0=ALU.mult).then_inc(wcols_step, 1)
                dve.wait_ge(wcols_step, base + WSTEPS)

            def low_parts(s):
                for k in range(*SETS[s]):
                    for p, (u, n) in enumerate(PIECES[k]):
                        dve.wait_ge(wh_ready, PIECE0[k] + p + 1)
                        nc.vector.scalar_tensor_tensor(out=wparts[:, u:u + n, C:2 * C], in0=wraw[:, G + u:G + u + n, :], scalar=wcols[:, 2, k:k + 1],
                                                       in1=wparts[:, u:u + n, 0:C], op0=ALU.mult, op1=ALU.subtract).then_inc(wl_ready, 1)

            dve.wait_ge(x_in, 16 * CC)
            gn_vec(dve)
            nc.vector.tensor_scalar(out=xcols[:, :, :], in0=cols[:, 0:2, :], scalar1=XSCALE, scalar2=None, op0=ALU.mult).then_inc(xcols_ready, 1)
            sum_weights(0)
            weight_cols(0)
            low_parts(0)
            dve.wait_ge(xpad_zero, 2)
            for t in range(TILES):
                for c in range(CC):
                    j = t * CC + c
                    dve.wait_ge(xn_ready, j + 1)
                    dve.wait_ge(xh_ready, j + 1)
                    tmp = sq[:, j % TMP * NT:(j % TMP + 1) * NT].rearrange("p (h w) -> p h w", h=TR)
                    at = (slice(None), c, slice(2 + t * TR, 2 + (t + 1) * TR), slice(2, 2 + W))
                    nc.vector.tensor_tensor(xl[at], tmp, xh[at], ALU.subtract).then_inc(xl_ready, 1)
            dve.wait_ge(small_in, 32)

            def taps(i, q, base):
                kind, cc, slot = ORDER[i]
                out = X[:, slot, ds(q * (QR * W), QR * W)].rearrange("p (h w) -> p h w", h=QR)
                for tap in range(9):
                    dy, dx = divmod(tap, 3)
                    src = qpad[i % 2][:, ds(q * QR + dy, QR), dx:dx + W]
                    col = wd[:, kind * CC + cc, tap:tap + 1]
                    if tap == 0:
                        ins = nc.vector.tensor_scalar(out=out, in0=src, scalar1=col, scalar2=None, op0=ALU.mult)
                    else:
                        dve.wait_ge(dw_step, base + tap)
                        ins = nc.vector.scalar_tensor_tensor(out=out, in0=src, scalar=col, in1=out, op0=ALU.mult, op1=ALU.add)
                    ins.then_inc(dw_step, 1)

            PER = TILES // QTR

            def quarter(i, q):
                last = q == QTR - 1
                dve.wait_ge(evac_done, (i + 1) * TILES if last else i * TILES + (q + 1) * PER + 1)
                taps(i, q, q * 9 + i * DW)

            def depthwise(i):
                with dve.Fori(0, QTR - 1) as q:
                    dve.wait_ge(evac_done, q * PER + (i * TILES + PER + 1))
                    taps(i, q, q * 9 + i * DW)
                quarter(i, QTR - 1)

            def normalise(n):
                i = QK[n]
                kind, cc, slot = ORDER[i]
                for t in range(TILES):
                    m = n * TILES + t
                    b = m % 2
                    base = m * POST
                    dve.wait_ge(nrm_done, m + 1)
                    nc.vector.tensor_scalar(out=nrm[:, b, :], in0=nrm[:, b, :], scalar1=1e-12, scalar2=1.0 / SPLIT,
                                            op0=ALU.max, op1=ALU.mult).then_inc(post_step, 1)
                    dve.wait_ge(post_step, base + 1)
                    nc.vector.reciprocal(nrm[:, b, :], nrm[:, b, :]).then_inc(post_step, 1)
                    dve.wait_ge(post_step, base + 2)
                    D = X[:, slot, t * NT:(t + 1) * NT]
                    if kind == 0:
                        ins = nc.vector.scalar_tensor_tensor(out=qn[:, b, :], in0=D, scalar=tcol[:, cc:cc + 1],
                                                             in1=nrm[:, b, :], op0=ALU.mult, op1=ALU.mult)
                    else:
                        ins = nc.vector.tensor_tensor(qn[:, b, :], D, nrm[:, b, :], ALU.mult)
                    ins.then_inc(post_step, 1)
                    dve.wait_ge(post_step, base + 3)
                    if m >= 2:
                        dve.wait_ge(split_out[b], 32 * (m // 2))
                    nc.vector.tensor_copy(hi[:, b, :], qn[:, b, :]).then_inc(post_step, 1)
                    dve.wait_ge(post_step, base + 4)
                    nc.vector.tensor_tensor(lo[:, b, :], qn[:, b, :], hi[:, b, :], ALU.subtract).then_inc(post_step, 1)

            depthwise(0)
            quarter(1, 0)
            sum_weights(1)
            quarter(1, 1)
            weight_cols(1)
            low_parts(1)
            quarter(1, 2)
            quarter(1, 3)
            normalise(0)
            normalise(1)
            depthwise(2)
            depthwise(3)
            normalise(2)
            depthwise(4)
            normalise(3)
            depthwise(5)


def layer0_attention(nc, sem, X, x, Qhl, Khl, w_proj, ident):
    SPLIT2 = 1.0 / (256.0 * 256.0)
    HG = 4
    GROUPS = HEADS // HG
    MT = N // P
    UN = 2 * MT
    UI = GROUPS * UN
    RING = 3
    PRING = 8
    AHEAD = 3
    POOL_U = [1, 3, 6, 8] + list(range(11, 60, 3))
    DVE_U = [u for u in range(UN) if u not in POOL_U]
    PIECES = 4
    PIECE_U = [10, 22, 34, 46]
    PW = NT // PIECES
    SUM_U = 3
    assert UI % PRING == 0 and PRING == TILES

    def add_steps(units):
        steps, done, first = [], {}, {}
        for u in units:
            pair = u % 2
            if pair not in first:
                first[pair] = u
                continue
            fresh = not any(p == pair for p, _, _ in steps)
            steps.append((pair, u, first[pair] if fresh else None))
            done[u] = len(steps)
            if fresh:
                done[first[pair]] = len(steps)
        return steps, done

    def last_add(steps, j):
        return max(i + 1 for i in range(j) if steps[i][0] == steps[j][0])

    (DSTEPS, DDONE), (PSTEPS, PDONE) = add_steps(DVE_U), add_steps(POOL_U)
    ND, NPOOL = len(DSTEPS), len(PSTEPS)
    with ExitStack() as ctx:
        def sb(name, shape, dt):
            return ctx.enter_context(nc.sbuf_tensor(name, shape, dt))

        Kst = sb("Kst", [P, HEADS, N], F16)
        Qst = sb("Qst", [P, GROUPS, HG, NT], F16)
        V = sb("V", [P, MT, C], F32)
        prob = sb("prob", [P, PRING, 2, NT], F32)
        acc = sb("acc", [P, GROUPS, HG, NT], F32)
        accp = sb("accp", [P, GROUPS, HG, NT], F32)
        ones = sb("ones32", [P, HD], F32)
        rsum = sb("rsum", [P, NT], F32)
        wp = sb("wp", [P, CC, C], F32)
        O = X
        S = ctx.enter_context(nc.psum_tensor("S", [P, RING, 2, NT], F32))
        PO = ctx.enter_context(nc.psum_tensor("PO", [P, NT], F32))
        PS = ctx.enter_context(nc.psum_tensor("PS", [P, NT], F32))

        k_in = [sem(f"l0_k_in{g}") for g in range(GROUPS)]
        q_in = [sem(f"l0_q_in{g}") for g in range(GROUPS)]
        w_in = sem("l0_wproj_in")
        x_in = [sem(f"l0_x_again{t}") for t in range(TILES)]
        ones_ready = sem("l0_ones")
        vt_done = sem("l0_v_transposed")
        v_ready = sem("l0_v_ready")
        qk_done = sem("l0_scores")
        exp_done = sem("l0_exp")
        pv_done = sem("l0_pv")
        dve_add = sem("l0_dve_add")
        pool_add = sem("l0_pool_add")
        sums_done = sem("l0_sums")
        po_free = sem("l0_po_free")
        ps_free = sem("l0_ps_free")
        o_ready = sem("l0_o_ready")
        proj_done = sem("l0_proj")
        x_ready = sem("l0_x_ready")
        block = ctx.enter_context(nc.Block())

        @block.sync
        def _(sp):
            def load_q(g, off):
                for r in range(4):
                    sp.dma_start(Qst[r * HD:(r + 1) * HD, g, :, :],
                                 Qhl[r // 2, g * P:(g + 1) * P, ds(off, NT)].rearrange("(h d) n -> d h n", d=HD)).then_inc(q_in[g], 16)

            for g in range(GROUPS):
                for r in range(4):
                    sp.dma_start(Kst[r * HD:(r + 1) * HD, g * HG:(g + 1) * HG, :],
                                 Khl[r % 2, g * P:(g + 1) * P, :].rearrange("(h d) n -> d h n", d=HD)).then_inc(k_in[g], 16)
                load_q(g, 0)
            sp.dma_start(wp[:, :, :], w_proj.rearrange("(c p) n -> p c n", p=P)).then_inc(w_in, 16)
            with sp.Fori(1, TILES) as n:
                for g in range(GROUPS):
                    sp.wait_ge(qk_done, n * UI + ((g + 1) * UN - UI))
                    load_q(g, n * NT)
            sp.wait_ge(qk_done, (TILES - 1) * UI + UN)
            load_q(0, (TILES - 1) * NT)
            sp.wait_ge(pv_done, TILES * UI // 2)
            sp.wait_ge(dve_add, TILES * GROUPS * ND)
            sp.wait_ge(pool_add, TILES * GROUPS * NPOOL)
            for t in range(TILES):
                sp.dma_start(prob[:, t, :, :], x[:, t * NT:(t + 1) * NT].rearrange("(c p) n -> p c n", p=P)).then_inc(x_in[t], 16)

        @block.gpsimd
        def _(pool):
            nc.gpsimd.memset(ones[:, :], 1.0).then_inc(ones_ready, 1)

            def token_tile(n, first):
                for g in range(GROUPS):
                    for j, (pair, u, u0) in enumerate(PSTEPS):
                        dst = accp[:, g, 2 * pair:2 * pair + 2, :]
                        if j == 0 and not first:
                            pool.wait_ge(sums_done, n * GROUPS + (g + 1 - GROUPS))
                        if u0 is None:
                            pool.wait_ge(pool_add, n * (GROUPS * NPOOL) + (g * NPOOL + last_add(PSTEPS, j)))
                        pool.wait_ge(exp_done, n * UI + (g * UN + u + 1))
                        a = dst if u0 is None else prob[:, (g * UN + u0) % PRING, :, :]
                        nc.gpsimd.tensor_tensor(dst, a, prob[:, (g * UN + u) % PRING, :, :], ALU.add).then_inc(pool_add, 1)

            token_tile(0, True)
            with pool.Fori(1, TILES) as n:
                token_tile(n, False)

        @block.scalar
        def _(act):
            def wait_summed(n, k):
                g, u = k // UN, k % UN
                if u in DDONE:
                    act.wait_ge(dve_add, n * (GROUPS * ND) + (g * ND + DDONE[u]))
                else:
                    act.wait_ge(pool_add, n * (GROUPS * NPOOL) + (g * NPOOL + PDONE[u]))

            def token_tile(n, before):
                for k in range(UI):
                    act.wait_ge(qk_done, n * UI + (k + 1))
                    if k >= PRING:
                        act.wait_ge(pv_done, n * (UI // 2) + ((k - PRING) // 2 + 1))
                        wait_summed(n, k - PRING)
                    elif before is not None:
                        act.wait_ge(pv_done, n * (UI // 2) + (k - PRING) // 2 + 1)
                        wait_summed(before, k - PRING + UI)
                    nc.scalar.activation(prob[:, k % PRING, :, :], S[:, k % RING, :, :], ACT.Exp, scale=SPLIT2).then_inc(exp_done, 1)

            token_tile(0, None)
            with act.Fori(1, TILES) as n:
                token_tile(n, n - 1)

        @block.tensor
        def _(pe):
            for r in range(MT // 2):
                if r >= 2 * RING:
                    pe.wait_ge(v_ready, r - 2 * RING + 1)
                s = r % (2 * RING)
                for q in range(4):
                    j, c = 2 * r + q // 2, q % 2
                    last = nc.tensor.transpose(S[:, s // 2, s % 2, q * P:(q + 1) * P], X[:, c, j * P:(j + 1) * P], ident[:, :])
                last.then_inc(vt_done, 1)
            pe.wait_ge(v_ready, MT // 2)
            pe.wait_ge(ones_ready, 1)

            def scores(n, k, first):
                g, m, pair = k // UN, k % UN // 2, k % 2
                if k % UN == 0:
                    pe.wait_ge(q_in[g], (n + 1) * 64)
                    if first:
                        pe.wait_ge(k_in[g], 64)
                if k >= RING:
                    pe.wait_ge(exp_done, n * UI + (k - RING + 1))
                elif not first:
                    prev = max(u for u in range(UI - RING, UI) if u % RING == k)
                    pe.wait_ge(exp_done, n * UI + (prev + 1 - UI))
                for hh in range(2):
                    h = 2 * pair + hh
                    last = nc.tensor.matmul(S[:, k % RING, hh, :], Kst[:, g * HG + h, m * P:(m + 1) * P], Qst[:, g, h, :], start=True, stop=True)
                last.then_inc(qk_done, 1)

            def sums(n, g, first):
                if not first:
                    pe.wait_ge(ps_free, n * (GROUPS * PIECES) + g * PIECES)
                for h in range(HG):
                    if h == 0:
                        pe.wait_ge(pool_add, n * (GROUPS * NPOOL) + (g + 1) * NPOOL)
                    nc.tensor.matmul(PS[h * HD:(h + 1) * HD, :], ones[:, :], accp[:, g, h, :], start=True, stop=False)
                for h in range(HG):
                    if h == 0:
                        pe.wait_ge(dve_add, n * (GROUPS * ND) + (g + 1) * ND)
                    last = nc.tensor.matmul(PS[h * HD:(h + 1) * HD, :], ones[:, :], acc[:, g, h, :], start=False, stop=True)
                last.then_inc(sums_done, 1)

            def token_tile(n, first):
                for k in range(UI):
                    g, m, pair = k // UN, k % UN // 2, k % 2
                    ahead = k + AHEAD
                    if ahead < UI:
                        scores(n, ahead, first)
                    else:
                        scores(n + 1, ahead - UI, False)
                    if pair == 0:
                        continue
                    pe.wait_ge(exp_done, n * UI + (k + 1))
                    if m == 0 and not (first and g == 0):
                        pe.wait_ge(po_free, n * GROUPS + g)
                    for h in range(HG):
                        u = k - 1 + h // 2
                        last = nc.tensor.matmul(PO[h * HD:(h + 1) * HD, :], V[:, m, (g * HG + h) * HD:(g * HG + h + 1) * HD],
                                                prob[:, u % PRING, h % 2, :], start=(m == 0), stop=(m == MT - 1))
                    last.then_inc(pv_done, 1)
                    if k % UN == SUM_U:
                        if g:
                            sums(n, g - 1, first)
                        elif not first:
                            sums(n - 1, GROUPS - 1, False)

            for k in range(AHEAD):
                scores(0, k, True)
            token_tile(0, True)
            with pe.Fori(1, TILES) as n:
                token_tile(n, False)
            sums(TILES - 1, GROUPS - 1, False)
            pe.wait_ge(w_in, 16)
            pe.wait_ge(exp_done, TILES * UI)
            for t in range(TILES):
                pe.wait_ge(o_ready, (t + 1) * GROUPS * PIECES)
                for o in range(CC):
                    r = t * CC + o
                    s = r % (2 * RING)
                    if r >= 2 * RING:
                        pe.wait_ge(x_ready, r - 2 * RING + 1)
                    for c in range(CC):
                        last = nc.tensor.matmul(S[:, s // 2, s % 2, :], wp[:, c, o * P:(o + 1) * P], O[:, c, t * NT:(t + 1) * NT],
                                                start=(c == 0), stop=(c == CC - 1))
                last.then_inc(proj_done, 1)

        @block.vector
        def _(dve):
            for r in range(MT // 2):
                dve.wait_ge(vt_done, r + 1)
                s = r % (2 * RING)
                nc.vector.tensor_copy(V[:, 2 * r:2 * r + 2, :].rearrange("p j c -> p (j c)"), S[:, s // 2, s % 2, :]).then_inc(v_ready, 1)

            def copy_values(n, g):
                dve.wait_ge(pv_done, n * (UI // 2) + (g + 1) * MT)
                nc.vector.tensor_copy(O[:, g, ds(n * NT, NT)], PO[:, :]).then_inc(po_free, 1)

            def normalise_piece(n, g, j):
                dve.wait_ge(po_free, n * GROUPS + (g + 1))
                dve.wait_ge(sums_done, n * GROUPS + (g + 1))
                count = n * (GROUPS * PIECES) + (g * PIECES + j + 1)
                part = slice(j * PW, (j + 1) * PW)
                nc.vector.reciprocal(rsum[:, part], PS[:, part]).then_inc(ps_free, 1)
                dve.wait_ge(ps_free, count)
                out = O[:, g, ds(n * NT + j * PW, PW)]
                nc.vector.tensor_tensor(out, out, rsum[:, part], ALU.mult).then_inc(o_ready, 1)

            def token_tile(n, before):
                for g in range(GROUPS):
                    prev = (n, 0) if g else (before, 1)
                    pieces = list(zip(PIECE_U, range(PIECES))) if prev[0] is not None else []
                    for j, (pair, u, u0) in enumerate(DSTEPS):
                        while pieces and u >= pieces[0][0]:
                            normalise_piece(*prev, pieces.pop(0)[1])
                        dst = acc[:, g, 2 * pair:2 * pair + 2, :]
                        if j == 0 and before is not None:
                            dve.wait_ge(sums_done, n * GROUPS + (g + 1 - GROUPS))
                        if u0 is None:
                            dve.wait_ge(dve_add, n * (GROUPS * ND) + (g * ND + last_add(DSTEPS, j)))
                        dve.wait_ge(exp_done, n * UI + (g * UN + u + 1))
                        a = dst if u0 is None else prob[:, (g * UN + u0) % PRING, :, :]
                        nc.vector.tensor_tensor(dst, a, prob[:, (g * UN + u) % PRING, :, :], ALU.add).then_inc(dve_add, 1)
                    copy_values(n, g)

            token_tile(0, None)
            with dve.Fori(1, TILES) as n:
                token_tile(n, n - 1)
            for j in range(PIECES):
                normalise_piece(TILES - 1, GROUPS - 1, j)
            for t in range(TILES):
                dve.wait_ge(x_in[t], 16)
                dve.wait_ge(proj_done, t + 1)
                for o in range(CC):
                    s = (t * CC + o) % (2 * RING)
                    nc.vector.tensor_tensor(X[:, o, t * NT:(t + 1) * NT], S[:, s // 2, s % 2, :], prob[:, t, o, :], ALU.add).then_inc(x_ready, 1)


def layer1_codebook(nc, sem, X, Xs, Os, codes, codes_t, ident, group_avg, eps_col):
    K = codes.shape[1]
    KB = K // NT
    MT = N // P
    RING = 4
    with ExitStack() as ctx:
        def sb(name, shape, dt):
            return ctx.enter_context(nc.sbuf_tensor(name, shape, dt))

        E2 = sb("E2", [P, CC, K], F32)
        Esq = sb("Esq", [P, CC, K], F32)
        nee = sb("nee", [1, K], F32)
        ones = sb("ones1", [P, P], F32)
        stats = sb("stats1", [P, CC, TILES, 6], F32)
        aggr = sb("aggr1", [P, CC, 2], F32)
        cols = sb("cols1", [P, 8, 2], F32)
        xt = sb("xt1", [P, RING, CC, P], F32)
        xsq = sb("xsq1", [P, RING, CC, P], F32)
        nxx = sb("nxx", [P, RING, 1], F32)
        nd = sb("nd", [P, RING, K], F32)
        best = sb("best", [P, RING, 8], F32)
        idx = sb("idx", [P, RING, 8], U32)
        quant = sb("quant", [P, RING, C], F32)
        zeros = sb("zeros1", [P, 2048], F32)
        D = ctx.enter_context(nc.psum_tensor("D1", [P, 2, KB, NT], F32))
        T = ctx.enter_context(nc.psum_tensor("T1", [P, 2, NT], F32))
        px = ctx.enter_context(nc.psum_tensor("px1", [P, 2, NT], F32))
        ps = px[:, 0, :]

        zeros_set = sem("l1_zeros_set")
        rows_zero = sem("l1_rows_zero")
        e_in = sem("l1_codes_in")
        ones_ready = sem("l1_ones")
        e_step = sem("l1_code_steps")
        ee_done = sem("l1_ee")
        nee_ready = sem("l1_nee")
        xt_ready = sem("l1_xt")
        sq_ready = sem("l1_xsq")
        d_done = sem("l1_products")
        nxx_ready = sem("l1_nxx")
        nd_ready = sem("l1_nd")
        best_ready = sem("l1_best")
        idx_ready = sem("l1_idx")
        q_in = [sem(f"l1_quant_in{b}") for b in range(RING)]
        qt_done = sem("l1_quant_t")
        x_done = sem("l1_x")
        gn_vec, gn_pe, gn_act, gn_wait = group_norm_stats(nc, "gn1", sem, X, stats, aggr, group_avg, ps, cols)
        block = ctx.enter_context(nc.Block())

        @block.sync
        def _(sp):
            sp.dma_start(E2[:, :, :], codes.rearrange("(c p) k -> p c k", p=P)).then_inc(e_in, 16)
            sp.wait_ge(zeros_set, 1)
            per = zeros.shape[1]
            count = 0
            for rows in (Xs, Os):
                flat = rows.rearrange("(p r) c -> p (r c)", p=P)
                for o in range(0, flat.shape[1], per):
                    sp.dma_start(flat[:, o:o + per], zeros[:, :]).then_inc(rows_zero, 16)
                    count += 16
            sp.wait_ge(rows_zero, count)

        @block.gpsimd
        def _(pool):
            nc.gpsimd.memset(ones[:, :], 1.0).then_inc(ones_ready, 1)
            nc.gpsimd.memset(zeros[:, :], 0.0).then_inc(zeros_set, 1)

            def square(i):
                b = i % RING
                pool.wait_ge(xt_ready, i + 1)
                nc.gpsimd.tensor_tensor(xsq[:, b, :, :], xt[:, b, :, :], xt[:, b, :, :], ALU.mult).then_inc(sq_ready, 1)

            square(0)
            square(1)
            for i in range(MT):
                if i + 2 < MT:
                    square(i + 2)
                if i >= RING:
                    pool.wait_ge(qt_done, i - RING + 1)
                pool.wait_ge(idx_ready, i + 1)
                nc.gpsimd.indirect_dma_start(out=quant[:, i % RING, :], out_offset=None, in_=codes_t,
                                             in_offset=bass.IndirectOffsetOnAxis(ap=idx[:, i % RING, 0:1], axis=0)).then_inc(q_in[i % RING], 16)

        @block.scalar
        def _(act):
            gn_act(act, eps_col)
            act.wait_ge(ee_done, KB)
            nc.scalar.activation(nee[0:1, :], D[0:1, 0, :, :].rearrange("p k n -> p (k n)"), ACT.Copy, scale=-1.0).then_inc(nee_ready, 1)
            gn_wait(act)

            def norm(r, b, first):
                i = r * RING + b
                if not first:
                    act.wait_ge(d_done, r * RING + (b - RING + 1))
                for c in range(CC):
                    ins = nc.scalar.activation(xt[:, b, c, :], X[:, c, ds(r * (RING * P) + b * P, P)], ACT.Identity,
                                               scale=cols[:, 0, c:c + 1], bias=cols[:, 1, c:c + 1])
                ins.then_inc(xt_ready, 1)

            def distances(r, b, first):
                act.wait_ge(d_done, r * RING + (b + 1))
                nc.scalar.activation(nxx[:, b, :], px[:, b % 2, 0:1], ACT.Copy, scale=-1.0).then_inc(nxx_ready, 1)
                act.wait_ge(nxx_ready, r * RING + (b + 1))
                if not first:
                    act.wait_ge(idx_ready, r * RING + (b - RING + 1))
                nc.scalar.activation(nd[:, b, :], D[:, b % 2, :, :].rearrange("p k n -> p (k n)"), ACT.Identity,
                                     bias=nxx[:, b, :]).then_inc(nd_ready, 1)

            for b in range(RING):
                norm(0, b, True)
            for b in range(RING):
                distances(0, b, True)
                norm(1, b, False)
            with act.Fori(1, MT // RING - 1) as r:
                for b in range(RING):
                    distances(r, b, False)
                    norm(r + 1, b, False)
            for b in range(RING):
                distances(MT // RING - 1, b, False)

        @block.tensor
        def _(pe):
            gn_pe(pe)
            pe.wait_ge(ones_ready, 1)
            pe.wait_ge(e_step, 1)
            for k in range(KB):
                for c in range(CC):
                    last = nc.tensor.matmul(D[0:1, 0, k, :], ones[:, 0:1], Esq[:, c, k * NT:(k + 1) * NT], start=(c == 0), stop=(c == CC - 1))
                last.then_inc(ee_done, 1)
            pe.wait_ge(nee_ready, 1)
            pe.wait_ge(e_step, 2)

            def products(r, b, early):
                pe.wait_ge(xt_ready, r * RING + (b + 1))
                pe.wait_ge(sq_ready, r * RING + (b + 1))
                if not early:
                    pe.wait_ge(nd_ready, r * RING + (b - 1))
                for c in range(CC):
                    nc.tensor.matmul(px[:, b % 2, 0:1], xsq[:, b, c, :], ones[:, 0:1], start=(c == 0), stop=(c == CC - 1))
                for k in range(KB):
                    part = slice(k * NT, (k + 1) * NT)
                    for c in range(CC):
                        nc.tensor.matmul(D[:, b % 2, k, :], xt[:, b, c, :], E2[:, c, part], start=(c == 0), stop=False)
                    last = nc.tensor.matmul(D[:, b % 2, k, :], ones[0:1, :], nee[0:1, part], start=False, stop=True)
                last.then_inc(d_done, 1)

            def transpose(r, b, early):
                pe.wait_ge(q_in[b], r * 16 + 16)
                if not early:
                    pe.wait_ge(x_done, r * RING + (b - 1))
                for c in range(CC):
                    last = nc.tensor.transpose(T[:, b % 2, c * P:(c + 1) * P], quant[:, b, c * P:(c + 1) * P], ident)
                last.then_inc(qt_done, 1)

            for b in range(RING):
                products(0, b, b < 2)
            for b in range(RING):
                products(1, b, False)
                transpose(0, b, b < 2)
            with pe.Fori(2, MT // RING) as r:
                for b in range(RING):
                    products(r, b, False)
                    transpose(r - 1, b, False)
            for b in range(RING):
                transpose(MT // RING - 1, b, False)

        @block.vector
        def _(dve):
            dve.wait_ge(e_in, 16)
            nc.vector.tensor_tensor(Esq[:, :, :], E2[:, :, :], E2[:, :, :], ALU.mult).then_inc(e_step, 1)
            dve.wait_ge(e_step, 1)
            nc.vector.tensor_scalar(out=E2[:, :, :], in0=E2[:, :, :], scalar1=2.0, scalar2=None, op0=ALU.mult).then_inc(e_step, 1)
            gn_vec(dve)

            def add_codes(i):
                xi = X[:, :, i * P:(i + 1) * P]
                dve.wait_ge(qt_done, i + 1)
                nc.vector.tensor_tensor(xi, T[:, i % 2, 0:C].rearrange("p (c n) -> p c n", c=CC), xi, ALU.add).then_inc(x_done, 1)

            for i in range(MT):
                b = i % RING
                dve.wait_ge(nd_ready, i + 1)
                nc.vector.max(best[:, b, :], nd[:, b, :]).then_inc(best_ready, 1)
                if i >= RING:
                    dve.wait_ge(q_in[b], 16 * (i // RING))
                dve.wait_ge(best_ready, i + 1)
                nc.vector.max_index(idx[:, b, :], best[:, b, :], nd[:, b, :]).then_inc(idx_ready, 1)
                if i >= RING:
                    add_codes(i - RING)
            for i in range(MT - RING, MT):
                add_codes(i)


EXPERTS = 8
SLOTS = N // P + EXPERTS
WIN = 8
PAIRS = N // P


def by_window(ap):
    return ap.rearrange("p (r w c) -> p w r c", r=WIN, c=WIN)


def expert_weights(nc, ctx, sem, tag, w, bias):
    wsb = ctx.enter_context(nc.sbuf_tensor(tag + "w", [P, CC, w.shape[1]], F32))
    bsb = ctx.enter_context(nc.sbuf_tensor(tag + "b", [P, w.shape[1]], F32))
    w_in = sem(tag + "_w_in")

    def load(sp):
        for c in range(CC):
            sp.dma_start(wsb[:, c, :], w[c * P:(c + 1) * P, :]).then_inc(w_in, 16)
        sp.dma_start(bsb[:, :], bias.partition_broadcast(P)).then_inc(w_in, 16)
    return wsb, bsb, w_in, 16 * (CC + 1), load


def layer2_route(nc, sem, X, rw1, rb1, rw2, rb2, consts2, ident, group_avg, eps_col, pos, pmax, expert, Xs, load_weights):
    HID = rw1.shape[1]
    with ExitStack() as ctx:
        def sb(name, shape, dt):
            return ctx.enter_context(nc.sbuf_tensor(name, shape, dt))

        xw = sb("xw", [P, CC, N], F32)
        XT = sb("XT", [P, PAIRS, C], F32)
        w1 = sb("rw1", [P, CC, HID], F32)
        b1 = sb("rb1", [P, 1], F32)
        w2 = sb("rw2", [P, EXPERTS], F32)
        b2 = sb("rb2", [1, EXPERTS], F32)
        cst = sb("cst2", [P, 2, P], F32)
        iota = sb("iota8", [P, PAIRS, EXPERTS], F32)
        tilec = sb("tilec", [P, SLOTS, EXPERTS], F32)
        hid = sb("hid", [P, 2, NT], F32)
        stats = sb("stats2", [P, CC, TILES, 6], F32)
        aggr = sb("aggr2", [P, CC, 2], F32)
        cols = sb("cols2", [P, 8, 2], F32)
        te = [sb(f"te{k}", [P, PAIRS, EXPERTS], F32) for k in range(4)]
        et = [sb(f"et{k}", [P, EXPERTS, PAIRS], F32) for k in range(3)]
        tk = [sb(f"tk{k}", [P, PAIRS], F32) for k in range(4)]
        ex = [sb(f"ex{k}", [P, EXPERTS], F32) for k in range(4)]
        exi = sb("exi", [P, 2, EXPERTS], I32)
        ones = sb("ones2", [P, PAIRS], F32)
        tcmp = sb("tcmp", [P, SLOTS, EXPERTS], F32)
        tsum = sb("tsum", [P, SLOTS], F32)
        psh = ctx.enter_context(nc.psum_tensor("psh", [P, 2, NT], F32))
        psl = ctx.enter_context(nc.psum_tensor("psl", [P, NT], F32))
        psx = ctx.enter_context(nc.psum_tensor("psx", [P, 3, NT], F32))
        psc = ctx.enter_context(nc.psum_tensor("psc2", [P, NT], F32))
        ps = ctx.enter_context(nc.psum_tensor("ps2", [P, NT], F32))

        w_in = sem("l2_w_in")
        xw_ready = sem("l2_xw")
        hid_done = sem("l2_hid")
        relu_done = sem("l2_relu")
        logits_done = sem("l2_logits")
        xt_done = sem("l2_xt")
        xt_ready = sem("l2_xt_ready")
        shift_ready = sem("l2_shift")
        exp_done = sem("l2_exp")
        onehot_ready = sem("l2_onehot")
        count_done = sem("l2_count")
        pos_ready = sem("l2_pos")
        chain_sem = sem("l2_chain")
        scattered = sem("l2_scattered")
        gn_vec, gn_pe, gn_act, gn_wait = group_norm_stats(nc, "gn2", sem, X, stats, aggr, group_avg, ps, cols)
        block = ctx.enter_context(nc.Block())
        LOADS = 7

        @block.sync
        def _(sp):
            loads = [(w1[:, :, :], rw1.rearrange("(c p) m -> p c m", p=P)), (b1[:, :], rb1), (w2[:, :], rw2), (b2[:, :], rb2),
                     (cst[:, :, :], consts2["tri"]), (iota[:, :, :], consts2["iota"]), (tilec[:, :, :], consts2["tile"])]
            assert len(loads) == LOADS
            for dst, src in loads:
                sp.dma_start(dst, src).then_inc(w_in, 16)
            load_weights(sp)

        @block.gpsimd
        def _(pool):
            pool.wait_ge(xt_ready, PAIRS // 2)
            pool.wait_ge(pos_ready, 1)
            for i in range(PAIRS):
                nc.gpsimd.indirect_dma_start(out=Xs, out_offset=bass.IndirectOffsetOnAxis(ap=pos[:, i:i + 1], axis=0),
                                             in_=XT[:, i, :], in_offset=None).then_inc(scattered, 16)
            pool.wait_ge(scattered, 16 * PAIRS)

        @block.scalar
        def _(act):
            gn_act(act, eps_col)
            act.wait_ge(w_in, 16 * LOADS)

            def transposed(r):
                act.wait_ge(xt_done, r + 1)
                nc.scalar.activation(XT[:, 2 * r:2 * r + 2, :].rearrange("p j c -> p (j c)"), psx[:, r % 3, :], ACT.Copy).then_inc(xt_ready, 1)

            for t in range(TILES):
                act.wait_ge(hid_done, t + 1)
                if t >= 2:
                    act.wait_ge(logits_done, t - 1)
                nc.scalar.activation(hid[:, t % 2, :], psh[:, t % 2, :], ACT.Relu, bias=b1[:, 0:1]).then_inc(relu_done, 1)
                transposed(2 * t)
                transposed(2 * t + 1)
            act.wait_ge(shift_ready, 1)
            nc.scalar.activation(te[1][:, :, :], te[0][:, :, :], ACT.Exp).then_inc(exp_done, 1)

        @block.tensor
        def _(pe):
            gn_pe(pe)
            pe.wait_ge(w_in, 16 * LOADS)

            def hidden(t):
                pe.wait_ge(xw_ready, CC * (t + 1))
                if t >= 2:
                    pe.wait_ge(relu_done, t - 1)
                for c in range(CC):
                    last = nc.tensor.matmul(psh[:, t % 2, :], w1[:, c, :], xw[:, c, t * NT:(t + 1) * NT], start=(c == 0), stop=(c == CC - 1))
                last.then_inc(hid_done, 1)

            hidden(0)
            for t in range(TILES):
                if t + 1 < TILES:
                    hidden(t + 1)
                for r in (2 * t, 2 * t + 1):
                    if r >= 3:
                        pe.wait_ge(xt_ready, r - 2)
                    for q in range(4):
                        i, c = 2 * r + q // 2, q % 2
                        last = nc.tensor.transpose(psx[:, r % 3, q * P:(q + 1) * P], xw[:, c, i * P:(i + 1) * P], ident)
                    last.then_inc(xt_done, 1)
                pe.wait_ge(relu_done, t + 1)
                for q in range(NT // P):
                    i = t * (NT // P) + q
                    o = psl[:, i * EXPERTS:(i + 1) * EXPERTS]
                    nc.tensor.matmul(o, hid[:, t % 2, q * P:(q + 1) * P], w2[:, :], start=True, stop=False)
                    last = nc.tensor.matmul(o, cst[0:1, 1, :], b2[0:1, :], start=False, stop=True)
                last.then_inc(logits_done, 1)
            pe.wait_ge(onehot_ready, 1)
            half = PAIRS * EXPERTS
            rhs = te[3][:, :, :].rearrange("p i e -> p (i e)")
            for k in range(2):
                last = nc.tensor.matmul(psc[:, k * half:(k + 1) * half], cst[:, k, :], rhs, start=True, stop=True)
            last.then_inc(count_done, 1)

        @block.vector
        def _(dve):
            gn_vec(dve)
            for t in range(TILES):
                for c in range(CC):
                    nc.vector.tensor_scalar(out=xw[:, c, t * NT:(t + 1) * NT].rearrange("p (w r c) -> p w r c", r=WIN, c=WIN),
                                            in0=by_window(X[:, c, t * NT:(t + 1) * NT]),
                                            scalar1=cols[:, 0, c:c + 1], scalar2=cols[:, 1, c:c + 1],
                                            op0=ALU.mult, op1=ALU.add).then_inc(xw_ready, 1)
            chain = Chain(dve, chain_sem)

            def step(ins):
                chain.done(ins)
                chain.wait()

            def each(ap):
                return ap.unsqueeze(2).to_broadcast([P, PAIRS, EXPERTS])

            V = nc.vector
            dve.wait_ge(logits_done, TILES)
            logits = psl[:, 0:PAIRS * EXPERTS].rearrange("p (i e) -> p i e", e=EXPERTS)
            step(V.tensor_reduce(out=tk[0][:, :], in_=logits, axis=AX_X, op=ALU.max))
            V.tensor_tensor(te[0][:, :, :], logits, each(tk[0][:, :]), ALU.subtract).then_inc(shift_ready, 1)
            dve.wait_ge(exp_done, 1)
            step(V.tensor_reduce(out=tk[1][:, :], in_=te[1][:, :, :], axis=AX_X, op=ALU.add))
            step(V.reciprocal(tk[1][:, :], tk[1][:, :]))
            step(V.tensor_tensor(te[2][:, :, :], te[1][:, :, :], each(tk[1][:, :]), ALU.mult))
            step(V.tensor_reduce(out=pmax[:, :], in_=te[2][:, :, :], axis=AX_X, op=ALU.max))
            dve.wait_ge(w_in, 16 * LOADS)
            step(V.tensor_tensor(te[0][:, :, :], te[2][:, :, :], each(pmax[:, :]), ALU.is_equal))
            step(V.scalar_tensor_tensor(out=te[1][:, :, :].rearrange("p i e -> p (i e)"), in0=te[0][:, :, :].rearrange("p i e -> p (i e)"),
                                        scalar=-float(EXPERTS), in1=iota[:, :, :].rearrange("p i e -> p (i e)"), op0=ALU.mult, op1=ALU.add))
            step(V.tensor_reduce(out=tk[2][:, :], in_=te[1][:, :, :], axis=AX_X, op=ALU.min))
            V.tensor_tensor(te[3][:, :, :], te[1][:, :, :], each(tk[2][:, :]), ALU.is_equal).then_inc(onehot_ready, 1)
            step(V.memset(ones[:, :], 1.0))
            dve.wait_ge(count_done, 1)
            half = PAIRS * EXPERTS
            step(V.tensor_copy(et[0][:, :, :], psc[:, half:2 * half].rearrange("p (i e) -> p e i", e=EXPERTS)))
            for e in range(EXPERTS):
                chain.done(V.tensor_tensor_scan(out=et[1][:, e, :], data0=ones[:, 0:PAIRS], data1=et[0][:, e, :], initial=0.0,
                                                op0=ALU.mult, op1=ALU.add))
            chain.wait()
            step(V.tensor_tensor(et[2][:, :, :], et[1][:, :, :], et[0][:, :, :], ALU.subtract))
            step(V.tensor_scalar(out=exi[:, 0, :], in0=et[1][:, :, PAIRS - 1], scalar1=float(P - 1), scalar2=None, op0=ALU.add))
            step(V.tensor_scalar(out=exi[:, 1, :], in0=exi[:, 0, :], scalar1=P.bit_length() - 1, scalar2=None, op0=ALU.arith_shift_right))
            step(V.tensor_copy(ex[0][:, :], exi[:, 1, :]))
            step(V.tensor_tensor_scan(out=ex[1][:, :], data0=ones[:, 0:EXPERTS], data1=ex[0][:, :], initial=0.0, op0=ALU.mult, op1=ALU.add))
            step(V.tensor_tensor(ex[2][:, :], ex[1][:, :], ex[0][:, :], ALU.subtract))
            step(V.tensor_scalar(out=ex[3][:, :], in0=ex[2][:, :], scalar1=float(P), scalar2=-1.0, op0=ALU.mult, op1=ALU.add))
            step(V.tensor_tensor(et[0][:, :, :], et[2][:, :, :], ex[3][:, :].unsqueeze(2).to_broadcast([P, EXPERTS, PAIRS]), ALU.add))
            step(V.tensor_tensor(te[0][:, :, :], psc[:, 0:half].rearrange("p (i e) -> p i e", e=EXPERTS),
                                 et[0][:, :, :].rearrange("p e i -> p i e"), ALU.add))
            step(V.tensor_tensor(te[1][:, :, :], te[0][:, :, :], te[3][:, :, :], ALU.mult))
            step(V.tensor_reduce(out=tk[3][:, :], in_=te[1][:, :, :], axis=AX_X, op=ALU.add))
            V.tensor_copy(pos[:, :], tk[3][:, :]).then_inc(pos_ready, 1)
            step(V.tensor_tensor(tcmp[:, :, :], tilec[:, :, :], ex[1][:, :].unsqueeze(1).to_broadcast([P, SLOTS, EXPERTS]), ALU.is_ge))
            step(V.tensor_reduce(out=tsum[:, :], in_=tcmp[:, :, :], axis=AX_X, op=ALU.add))
            step(V.tensor_copy(expert[:, :], tsum[:, :]))


def layer2_sorted_linear(nc, sem, tag, src, dst, weights, expert, ident):
    M = dst.shape[1]
    HALVES = [(o, min(NT, M - o)) for o in range(0, M, NT)]
    XB = 4
    BUF = 2
    wsb, bsb, w_in, w_loaded, _ = weights
    with ExitStack() as ctx:
        def sb(name, shape, dt):
            return ctx.enter_context(nc.sbuf_tensor(tag + name, shape, dt))

        xs = sb("xs", [P, XB, C], F32)
        xsT = sb("xsT", [P, BUF, CC, P], F32)
        y = sb("y", [P, XB, M], F32)
        psT = ctx.enter_context(nc.psum_tensor(tag + "psT", [P, BUF, NT], F32))
        psY = ctx.enter_context(nc.psum_tensor(tag + "psY", [P, BUF, 2 * NT], F32))

        x_in = [sem(tag + f"_x_in{b}") for b in range(XB)]
        t_done = sem(tag + "_t")
        t_ready = sem(tag + "_t_ready")
        y_done = sem(tag + "_y")
        y_ready = sem(tag + "_y_ready")
        stored = [sem(tag + f"_stored{b}") for b in range(XB)]
        block = ctx.enter_context(nc.Block())
        ROUNDS = SLOTS // XB

        def rounds(engine, body):
            for b in range(XB):
                body(0, b, b)
            with engine.Fori(1, ROUNDS) as r:
                for b in range(XB):
                    body(r, b, r * XB + b)

        def again(j, n):
            return not isinstance(j, int) or j >= n

        @block.sync
        def _(sp):
            def load(b, row):
                sp.dma_start(xs[:, b, :], src[ds(row, P), :]).then_inc(x_in[b], 16)

            def store(b, j):
                sp.wait_ge(y_ready, j + 1)
                sp.dma_start(dst[ds(j * P, P), :], y[:, b, :]).then_inc(stored[b], 16)

            for b in range(XB):
                load(b, b * P)
            with sp.Fori(0, ROUNDS - 1) as r:
                for b in range(XB):
                    sp.wait_ge(t_done, r * XB + (b + 1))
                    load(b, r * (XB * P) + (XB + b) * P)
                    store(b, r * XB + b)
            for b in range(XB):
                store(b, SLOTS - XB + b)
            for b in range(XB):
                sp.wait_ge(stored[b], 16 * ROUNDS)

        @block.scalar
        def _(act):
            def body(r, b, j):
                act.wait_ge(t_done, j + 1)
                if again(j, BUF):
                    act.wait_ge(y_done, j - (BUF - 1))
                nc.scalar.activation(xsT[:, b % BUF, :, :].rearrange("p c n -> p (c n)"), psT[:, b % BUF, 0:C], ACT.Copy).then_inc(t_ready, 1)
            rounds(act, body)

        @block.tensor
        def _(pe):
            def transpose(r, b, j):
                pe.wait_ge(x_in[b], r * 16 + 16)
                if again(j, BUF):
                    pe.wait_ge(t_ready, j - (BUF - 1))
                for c in range(CC):
                    last = nc.tensor.transpose(psT[:, b % BUF, c * P:(c + 1) * P], xs[:, b, c * P:(c + 1) * P], ident)
                last.then_inc(t_done, 1)

            def multiply(b, j):
                off = nc.tensor.value_load(expert[0:1, ds(j, 1)], min_val=0, max_val=EXPERTS - 1) * M
                pe.wait_ge(t_ready, j + 1)
                if again(j, BUF):
                    pe.wait_ge(y_ready, j - (BUF - 1))
                for o, n in HALVES:
                    for c in range(CC):
                        last = nc.tensor.matmul(psY[:, b % BUF, o:o + n], xsT[:, b % BUF, c, :], wsb[:, c, ds(off + o, n)],
                                                start=(c == 0), stop=(c == CC - 1))
                last.then_inc(y_done, 1)

            transpose(0, 0, 0)
            transpose(0, 1, 1)
            pe.wait_ge(w_in, w_loaded)

            def body(r, b, j):
                multiply(b, j)
                after = b + BUF
                transpose(r + after // XB, after % XB, j + BUF)

            for b in range(XB):
                body(0, b, b)
            with pe.Fori(1, ROUNDS - 1) as r:
                for b in range(XB):
                    body(r, b, r * XB + b)
            for b in range(XB):
                j = SLOTS - XB + b
                if b + BUF < XB:
                    body(ROUNDS - 1, b, j)
                else:
                    multiply(b, j)

        @block.vector
        def _(dve):
            dve.wait_ge(w_in, w_loaded)

            def body(r, b, j):
                off = nc.vector.value_load(expert[0:1, ds(j, 1)], min_val=0, max_val=EXPERTS - 1) * M
                if again(j, XB):
                    dve.wait_ge(stored[b], r * 16)
                dve.wait_ge(y_done, j + 1)
                nc.vector.tensor_tensor(y[:, b, :], psY[:, b % BUF, 0:M], bsb[:, ds(off, M)], ALU.add).then_inc(y_ready, 1)
            rounds(dve, body)


def layer2_windows(nc, sem, pos, QKVs, Os, rope, ident, load_weights):
    SCALE = float(HD) ** -0.5
    HG = 4
    G = HEADS // HG
    WT = WIN * WIN
    VW = HD + 1
    RING = 4
    LAG = 4
    with ExitStack() as ctx:
        def sb(name, shape, dt):
            return ctx.enter_context(nc.sbuf_tensor(name, shape, dt))

        qkv = sb("qkv2", [P, RING, 3 * C], F32)
        tab = sb("tab2", [P, 2, 2 * C], F32)
        t1 = sb("t1", [P, 2, 2 * C], F32)
        t2 = sb("t2", [P, 2, 2 * C], F32)
        rqk = sb("rqk", [P, 2, 2 * C], F32)
        vx = sb("vx", [P, RING, HEADS, VW], F32)
        qT = sb("qT", [P, 2, G, P], F32)
        kT = sb("kT", [P, 2, G, HG, P], F32)
        mx = sb("mx", [P, 2, HEADS], F32)
        sh = sb("sh", [P, 2, HEADS, WT], F32)
        pb = sb("pb", [P, 2, HEADS, P], F32)
        pT = sb("pT", [P, 2, HEADS, P], F32)
        rs = sb("rs", [P, 2, HEADS], F32)
        ob = sb("ob", [P, RING, HEADS, HD], F32)
        psA = ctx.enter_context(nc.psum_tensor("psA", [P, NT], F32))
        psS = ctx.enter_context(nc.psum_tensor("psS", [P, 2, NT], F32))
        psP = ctx.enter_context(nc.psum_tensor("psP", [P, 2, 2, NT], F32))
        psO = ctx.enter_context(nc.psum_tensor("psO", [P, NT], F32))

        tab_in = sem("w2_tab_in")
        zeroed = sem("w2_zeroed")
        g_in = [sem(f"w2_gather{b}") for b in range(RING)]
        t1_done = sem("w2_t1")
        t2_done = sem("w2_t2")
        vx_ready = sem("w2_vx")
        r_ready = sem("w2_r")
        a_done = sem("w2_a")
        a_ready = sem("w2_a_ready")
        s_done = sem("w2_s")
        mx_done = sem("w2_mx")
        sh_ready = sem("w2_sh")
        e_ready = sem("w2_e")
        p_done = sem("w2_p")
        p_ready = [sem("w2_p_ready_act"), sem("w2_p_ready_dve")]
        o_done = sem("w2_o")
        rs_done = sem("w2_rs")
        o_ready = sem("w2_o_ready")
        out_done = [sem(f"w2_out{b}") for b in range(RING)]
        block = ctx.enter_context(nc.Block())
        SLOT0, SLOT1 = 2 * RING, PAIRS

        def slots(engine, body):
            def fixed(s):
                def tile(k):
                    i = s - k
                    return (i, i % RING, i // RING) if 0 <= i < PAIRS else None
                return tile
            for s in range(SLOT0):
                body(fixed(s))
            with engine.Fori(0, (SLOT1 - SLOT0) // RING) as r:
                for b in range(RING):
                    body(lambda k: (r * RING + (SLOT0 + b - k), (b - k) % RING, r + (SLOT0 // RING + (b - k) // RING)))
            for s in range(SLOT1, PAIRS + LAG):
                body(fixed(s))

        def again(i, n):
            return not isinstance(i, int) or i >= n

        @block.sync
        def _(sp):
            sp.dma_start(tab[:, :, :], rope).then_inc(tab_in, 16)
            load_weights(sp)

        @block.gpsimd
        def _(pool):
            nc.gpsimd.memset(pb[:, :, :, :].rearrange("p b h n -> p (b h n)"), 0.0).then_inc(zeroed, 1)
            nc.gpsimd.memset(kT[:, :, :, :, :].rearrange("p b g h n -> p (b g h n)"), 0.0).then_inc(zeroed, 1)
            nc.gpsimd.memset(vx[:, :, :, HD:VW].rearrange("p b h o -> p (b h o)"), 1.0).then_inc(zeroed, 1)
            pool.wait_ge(tab_in, 16)

            LATE = 1

            def gather(i):
                if i >= RING:
                    pool.wait_ge(t1_done, i - RING + 1)
                    pool.wait_ge(vx_ready, i - RING + 1)
                    pool.wait_ge(t2_done, 2 * (i - RING + 1))
                nc.gpsimd.indirect_dma_start(out=qkv[:, i % RING, :], out_offset=None, in_=QKVs,
                                             in_offset=bass.IndirectOffsetOnAxis(ap=pos[:, i:i + 1], axis=0)).then_inc(g_in[i % RING], 16)

            def scatter(i):
                pool.wait_ge(o_ready, i + 1)
                nc.gpsimd.indirect_dma_start(out=Os, out_offset=bass.IndirectOffsetOnAxis(ap=pos[:, i:i + 1], axis=0),
                                             in_=ob[:, i % RING, :, :].rearrange("p h d -> p (h d)"), in_offset=None).then_inc(out_done[i % RING], 16)

            def rotate(i):
                pool.wait_ge(g_in[i % RING], 16 * (i // RING + 1))
                if i >= 2:
                    pool.wait_ge(r_ready, i - 1)
                x = qkv[:, i % RING, 0:2 * C].rearrange("p (n two) -> p n two", two=2)
                s = tab[:, 1, :].rearrange("p (n two) -> p n two", two=2)
                o = t2[:, i % 2, :].rearrange("p (n two) -> p n two", two=2)
                nc.gpsimd.tensor_tensor(o[:, :, 0], x[:, :, 1], s[:, :, 0], ALU.mult).then_inc(t2_done, 1)
                nc.gpsimd.tensor_tensor(o[:, :, 1], x[:, :, 0], s[:, :, 1], ALU.mult).then_inc(t2_done, 1)

            for i in range(RING - 1):
                gather(i)
            rotate(0)
            for i in range(PAIRS + LAG + LATE):
                if i + 1 < PAIRS:
                    rotate(i + 1)
                if RING - 1 <= i + RING - 1 < PAIRS:
                    gather(i + RING - 1)
                if 0 <= i - LAG - LATE < PAIRS:
                    scatter(i - LAG - LATE)
            for b in range(RING):
                pool.wait_ge(out_done[b], 16 * (PAIRS // RING))

        @block.vector
        def _(dve):
            def rope1(i, b, r):
                dve.wait_ge(g_in[b], r * 16 + 16)
                nc.vector.tensor_tensor(t1[:, b % 2, :], qkv[:, b, 0:2 * C], tab[:, 0, :], ALU.mult).then_inc(t1_done, 1)

            def rope2(i, b, r):
                dve.wait_ge(t1_done, i + 1)
                if again(i, 2):
                    dve.wait_ge(a_done, i - 1)
                dve.wait_ge(t2_done, i * 2 + 2)
                nc.vector.tensor_tensor(rqk[:, b % 2, :], t1[:, b % 2, :], t2[:, b % 2, :], ALU.add).then_inc(r_ready, 1)

            def shift(i, b, r):
                S = psS[:, b % 2, :].rearrange("p (h m) -> p h m", m=WT)
                dve.wait_ge(s_done, i + 1)
                nc.vector.tensor_reduce(out=mx[:, b % 2, :], in_=S, axis=AX_X, op=ALU.max).then_inc(mx_done, 1)
                if again(i, 2):
                    dve.wait_ge(e_ready, i - 1)
                dve.wait_ge(mx_done, i + 1)
                nc.vector.tensor_tensor(sh[:, b % 2, :, :], S, mx[:, b % 2, :].unsqueeze(2).to_broadcast([P, HEADS, WT]), ALU.subtract).then_inc(sh_ready, 1)

            def evacuate(i, b, r):
                if again(i, 2):
                    dve.wait_ge(o_done, i - 1)
                dve.wait_ge(p_done, i + 1)
                nc.vector.tensor_copy(pT[:, b % 2, HG:, :].rearrange("p h n -> p (h n)"), psP[:, b % 2, 1, :]).then_inc(p_ready[1], 1)

            def normalise(i, b, r):
                O = psO[:, 0:HEADS * VW].rearrange("p (h d) -> p h d", d=VW)
                dve.wait_ge(o_done, i + 1)
                nc.vector.reciprocal(rs[:, b % 2, :], O[:, :, HD]).then_inc(rs_done, 1)
                if again(i, RING):
                    dve.wait_ge(out_done[b], r * 16)
                dve.wait_ge(rs_done, i + 1)
                nc.vector.tensor_tensor(ob[:, b, :, :], O[:, :, 0:HD], rs[:, b % 2, :].unsqueeze(2).to_broadcast([P, HEADS, HD]), ALU.mult).then_inc(o_ready, 1)

            dve.wait_ge(tab_in, 16)

            def body(tile):
                for k, stages in ((0, (rope1, rope2)), (4, (normalise,)), (3, (evacuate,)), (2, (shift,))):
                    at = tile(k)
                    if at is not None:
                        for stage in stages:
                            stage(*at)
            slots(dve, body)

        @block.scalar
        def _(act):
            def spread(i, b, r):
                act.wait_ge(a_done, i + 1)
                if again(i, 2):
                    act.wait_ge(s_done, i - 1)
                A = psA[:, :].rearrange("p (s n) -> p s n", n=P)
                nc.scalar.activation(qT[:, b % 2, :, :], A[:, 0:G, :], ACT.Copy)
                for h in range(HG):
                    on = slice(h * HD, (h + 1) * HD)
                    last = nc.scalar.activation(kT[on, b % 2, :, h, :], A[on, G:2 * G, :], ACT.Copy)
                last.then_inc(a_ready, 1)

            def place_v(i, b, r):
                act.wait_ge(g_in[b], r * 16 + 16)
                if again(i, RING):
                    act.wait_ge(o_done, i - (RING - 1))
                nc.scalar.activation(vx[:, b, :, 0:HD], qkv[:, b, 2 * C:3 * C].rearrange("p (h d) -> p h d", d=HD), ACT.Copy).then_inc(vx_ready, 1)

            def exponent(i, b, r):
                act.wait_ge(sh_ready, i + 1)
                if again(i, 2):
                    act.wait_ge(p_done, i - 1)
                for w in range(2):
                    on = slice(w * WT, (w + 1) * WT)
                    last = nc.scalar.activation(pb[on, b % 2, :, w * WT:(w + 1) * WT], sh[on, b % 2, :, :], ACT.Exp, scale=SCALE)
                last.then_inc(e_ready, 1)

            def evacuate(i, b, r):
                if again(i, 2):
                    act.wait_ge(o_done, i - 1)
                act.wait_ge(p_done, i + 1)
                nc.scalar.activation(pT[:, b % 2, 0:HG, :].rearrange("p h n -> p (h n)"), psP[:, b % 2, 0, :], ACT.Copy).then_inc(p_ready[0], 1)

            act.wait_ge(zeroed, 3)

            def body(tile):
                for k, stage in ((3, evacuate), (0, place_v), (2, exponent), (0, spread)):
                    if tile(k) is not None:
                        stage(*tile(k))
            slots(act, body)

        @block.tensor
        def _(pe):
            def transpose_qk(i, b, r):
                pe.wait_ge(r_ready, i + 1)
                if again(i, 1):
                    pe.wait_ge(a_ready, i)
                for q in range(2 * G):
                    last = nc.tensor.transpose(psA[:, q * P:(q + 1) * P], rqk[:, b % 2, q * P:(q + 1) * P], ident)
                last.then_inc(a_done, 1)

            def scores(i, b, r):
                pe.wait_ge(a_ready, i + 1)
                if again(i, 2):
                    pe.wait_ge(sh_ready, i - 1)
                for g in range(G):
                    for w in range(2):
                        on = slice(w * WT, (w + 1) * WT)
                        last = nc.tensor.matmul(psS[on, b % 2, g * HG * WT:(g + 1) * HG * WT], qT[:, b % 2, g, on], kT[:, b % 2, g, :, on],
                                                start=True, stop=True)
                last.then_inc(s_done, 1)

            def transpose_p(i, b, r):
                pe.wait_ge(e_ready, i + 1)
                if again(i, 2):
                    pe.wait_ge(p_ready[0], i - 1)
                    pe.wait_ge(p_ready[1], i - 1)
                for h in range(HEADS):
                    last = nc.tensor.transpose(psP[:, b % 2, h // HG, h % HG * P:(h % HG + 1) * P], pb[:, b % 2, h, :], ident)
                last.then_inc(p_done, 1)

            def values(i, b, r):
                pe.wait_ge(p_ready[0], i + 1)
                pe.wait_ge(p_ready[1], i + 1)
                pe.wait_ge(vx_ready, i + 1)
                if again(i, 1):
                    pe.wait_ge(o_ready, i)
                for h in range(HEADS):
                    last = nc.tensor.matmul(psO[:, h * VW:(h + 1) * VW], pT[:, b % 2, h, :], vx[:, b, h, :], start=True, stop=True)
                last.then_inc(o_done, 1)

            pe.wait_ge(zeroed, 3)

            def body(tile):
                for k, stage in ((4, values), (3, transpose_p), (2, scores), (0, transpose_qk)):
                    if tile(k) is not None:
                        stage(*tile(k))
            slots(pe, body)


def layer2_combine(nc, sem, X, pos, pmax, Ps, ident):
    RING = 4
    with ExitStack() as ctx:
        g = ctx.enter_context(nc.sbuf_tensor("g2", [P, RING, C], F32))
        gs = ctx.enter_context(nc.sbuf_tensor("gs2", [P, RING, C], F32))
        ps = ctx.enter_context(nc.psum_tensor("psg", [P, RING, NT], F32))
        g_in = [sem(f"c2_in{b}") for b in range(RING)]
        s_ready = sem("c2_scaled")
        t_done = sem("c2_t")
        x_done = sem("c2_x")
        block = ctx.enter_context(nc.Block())

        @block.gpsimd
        def _(pool):
            for i in range(PAIRS):
                if i >= RING:
                    pool.wait_ge(s_ready, i - RING + 1)
                nc.gpsimd.indirect_dma_start(out=g[:, i % RING, :], out_offset=None, in_=Ps,
                                             in_offset=bass.IndirectOffsetOnAxis(ap=pos[:, i:i + 1], axis=0)).then_inc(g_in[i % RING], 16)

        @block.scalar
        def _(act):
            for i in range(PAIRS):
                act.wait_ge(g_in[i % RING], 16 * (i // RING + 1))
                if i >= RING:
                    act.wait_ge(t_done, i - RING + 1)
                nc.scalar.activation(gs[:, i % RING, :], g[:, i % RING, :], ACT.Copy, scale=pmax[:, i:i + 1]).then_inc(s_ready, 1)

        @block.tensor
        def _(pe):
            for i in range(PAIRS):
                pe.wait_ge(s_ready, i + 1)
                if i >= RING:
                    pe.wait_ge(x_done, CC * (i - RING + 1))
                for c in range(CC):
                    last = nc.tensor.transpose(ps[:, i % RING, c * P:(c + 1) * P], gs[:, i % RING, c * P:(c + 1) * P], ident)
                last.then_inc(t_done, 1)

        @block.vector
        def _(dve):
            per = NT // P
            for i in range(PAIRS):
                dve.wait_ge(t_done, i + 1)
                for c in range(CC):
                    x = by_window(X[:, c, i // per * NT:(i // per + 1) * NT])[:, 2 * (i % per):2 * (i % per) + 2, :, :]
                    nc.vector.tensor_tensor(x, ps[:, i % RING, c * P:(c + 1) * P].rearrange("p (w r c) -> p w r c", r=WIN, c=WIN), x,
                                            ALU.add).then_inc(x_done, 1)


def layer3_chain(nc, sem, X, w1, b1, w2, b2, w3row, w3col, b3, ident, group_avg, eps_col, out):
    EX = w1.shape[1]
    ROUNDS = C // EX
    PW = W + 2
    HALF = TILES // 2
    with ExitStack() as ctx:
        def sb(name, shape, dt):
            return ctx.enter_context(nc.sbuf_tensor(name, shape, dt))

        xn = sb("xn3", [P, CC, N], F32)
        A = sb("A3", [P, CC, N], F32)
        B0 = sb("B0", [P, PW, PW], F32)
        B1 = sb("B1", [P, PW, PW], F32)
        B2 = sb("B2", [P, PW, PW], F32)
        S2 = sb("S2", [P, HALF, NT], F32)
        U = sb("U3", [P, HALF, NT], F32)
        w1s = sb("w1s", [P, CC, EX], F32)
        w2s = sb("w2s", [P, CC, 9, EX], F32)
        b12 = sb("b12", [P, 2], F32)
        w3r = sb("w3r", [P, C], F32)
        w3c = sb("w3c", [P, CC], F32)
        b3c = sb("b3c", [P, 1], F32)
        grow = sb("grow", [P, C], F32)
        step = sb("step3", [P, CC + 1, C], F32)
        MT3 = sb("MT3", [P, CC + 1, C], F32)
        ccol = sb("ccol", [P, CC], F32)
        one = sb("one3", [1, 1], F32)
        stats = sb("stats3", [P, CC, TILES, 6], F32)
        aggr = sb("aggr3", [P, CC, 2], F32)
        cols = sb("cols3", [P, 8, 2], F32)
        banks = [ctx.enter_context(nc.psum_tensor(f"bank3_{i}", [P, NT], F32)) for i in range(7)]
        ps = ctx.enter_context(nc.psum_tensor("ps3", [P, NT], F32))

        w_in = sem("l3_w_in")
        pads_zero = sem("l3_pads")
        xn_ready = sem("l3_xn")
        a0_ready = sem("l3_a0")
        y_ready = sem("l3_y")
        pair_done = sem("l3_pairs")
        a_ready = sem("l3_a")
        relu_done = sem("l3_relu")
        z_ready = sem("l3_z")
        u_ready = sem("l3_u")
        z_copied = sem("l3_z_copied")
        mat_step = sem("l3_mat")
        col_done = sem("l3_col")
        ccol_ready = sem("l3_ccol")
        last_relu = sem("l3_last_relu")
        m_done = sem("l3_m")
        o_ready = sem("l3_out_ready")
        x_out = sem("l3_x_out")
        gn_vec, gn_pe, gn_act, gn_wait = group_norm_stats(nc, "gn3", sem, X, stats, aggr, group_avg, ps, cols)
        block = ctx.enter_context(nc.Block())
        LOADS = 10
        MAT_STEPS = 11
        STAGES = [(B2, 1), (B0, 0), (B1, 0), (B0, 0), (B2, 1)]

        def lanes(h):
            return slice(h * EX, (h + 1) * EX)

        def rows(B, half, t):
            return B[lanes(half), 1 + t * TR:1 + (t + 1) * TR, 1:1 + W]

        def as_rows(ap):
            return ap.rearrange("p (h w) -> p h w", w=W)

        def pairs(stage, j):
            return (ROUNDS + stage) * HALF + j + 1

        @block.sync
        def _(sp):
            loads = [(w1s[:, :, :], w1.rearrange("(c p) m -> p c m", p=P))]
            loads += [(w2s[:, c, :, :], w2[:, c * P:(c + 1) * P, :].rearrange("t p m -> p t m")) for c in range(CC)]
            for h in range(2):
                loads += [(b12[lanes(h), 0:1], b1), (b12[lanes(h), 1:2], b2)]
            loads += [(w3r[:, :], w3row), (w3c[:, :], w3col), (b3c[:, :], b3)]
            assert len(loads) == LOADS
            for dst, src in loads:
                sp.dma_start(dst, src).then_inc(w_in, 16)
            for t in range(TILES):
                sp.wait_ge(o_ready, (t + 1) * CC)
                for c in range(CC):
                    sp.dma_start(out[c * P:(c + 1) * P, t * NT:(t + 1) * NT], X[:, c, t * NT:(t + 1) * NT]).then_inc(x_out, 16)
            sp.wait_ge(x_out, 16 * CC * TILES)

        @block.gpsimd
        def _(pool):
            for B in (B0, B1, B2):
                nc.gpsimd.memset(B[:, :, :].rearrange("p h w -> p (h w)"), 0.0).then_inc(pads_zero, 1)
            nc.gpsimd.memset(one[:, :], 1.0).then_inc(pads_zero, 1)
            for c in range(CC):
                for h in range(2):
                    part = slice(h * (N // 2), (h + 1) * (N // 2))
                    pool.wait_ge(xn_ready, CC * c + h + 1)
                    if c == 0 and h == 0:
                        pool.wait_ge(a0_ready, CC)
                    nc.gpsimd.tensor_tensor(X[:, c, part], X[:, c, part], xn[:, c, part], ALU.add).then_inc(y_ready, 1)
            for t in range(TILES):
                pool.wait_ge(z_ready, TILES + t + 1)
                pool.wait_ge(pair_done, pairs(1, min((t + 1) // 2, HALF - 1)))
                nc.gpsimd.tensor_copy(rows(B0, 0, t), rows(B1, 0, t)).then_inc(z_copied, 1)

        @block.scalar
        def _(act):
            gn_act(act, eps_col)
            gn_wait(act)
            act.wait_ge(w_in, 16 * LOADS)
            for c in range(CC):
                for h in range(2):
                    part = slice(h * (N // 2), (h + 1) * (N // 2))
                    nc.scalar.activation(xn[:, c, part], X[:, c, part], ACT.Identity, scale=cols[:, 0, c:c + 1],
                                         bias=cols[:, 1, c:c + 1]).then_inc(xn_ready, 1)
            for i in range(ROUNDS):
                for j in range(HALF):
                    act.wait_ge(pair_done, i * HALF + j + 1)
                    for h in range(2):
                        t = 2 * j + h
                        nc.scalar.activation(A[lanes(i % 2), i // 2, t * NT:(t + 1) * NT], banks[j][lanes(h), :], ACT.Identity,
                                             bias=b12[lanes(h), 0:1]).then_inc(a_ready, 1)
            for t in range(TILES):
                part = slice(t * NT, (t + 1) * NT)
                act.wait_ge(z_ready, 3 * TILES + t + 1)
                act.wait_ge(z_copied, t + 1)
                nc.scalar.activation(as_rows(A[:, 0, part]), B0[:, 1 + t * TR:1 + (t + 1) * TR, 1:1 + W], ACT.Relu).then_inc(last_relu, 1)
                nc.scalar.activation(as_rows(A[lanes(0), 1, part]), rows(B2, 0, t), ACT.Relu).then_inc(last_relu, 1)
            for t in range(TILES):
                part = slice(t * NT, (t + 1) * NT)
                act.wait_ge(z_ready, 4 * TILES + t + 1)
                nc.scalar.activation(A[lanes(1), 1, part], A[lanes(1), 1, part], ACT.Relu).then_inc(last_relu, 1)

        @block.tensor
        def _(pe):
            gn_pe(pe)
            pe.wait_ge(w_in, 16 * LOADS)
            pe.wait_ge(a0_ready, CC)
            for i in range(ROUNDS):
                for j in range(HALF):
                    if i:
                        pe.wait_ge(a_ready, (i - 1) * TILES + 2 * j + 2)
                    for c in range(CC):
                        for h in range(2):
                            t = 2 * j + h
                            last = nc.tensor.matmul(banks[j][lanes(h), :], w1s[:, c, :], A[:, c, t * NT:(t + 1) * NT],
                                                    start=(c == 0), stop=(c == CC - 1))
                    last.then_inc(pair_done, 1)
            pe.wait_ge(mat_step, MAT_STEPS)
            pe.wait_ge(pads_zero, 4)
            for c in range(CC):
                last = nc.tensor.matmul(ps[:, c:c + 1], MT3[0:1, CC, c * P:(c + 1) * P], one[0:1, 0:1], start=True, stop=True)
            last.then_inc(col_done, 1)
            pe.wait_ge(a_ready, ROUNDS * TILES)
            for s, (B, c) in enumerate(STAGES):
                for j in range(HALF):
                    reads = min(2 * j + 3, TILES)
                    if s < 2:
                        pe.wait_ge(relu_done, 3 * reads)
                    if s > 0:
                        pe.wait_ge(z_ready, (s - 1) * TILES + (reads if s > 1 else 2 * j + 2))
                    if s == 3:
                        pe.wait_ge(z_copied, reads)
                    for tap in range(9):
                        dy, dx = divmod(tap, 3)
                        for h in range(2):
                            t = 2 * j + h
                            last = nc.tensor.matmul(banks[j][lanes(h), :], w2s[:, c, tap, :],
                                                    B[:, t * TR + dy:t * TR + dy + TR, dx:dx + W],
                                                    start=(tap == 0), stop=(tap == 8))
                    last.then_inc(pair_done, 1)
            for t in range(TILES):
                pe.wait_ge(last_relu, 2 * TILES + t + 1)
                for o in range(CC):
                    r = t * CC + o
                    if r >= 3:
                        pe.wait_ge(o_ready, r - 2)
                    for c in range(CC):
                        last = nc.tensor.matmul(banks[4 + r % 3][:, :], MT3[:, c, o * P:(o + 1) * P], A[:, c, t * NT:(t + 1) * NT],
                                                start=(c == 0), stop=(c == CC - 1))
                    last.then_inc(m_done, 1)

        @block.vector
        def _(dve):
            gn_vec(dve)
            for c in range(CC):
                nc.vector.tensor_scalar(out=A[:, c, :], in0=X[:, c, :], scalar1=cols[:, 0, c:c + 1], scalar2=cols[:, 1, c:c + 1],
                                        op0=ALU.mult, op1=ALU.add).then_inc(a0_ready, 1)
            dve.wait_ge(w_in, 16 * LOADS)
            chain = Chain(dve, mat_step)
            chain.done(nc.vector.tensor_scalar(out=grow[:, :], in0=w3r[:, :], scalar1=1.0, scalar2=None, op0=ALU.add))
            chain.done(nc.vector.memset(step[:, :, :], 0.0))
            chain.wait()
            for c in range(CC):
                part = slice(c * P, (c + 1) * P)
                chain.done(nc.vector.scalar_tensor_tensor(out=step[:, c, part], in0=ident, scalar=-1.0, in1=w3r[:, part],
                                                          op0=ALU.mult, op1=ALU.mult))
            chain.done(nc.vector.tensor_scalar(out=step[:, CC, :], in0=w3r[:, :], scalar1=b3c[:, 0:1], scalar2=None, op0=ALU.mult))
            chain.done(nc.vector.tensor_copy(MT3[:, 0:CC, 0], w3c[:, :]))
            chain.done(nc.vector.memset(MT3[:, CC, 0:1], 0.0))
            chain.wait()
            for c in range(CC + 1):
                chain.done(nc.vector.tensor_tensor_scan(out=MT3[:, c, 1:C], data0=grow[:, 0:C - 1], data1=step[:, c, 0:C - 1],
                                                        initial=w3c[:, c:c + 1] if c < CC else 0.0, op0=ALU.mult, op1=ALU.add))
            chain.wait()
            chain.done(nc.vector.tensor_scalar(out=MT3[:, CC, :], in0=MT3[:, CC, :], scalar1=b3c[:, 0:1], scalar2=None, op0=ALU.add))
            assert chain.n == MAT_STEPS
            dve.wait_ge(pads_zero, 3)
            for t in range(TILES):
                part = slice(t * NT, (t + 1) * NT)
                dve.wait_ge(a_ready, (ROUNDS - 1) * TILES + t + 1)
                for dst, src in ((B0[:, 1 + t * TR:1 + (t + 1) * TR, 1:1 + W], A[:, 0, part]),
                                 (B2[:, 1 + t * TR:1 + (t + 1) * TR, 1:1 + W], A[:, 1, part]),
                                 (rows(B1, 1, t), A[lanes(1), 0, part])):
                    nc.vector.tensor_scalar(out=dst, in0=as_rows(src), scalar1=0.0, scalar2=None, op0=ALU.max).then_inc(relu_done, 1)
            dve.wait_ge(col_done, 1)
            nc.vector.tensor_copy(ccol[:, :], ps[:, 0:CC]).then_inc(ccol_ready, 1)

            def biased(dst, t, share):
                j, h = divmod(t, 2)
                nc.vector.scalar_tensor_tensor(out=dst, in0=as_rows(banks[j][lanes(h), :]), scalar=b12[lanes(h), 1:2],
                                               in1=as_rows(share[lanes(h), j, :]), op0=ALU.add, op1=ALU.add).then_inc(z_ready, 1)

            for s in range(len(STAGES)):
                for t in range(TILES):
                    j, h = divmod(t, 2)
                    dve.wait_ge(pair_done, pairs(s, j))
                    if s == 0:
                        nc.vector.tensor_copy(S2[lanes(h), j, :], banks[j][lanes(h), :]).then_inc(z_ready, 1)
                    elif s == 1:
                        dve.wait_ge(z_ready, t + 1)
                        biased(rows(B1, 0, t), t, S2)
                    elif s == 2:
                        biased(rows(B0, 1, t), t, S2)
                    elif s == 3:
                        nc.vector.tensor_copy(U[lanes(h), j, :], banks[j][lanes(h), :]).then_inc(u_ready, 1)
                        biased(rows(B2, 0, t), t, S2)
                    else:
                        dve.wait_ge(u_ready, t + 1)
                        biased(as_rows(A[lanes(1), 1, t * NT:(t + 1) * NT]), t, U)
            dve.wait_ge(y_ready, 2 * CC)
            dve.wait_ge(ccol_ready, 1)
            for t in range(TILES):
                for o in range(CC):
                    r = t * CC + o
                    xt = X[:, o, t * NT:(t + 1) * NT]
                    dve.wait_ge(m_done, r + 1)
                    nc.vector.scalar_tensor_tensor(out=xt, in0=banks[4 + r % 3][:, :], scalar=ccol[:, o:o + 1], in1=xt,
                                                   op0=ALU.add, op1=ALU.add).then_inc(o_ready, 1)


def build(nc, a, out):
    with ExitStack() as ctx:
        def sem(name):
            return nc.alloc_semaphore(name=name)

        X = ctx.enter_context(nc.sbuf_tensor("X", [P, CC, N], F32))
        consts = ctx.enter_context(nc.sbuf_tensor("consts", [P, 3, P], F32))
        pos = ctx.enter_context(nc.sbuf_tensor("pos", [P, PAIRS], U32))
        pmax = ctx.enter_context(nc.sbuf_tensor("pmax", [P, PAIRS], F32))
        expert = ctx.enter_context(nc.sbuf_tensor("expert", [P, SLOTS], U32))
        eps = ctx.enter_context(nc.sbuf_tensor("eps", [P, 1], F32))
        Qhl = nc.dram_tensor("q_parts", [2, C, N], F16).ap()
        Xs = nc.dram_tensor("tokens_by_expert", [SLOTS * P, C], F32).ap()
        QKVs = nc.dram_tensor("qkv_by_expert", [SLOTS * P, 3 * C], F32).ap()
        Os = nc.dram_tensor("attended_by_expert", [SLOTS * P, C], F32).ap()
        Ps = nc.dram_tensor("projected_by_expert", [SLOTS * P, C], F32).ap()
        Khl = nc.dram_tensor("k_parts", [2, C, N], F16).ap()
        consts_in = sem("consts_in")
        eps_set = sem("eps_set")
        with nc.Block() as block:
            @block.sync
            def _(sp):
                sp.dma_start(consts[:, :, :], a["consts"]).then_inc(consts_in, 16)
                sp.wait_ge(consts_in, 16)

            @block.vector
            def _(dve):
                nc.vector.memset(eps[:, :], GN_EPS).then_inc(eps_set, 1)
                dve.wait_ge(eps_set, 1)
        ident, ones_head, group_avg = consts[:, 0, :], consts[:, 1, :], consts[:, 2, :]
        with nc.cleanup_on_exit():
            layer0_conv(nc, sem, X, a["x"], (a["L0_conv_W1"], a["L0_conv_W3"], a["L0_conv_W5"]), a["L0_conv_Wdw"],
                        a["temp"], ones_head, group_avg, eps[:, 0:1], Qhl, Khl, consts_in)
        with nc.cleanup_on_exit():
            layer0_attention(nc, sem, X, a["x"], Qhl, Khl, a["L0_conv_Wproj"], ident)
        with nc.cleanup_on_exit():
            layer1_codebook(nc, sem, X, Xs, Os, a["codes"], a["codes_t"], ident, group_avg, eps[:, 0:1])
        with nc.cleanup_on_exit(), ExitStack() as stage:
            weights = expert_weights(nc, stage, sem, "qkv", a["qkv_w"], a["qkv_b"])
            layer2_route(nc, sem, X, a["rw1"], a["rb1"], a["rw2"], a["rb2"], a, ident, group_avg, eps[:, 0:1], pos, pmax, expert, Xs, weights[-1])
            layer2_sorted_linear(nc, sem, "qkv", Xs, QKVs, weights, expert, ident)
        with nc.cleanup_on_exit(), ExitStack() as stage:
            weights = expert_weights(nc, stage, sem, "proj", a["proj_w"], a["proj_b"])
            layer2_windows(nc, sem, pos, QKVs, Os, a["rope"], ident, weights[-1])
            layer2_sorted_linear(nc, sem, "proj", Os, Ps, weights, expert, ident)
        with nc.cleanup_on_exit():
            layer2_combine(nc, sem, X, pos, pmax, Ps, ident)
            layer3_chain(nc, sem, X, a["w1"], a["b1"], a["w2"], a["b2"], a["w3row"], a["w3col"], a["b3"], ident, group_avg, eps[:, 0:1], out)


def kernel(**inputs):
    import numpy as np
    import concourse.bacc as bacc
    from concourse.bass_utils import run_bass_kernel_spmd

    a = {name: np.asarray(value) for name, value in inputs.items()}
    arrays = {
        "x": a["x"].reshape(N, C).T,
        "L0_conv_W1": a["L0_conv_W1"].reshape(C, C, 1).transpose(1, 2, 0),
        "L0_conv_W3": a["L0_conv_W3"].reshape(C, C, 9).transpose(1, 2, 0),
        "L0_conv_W5": a["L0_conv_W5"].reshape(C, C, 25).transpose(1, 2, 0),
        "L0_conv_Wdw": a["L0_conv_Wdw"].reshape(3 * C, 9),
        "L0_conv_Wproj": a["L0_conv_Wproj"].reshape(C, C).T,
        "temp": np.repeat(a["L0_conv_temperature"].reshape(HEADS), HD).reshape(CC, P).T,
        "rw1": a["L2_conv_router_w1"].T,
        "rb1": a["L2_conv_router_b1"].reshape(-1, 1),
        "rw2": a["L2_conv_router_w2"].T,
        "rb2": a["L2_conv_router_b2"].reshape(1, -1),
        "qkv_w": a["L2_conv_qkv_w"].reshape(EXPERTS * 3 * C, C).T,
        "qkv_b": a["L2_conv_qkv_b"].reshape(-1),
        "proj_w": a["L2_conv_proj_w"].reshape(EXPERTS * C, C).T,
        "proj_b": a["L2_conv_proj_b"].reshape(-1),
        "w1": a["L3_conv_w1"].reshape(C, -1),
        "b1": a["L3_conv_b1"].reshape(-1, 1),
        "w2": a["L3_conv_w2"].reshape(9, C, -1),
        "b2": a["L3_conv_b2"].reshape(-1, 1),
        "w3row": np.broadcast_to(a["L3_conv_w3"].reshape(1, C), (P, C)),
        "w3col": a["L3_conv_w3"].reshape(CC, P).T,
        "b3": np.broadcast_to(a["L3_conv_b3"].reshape(1, 1), (P, 1)),
        "codes": a["L1_conv_embeddings"],
        "codes_t": a["L1_conv_embeddings"].T,
    }
    p = np.arange(P)
    same = lambda w: (p[:, None] // w == p[None, :] // w)
    arrays["consts"] = np.stack([np.eye(P), same(HD), same(C // 32) / (C // 32)], axis=1).astype(np.float32)
    arrays["tri"] = np.stack([p[:, None] <= p[None, :], np.ones((P, P))], axis=1).astype(np.float32)
    arrays["iota"] = np.broadcast_to(np.arange(EXPERTS, dtype=np.float32) + EXPERTS, (P, PAIRS, EXPERTS))
    tile = np.where(np.arange(EXPERTS) < EXPERTS - 1, np.arange(SLOTS)[:, None], -1)
    arrays["tile"] = np.broadcast_to(tile.astype(np.float32), (P, SLOTS, EXPERTS))
    half = HD // 2
    inv = (1.0 / 10000.0 ** (np.arange(0, half, 2, dtype=np.float32) / np.float32(half))).astype(np.float32)
    row, col = p // WIN % WIN, p % WIN
    ang = np.concatenate([row[:, None].astype(np.float32) * inv, col[:, None].astype(np.float32) * inv], axis=1)
    cos = np.repeat(np.cos(ang), 2, axis=1)
    sin = np.repeat(np.sin(ang), 2, axis=1) * np.where(np.arange(HD) % 2, 1, -1)
    arrays["rope"] = np.stack([np.tile(cos, 2 * HEADS), np.tile(sin, 2 * HEADS)], axis=1).astype(np.float32)
    arrays = {name: np.ascontiguousarray(value) for name, value in arrays.items()}
    nc = bacc.Bacc("TRN2", target_bir_lowering=False, num_devices=1)
    args = {name: nc.dram_tensor(name + "_dram", v.shape, mybir.dt.from_np(v.dtype), kind="ExternalInput").ap()
            for name, v in arrays.items()}
    out = nc.dram_tensor("out_dram", (C, N), F32, kind="ExternalOutput").ap()
    build(nc, args, out)
    r = run_bass_kernel_spmd(nc, [{name + "_dram": v for name, v in arrays.items()}], core_ids=[0])
    return r.results[0]["out_dram"].T.reshape(1, H, W, C)
```

```python
from contextlib import ExitStack

import concourse.bass as bass
from concourse import mybir
from concourse.alu_op_type import AluOpType as ALU

ACT = mybir.ActivationFunctionType
AX_X = mybir.AxisListType.X
F32 = mybir.dt.float32
F16 = mybir.dt.float16
U32 = mybir.dt.uint32
I32 = mybir.dt.int32
ds = bass.ds

P = 128
H = W = 64
C = 256
CC = C // P
N = H * W
NT = 512
TILES = N // NT
TR = NT // W
HD = 32
HEADS = C // HD
GN_EPS = 1e-5


class Chain:

    def __init__(self, engine, sem):
        self.engine, self.sem, self.n = engine, sem, 0

    def done(self, ins):
        ins.then_inc(self.sem, 1)
        self.n += 1
        return ins

    def wait(self):
        self.engine.wait_ge(self.sem, self.n)


def tile_statistics(nc, X, stats, c, t):
    return nc.vector.bn_stats(stats[:, c, t, :], X[:, c, t * NT:(t + 1) * NT])


def group_norm_stats(nc, name, sem, X, stats, aggr, group_avg, ps_stat, cols, early=False, wait_tile=None):
    chan_ready = sem(name + "_channel_means")
    mean_ready = sem(name + "_group_means")
    dev_ready = sem(name + "_channel_vars")
    var_ready = sem(name + "_group_vars")
    std_ready = sem(name + "_group_std")
    dve_step = sem(name + "_dve_step")
    STEPS = 7 + (0 if early else CC * TILES)

    def vector(dve):
        chain = Chain(dve, dve_step)
        if not early:
            for c in range(CC):
                for t in range(TILES):
                    if wait_tile:
                        wait_tile(dve, c, t)
                    chain.done(tile_statistics(nc, X, stats, c, t))
            chain.wait()
        for c in range(CC):
            chain.done(nc.vector.bn_aggr(aggr[:, c, 0:2], stats[:, c, :, :].rearrange("p t s -> p (t s)")))
        chain.wait()
        nc.vector.tensor_copy(cols[:, 2, :], aggr[:, :, 0]).then_inc(chan_ready, 1)
        dve.wait_ge(mean_ready, 1)
        chain.done(nc.vector.tensor_copy(cols[:, 3, :], ps_stat[:, 0:CC]))
        chain.wait()
        chain.done(nc.vector.tensor_tensor(cols[:, 4, :], aggr[:, :, 0], cols[:, 3, :], ALU.subtract))
        chain.wait()
        chain.done(nc.vector.tensor_tensor(cols[:, 5, :], cols[:, 4, :], cols[:, 4, :], ALU.mult))
        chain.wait()
        nc.vector.tensor_tensor(cols[:, 6, :], cols[:, 5, :], aggr[:, :, 1], ALU.add).then_inc(dev_ready, 1)
        dve.wait_ge(std_ready, 1)
        chain.done(nc.vector.reciprocal(cols[:, 0, :], cols[:, 7, :]))
        chain.wait()
        chain.done(nc.vector.scalar_tensor_tensor(out=cols[:, 1, :], in0=cols[:, 3, :], scalar=-1.0,
                                                  in1=cols[:, 0, :], op0=ALU.mult, op1=ALU.mult))
        chain.wait()
        assert chain.n == STEPS

    def tensor(pe):
        pe.wait_ge(chan_ready, 1)
        nc.tensor.matmul(ps_stat[:, 0:CC], group_avg[:, :], cols[:, 2, :], start=True, stop=True).then_inc(mean_ready, 1)
        pe.wait_ge(dev_ready, 1)
        nc.tensor.matmul(ps_stat[:, CC:2 * CC], group_avg[:, :], cols[:, 6, :], start=True, stop=True).then_inc(var_ready, 1)

    def scalar(act, eps_col):
        act.wait_ge(var_ready, 1)
        nc.scalar.activation(cols[:, 7, :], ps_stat[:, CC:2 * CC], ACT.Sqrt, bias=eps_col).then_inc(std_ready, 1)

    def wait_ready(engine):
        engine.wait_ge(dve_step, STEPS)

    return vector, tensor, scalar, wait_ready


def layer0_conv(nc, sem, X, x, w_convs, w_dw, temp, ones_head, group_avg, eps_col, stats, Qhl, Khl, consts_ready):
    KS = (1, 3, 5)
    TAPS = [k * k for k in KS]
    UNIT0 = [0, CC * TAPS[0], CC * (TAPS[0] + TAPS[1])]
    UNITS = CC * sum(TAPS)
    G = 4
    PIECES = [[(UNIT0[k] + o, min(G, CC * TAPS[k] - o)) for o in range(0, CC * TAPS[k], G)] for k in range(3)]
    PIECE0 = [0, len(PIECES[0]), len(PIECES[0]) + len(PIECES[1]), sum(len(p) for p in PIECES)]
    PW = W + 4
    QW = W + 2
    ORDER = [(0, 0, 0), (1, 0, 1), (2, 0, 0), (0, 1, 1), (1, 1, 1), (2, 1, 1)]
    NB = 2
    SB = 4
    QTR = 4
    QR = H // QTR
    SPLIT = 256.0
    XSCALE = 128.0
    WSCALE = 32768.0
    TMP = 8
    with ExitStack() as ctx:
        def sb(name, shape, dt):
            return ctx.enter_context(nc.sbuf_tensor(name, shape, dt))

        xh = sb("xh", [P, CC, PW, PW], F16)
        xl = sb("xl", [P, CC, PW, PW], F16)
        wraw = sb("wraw", [P, G + UNITS, C], F32)
        wparts = wraw[:, :, :].bitcast(F16)
        qpad = [sb(f"qpad{b}", [P, QW, QW], F32) for b in range(2)]
        sq = sb("sq", [P, N], F32)
        ones = sb("ones0", [P, P], F32)
        wd = sb("wd", [P, 3 * CC, 9], F32)
        tcol = sb("tcol", [P, CC], F32)
        aggr = sb("aggr0", [P, CC, 2], F32)
        cols = sb("cols0", [P, 8, 2], F32)
        xcols = sb("xcols0", [P, 2, 2], F32)
        wss = sb("wss", [P, PIECE0[3]], F32)
        wsum = sb("wsum", [P, 3], F32)
        wroot = sb("wroot", [P, 3], F32)
        wcols = sb("wcols", [P, 4, 3], F32)
        nrm = sb("nrm", [P, 2, NT], F32)
        qn = sb("qn", [P, 2, NT], F32)
        hi = sb("hi", [P, 2, NT], F16)
        lo = sb("lo", [P, 2, NT], F16)
        psc = ctx.enter_context(nc.psum_tensor("psc", [P, NB, NT], F32))
        pss = ctx.enter_context(nc.psum_tensor("pss", [P, SB, NT], F32))
        ps_stat = ctx.enter_context(nc.psum_tensor("ps_stat0", [P, NT], F32))

        x_in = [sem(f"l0_x_in{i}") for i in range(2 * CC)]
        small_in = sem("l0_small_in")
        w_in = [sem(f"l0_w{k}_in") for k in KS]
        ones_set = sem("l0_ones_set")
        xpad_zero = sem("l0_xpad_zero")
        qpad_zero = sem("l0_qpad_zero")
        xcols_ready = sem("l0_xcols")
        xn_ready = sem("l0_xn")
        xh_ready = sem("l0_xh")
        xl_ready = sem("l0_xl")
        wss_ready = sem("l0_wss")
        wsum_ready = sem("l0_wsum")
        wall_ready = sem("l0_wall")
        wroot_ready = sem("l0_wroot")
        wcols_step = sem("l0_wcols")
        wh_ready = sem("l0_wh")
        wl_ready = sem("l0_wl")
        conv_done = sem("l0_conv_tiles")
        evac_done = sem("l0_conv_evacuated")
        dw_step = sem("l0_dw_steps")
        sq_done = sem("l0_squares")
        ss_done = sem("l0_square_sums")
        nrm_done = sem("l0_norms")
        post_step = sem("l0_post_steps")
        split_out = [sem(f"l0_split_out{b}") for b in range(2)]
        gn_vec, gn_pe, gn_act, _ = group_norm_stats(nc, "gn0", sem, X, stats, aggr, group_avg, ps_stat, cols,
                                                       wait_tile=lambda dve, c, t: dve.wait_ge(x_in[c * 2 + t // (TILES // 2)], 16))
        DW = QTR * 9
        POST = 5
        WSTEPS = 4
        QK = [i for i, (kind, _, _) in enumerate(ORDER) if kind < 2]

        block = ctx.enter_context(nc.Block())

        @block.sync
        def _(sp):
            def load_weights(k):
                for c in range(CC):
                    u = G + UNIT0[k] + c * TAPS[k]
                    sp.dma_start(wraw[:, u:u + TAPS[k], :], w_convs[k][c * P:(c + 1) * P, :, :]).then_inc(w_in[k], 16)

            load_weights(0)
            for c in range(CC):
                for h in range(2):
                    part = slice(h * (N // 2), (h + 1) * (N // 2))
                    sp.dma_start(X[:, c, part], x[c * P:(c + 1) * P, part]).then_inc(x_in[2 * c + h], 16)
            load_weights(1)
            load_weights(2)
            sp.dma_start(wd[:, :, :], w_dw.rearrange("(c p) t -> p c t", p=P)).then_inc(small_in, 16)
            sp.dma_start(tcol[:, :], temp).then_inc(small_in, 16)
            for n, i in enumerate(QK):
                kind, cc, _ = ORDER[i]
                dst = (Qhl, Khl)[kind]
                with sp.Fori(0, TILES // 2) as t:
                    for b in range(2):
                        sp.wait_ge(post_step, t * (2 * POST) + ((b + 1 + n * TILES) * POST))
                        sp.dma_start(dst[0, cc * P:(cc + 1) * P, ds(t * (2 * NT) + b * NT, NT)], hi[:, b, :]).then_inc(split_out[b], 16)
                        sp.dma_start(dst[1, cc * P:(cc + 1) * P, ds(t * (2 * NT) + b * NT, NT)], lo[:, b, :]).then_inc(split_out[b], 16)
            for b in range(2):
                sp.wait_ge(split_out[b], 32 * (TILES // 2) * len(QK))

        @block.gpsimd
        def _(pool):
            nc.gpsimd.memset(ones[:, :], 1.0).then_inc(ones_set, 1)
            for part in (xh, xl):
                nc.gpsimd.memset(part[:, :, :, :].bitcast(F32).rearrange("p c h w -> p (c h w)"), 0.0).then_inc(xpad_zero, 1)
            for b in range(2):
                nc.gpsimd.memset(qpad[b][:, :, :].rearrange("p h w -> p (h w)"), 0.0).then_inc(qpad_zero, 1)
            pool.wait_ge(xpad_zero, 2)
            for t in range(TILES):
                for c in range(CC):
                    j = t * CC + c
                    pool.wait_ge(xn_ready, j + 1)
                    tmp = sq[:, j % TMP * NT:(j % TMP + 1) * NT].rearrange("p (h w) -> p h w", h=TR)
                    nc.gpsimd.tensor_copy(xh[:, c, 2 + t * TR:2 + (t + 1) * TR, 2:2 + W], tmp).then_inc(xh_ready, 1)
            pool.wait_ge(xl_ready, TILES * CC)
            for n, i in enumerate(QK):
                slot = ORDER[i][2]
                pool.wait_ge(dw_step, (i + 1) * DW)
                if n:
                    pool.wait_ge(ss_done, n * TILES)
                for h in range(2):
                    part = X[:, slot, h * (N // 2):(h + 1) * (N // 2)]
                    nc.gpsimd.tensor_tensor(sq[:, h * (N // 2):(h + 1) * (N // 2)], part, part, ALU.mult).then_inc(sq_done, 1)

        @block.tensor
        def _(pe):
            def weight_sums(k):
                pe.wait_ge(ones_set, 1)
                pe.wait_ge(wsum_ready, k + 1)
                nc.tensor.matmul(ps_stat[:, 8 + k:9 + k], ones[:, :], wsum[:, k:k + 1], start=True, stop=True).then_inc(wall_ready, 1)

            weight_sums(0)
            pe.wait_ge(consts_ready, 16)
            gn_pe(pe)

            def conv_tile(kind, cc, t, b):
                k = KS[kind]
                off = 2 - (k - 1) // 2
                n, total = 0, 3 * CC * k * k
                for c in range(CC):
                    for dy in range(k):
                        for dx in range(k):
                            u = UNIT0[kind] + c * TAPS[kind] + dy * k + dx
                            at = (slice(None), c, ds(t * TR + off + dy, TR), slice(off + dx, off + dx + W))
                            wh = wparts[:, u, cc * P:(cc + 1) * P]
                            wl = wparts[:, u, C + cc * P:C + (cc + 1) * P]
                            for weights, image in ((wh, xh), (wh, xl), (wl, xh)):
                                last = nc.tensor.matmul(psc[:, b, :], weights, image[at], start=(n == 0), stop=(n == total - 1))
                                n += 1
                last.then_inc(conv_done, 1)

            def conv_chunk(i, first=0, last=TILES):
                kind, cc, _ = ORDER[i]
                pe.wait_ge(wl_ready, PIECE0[kind + 1])
                with pe.Fori(first // NB, last // NB) as t:
                    for b in range(NB):
                        pe.wait_ge(evac_done, t * NB + (i * TILES + b - NB + 1))
                        conv_tile(kind, cc, t * NB + b, b)

            def square_sums(n, half):
                pe.wait_ge(sq_done, 2 * (n + 1))
                for t in range(half * SB, (half + 1) * SB):
                    m = n * TILES + t
                    if m >= SB:
                        pe.wait_ge(nrm_done, m - SB + 1)
                    nc.tensor.matmul(pss[:, m % SB, :], ones_head[:, :], sq[:, t * NT:(t + 1) * NT],
                                     start=True, stop=True).then_inc(ss_done, 1)

            pe.wait_ge(wl_ready, PIECE0[1])
            for t in range(TILES):
                pe.wait_ge(xl_ready, (t + 1) * CC)
                if t >= NB:
                    pe.wait_ge(evac_done, t - NB + 1)
                conv_tile(0, 0, t, t % NB)
                if t == 5:
                    weight_sums(1)
            conv_chunk(1, 0, 4)
            weight_sums(2)
            conv_chunk(1, 4, TILES)
            square_sums(0, 0)
            conv_chunk(2, 0, 2)
            square_sums(0, 1)
            conv_chunk(2, 2, 4)
            square_sums(1, 0)
            conv_chunk(2, 4, 6)
            square_sums(1, 1)
            conv_chunk(2, 6, TILES)
            conv_chunk(3)
            conv_chunk(4, 0, 6)
            square_sums(2, 0)
            conv_chunk(4, 6, TILES)
            square_sums(2, 1)
            conv_chunk(5, 0, 4)
            square_sums(3, 0)
            conv_chunk(5, 4, 6)
            square_sums(3, 1)
            conv_chunk(5, 6, TILES)

        @block.scalar
        def _(act):
            squares = pss[:, :, :].rearrange("p b n -> p (b n)")

            def sum_squares(k):
                act.wait_ge(w_in[k], 16 * CC)
                for p, (u, n) in enumerate(PIECES[k]):
                    q = PIECE0[k] + p
                    if q:
                        act.wait_ge(wss_ready, q)
                    nc.scalar.activation(squares[:, 0:n * C], wraw[:, G + u:G + u + n, :].rearrange("p u c -> p (u c)"), ACT.Square,
                                         accum_out=wss[:, q:q + 1]).then_inc(wss_ready, 1)

            def root(k):
                act.wait_ge(wall_ready, k + 1)
                nc.scalar.activation(wroot[:, k:k + 1], ps_stat[:, 8 + k:9 + k], ACT.Sqrt).then_inc(wroot_ready, 1)

            def high_parts(k, first=0, last=None):
                act.wait_ge(wcols_step, WSTEPS * (k + 1))
                for p, (u, n) in list(enumerate(PIECES[k]))[first:last]:
                    q = PIECE0[k] + p
                    if q:
                        act.wait_ge(wl_ready, q)
                    nc.scalar.activation(wparts[:, u:u + n, 0:C], wraw[:, G + u:G + u + n, :], ACT.Copy,
                                         scale=wcols[:, 2, k:k + 1]).then_inc(wh_ready, 1)

            def evacuate_tile(i, t, b):
                kind = ORDER[i][0]
                act.wait_ge(conv_done, t + (i * TILES + 1))
                nc.scalar.activation(qpad[i % 2][:, ds(t * TR + 1, TR), 1:1 + W], psc[:, b, :].rearrange("p (h w) -> p h w", h=TR),
                                     ACT.Copy, scale=wcols[:, 3, kind:kind + 1]).then_inc(evac_done, 1)

            def wait_qpad(i):
                if i < 2:
                    act.wait_ge(qpad_zero, i + 1)
                else:
                    act.wait_ge(dw_step, (i - 1) * DW)

            def evacuate(i, first=0, last=TILES):
                if first == 0:
                    wait_qpad(i)
                with act.Fori(first // NB, last // NB) as t:
                    for b in range(NB):
                        evacuate_tile(i, t * NB + b, b)

            def norms(n, half):
                for t in range(half * SB, (half + 1) * SB):
                    m = n * TILES + t
                    act.wait_ge(ss_done, m + 1)
                    if m >= 2:
                        act.wait_ge(post_step, (m - 2) * POST + 3)
                    nc.scalar.activation(nrm[:, m % 2, :], pss[:, m % SB, :], ACT.Sqrt).then_inc(nrm_done, 1)

            sum_squares(0)
            root(0)
            high_parts(0)
            gn_act(act, eps_col)
            act.wait_ge(xcols_ready, 1)
            wait_qpad(0)
            for t in range(TILES):
                for c in range(CC):
                    j = t * CC + c
                    if j >= TMP:
                        act.wait_ge(xl_ready, j - TMP + 1)
                    nc.scalar.activation(sq[:, j % TMP * NT:(j % TMP + 1) * NT], X[:, c, t * NT:(t + 1) * NT], ACT.Identity,
                                         scale=xcols[:, 0, c:c + 1], bias=xcols[:, 1, c:c + 1]).then_inc(xn_ready, 1)
                if t >= 3:
                    evacuate_tile(0, t - 3, (t - 3) % NB)
                if t == 4:
                    sum_squares(1)
            evacuate_tile(0, TILES - 3, (TILES - 3) % NB)
            root(1)
            for t in range(TILES - 2, TILES):
                evacuate_tile(0, t, t % NB)
            high_parts(1)
            evacuate(1, 0, 2)
            sum_squares(2)
            evacuate(1, 2, 4)
            root(2)
            pieces = len(PIECES[2])
            for t in range(4, TILES):
                high_parts(2, (t - 4) * pieces // 3, min((t - 3) * pieces // 3, pieces))
                evacuate_tile(1, t, t % NB)
            norms(0, 0)
            evacuate(2, 0, 2)
            norms(0, 1)
            evacuate(2, 2, 4)
            norms(1, 0)
            evacuate(2, 4, 6)
            norms(1, 1)
            evacuate(2, 6, TILES)
            evacuate(3)
            evacuate(4, 0, 6)
            norms(2, 0)
            evacuate(4, 6, TILES)
            norms(2, 1)
            evacuate(5, 0, 4)
            norms(3, 0)
            evacuate(5, 4, 6)
            norms(3, 1)
            evacuate(5, 6, TILES)

        @block.vector
        def _(dve):
            def sum_weights(k):
                dve.wait_ge(wss_ready, PIECE0[k + 1])
                nc.vector.tensor_reduce(out=wsum[:, k:k + 1], in_=wss[:, PIECE0[k]:PIECE0[k + 1]], axis=AX_X, op=ALU.add).then_inc(wsum_ready, 1)

            def weight_cols(k):
                base = WSTEPS * k
                col = slice(k, k + 1)
                dve.wait_ge(wroot_ready, k + 1)
                nc.vector.tensor_scalar(out=wcols[:, 0, col], in0=wroot[:, col], scalar1=1e-15, scalar2=None, op0=ALU.max).then_inc(wcols_step, 1)
                dve.wait_ge(wcols_step, base + 1)
                nc.vector.reciprocal(wcols[:, 1, col], wcols[:, 0, col]).then_inc(wcols_step, 1)
                dve.wait_ge(wcols_step, base + 2)
                nc.vector.tensor_scalar(out=wcols[:, 2, col], in0=wcols[:, 1, col], scalar1=WSCALE, scalar2=None, op0=ALU.mult).then_inc(wcols_step, 1)
                nc.vector.tensor_scalar(out=wcols[:, 3, col], in0=wcols[:, 0, col], scalar1=1.0 / (WSCALE * XSCALE), scalar2=None,
                                        op0=ALU.mult).then_inc(wcols_step, 1)
                dve.wait_ge(wcols_step, base + WSTEPS)

            def low_parts(k):
                for p, (u, n) in enumerate(PIECES[k]):
                    dve.wait_ge(wh_ready, PIECE0[k] + p + 1)
                    nc.vector.scalar_tensor_tensor(out=wparts[:, u:u + n, C:2 * C], in0=wraw[:, G + u:G + u + n, :], scalar=wcols[:, 2, k:k + 1],
                                                   in1=wparts[:, u:u + n, 0:C], op0=ALU.mult, op1=ALU.subtract).then_inc(wl_ready, 1)

            sum_weights(0)
            weight_cols(0)
            low_parts(0)
            gn_vec(dve)
            nc.vector.tensor_scalar(out=xcols[:, :, :], in0=cols[:, 0:2, :], scalar1=XSCALE, scalar2=None, op0=ALU.mult).then_inc(xcols_ready, 1)
            dve.wait_ge(xpad_zero, 2)
            for t in range(TILES):
                for c in range(CC):
                    j = t * CC + c
                    dve.wait_ge(xn_ready, j + 1)
                    dve.wait_ge(xh_ready, j + 1)
                    tmp = sq[:, j % TMP * NT:(j % TMP + 1) * NT].rearrange("p (h w) -> p h w", h=TR)
                    at = (slice(None), c, slice(2 + t * TR, 2 + (t + 1) * TR), slice(2, 2 + W))
                    nc.vector.tensor_tensor(xl[at], tmp, xh[at], ALU.subtract).then_inc(xl_ready, 1)
                if t == 5:
                    sum_weights(1)
            weight_cols(1)
            low_parts(1)
            dve.wait_ge(small_in, 32)

            def taps(i, q, base):
                kind, cc, slot = ORDER[i]
                out = X[:, slot, ds(q * (QR * W), QR * W)].rearrange("p (h w) -> p h w", h=QR)
                for tap in range(9):
                    dy, dx = divmod(tap, 3)
                    src = qpad[i % 2][:, ds(q * QR + dy, QR), dx:dx + W]
                    col = wd[:, kind * CC + cc, tap:tap + 1]
                    if tap == 0:
                        ins = nc.vector.tensor_scalar(out=out, in0=src, scalar1=col, scalar2=None, op0=ALU.mult)
                    else:
                        dve.wait_ge(dw_step, base + tap)
                        ins = nc.vector.scalar_tensor_tensor(out=out, in0=src, scalar=col, in1=out, op0=ALU.mult, op1=ALU.add)
                    ins.then_inc(dw_step, 1)

            PER = TILES // QTR

            def quarter(i, q):
                last = q == QTR - 1
                dve.wait_ge(evac_done, (i + 1) * TILES if last else i * TILES + (q + 1) * PER + 1)
                taps(i, q, q * 9 + i * DW)

            def depthwise(i):
                with dve.Fori(0, QTR - 1) as q:
                    dve.wait_ge(evac_done, q * PER + (i * TILES + PER + 1))
                    taps(i, q, q * 9 + i * DW)
                quarter(i, QTR - 1)

            def normalise(n):
                i = QK[n]
                kind, cc, slot = ORDER[i]
                for t in range(TILES):
                    m = n * TILES + t
                    b = m % 2
                    base = m * POST
                    dve.wait_ge(nrm_done, m + 1)
                    nc.vector.tensor_scalar(out=nrm[:, b, :], in0=nrm[:, b, :], scalar1=1e-12, scalar2=1.0 / SPLIT,
                                            op0=ALU.max, op1=ALU.mult).then_inc(post_step, 1)
                    dve.wait_ge(post_step, base + 1)
                    nc.vector.reciprocal(nrm[:, b, :], nrm[:, b, :]).then_inc(post_step, 1)
                    dve.wait_ge(post_step, base + 2)
                    D = X[:, slot, t * NT:(t + 1) * NT]
                    if kind == 0:
                        ins = nc.vector.scalar_tensor_tensor(out=qn[:, b, :], in0=D, scalar=tcol[:, cc:cc + 1],
                                                             in1=nrm[:, b, :], op0=ALU.mult, op1=ALU.mult)
                    else:
                        ins = nc.vector.tensor_tensor(qn[:, b, :], D, nrm[:, b, :], ALU.mult)
                    ins.then_inc(post_step, 1)
                    dve.wait_ge(post_step, base + 3)
                    if m >= 2:
                        dve.wait_ge(split_out[b], 32 * (m // 2))
                    nc.vector.tensor_copy(hi[:, b, :], qn[:, b, :]).then_inc(post_step, 1)
                    dve.wait_ge(post_step, base + 4)
                    nc.vector.tensor_tensor(lo[:, b, :], qn[:, b, :], hi[:, b, :], ALU.subtract).then_inc(post_step, 1)

            depthwise(0)
            sum_weights(2)
            quarter(1, 0)
            weight_cols(2)
            low_parts(2)
            for q in range(1, QTR):
                quarter(1, q)
            normalise(0)
            normalise(1)
            depthwise(2)
            depthwise(3)
            normalise(2)
            depthwise(4)
            normalise(3)
            depthwise(5)


def layer0_attention(nc, sem, X, x, Qhl, Khl, w_proj, ident, stats):
    SPLIT2 = 1.0 / (256.0 * 256.0)
    HG = 4
    GROUPS = HEADS // HG
    MT = N // P
    UN = 2 * MT
    UI = GROUPS * UN
    RING = 3
    PRING = 8
    AHEAD = 3
    POOL_U = [1, 3, 6, 8] + list(range(11, 60, 3))
    PE_U = [UN - 2, UN - 1]
    DVE_U = [u for u in range(UN) if u not in POOL_U + PE_U]
    PIECES = 4
    PIECE_U = [18, 28, 38, 48]
    PW = NT // PIECES
    SUM_U = 13
    assert UI % PRING == 0 and PRING == TILES

    def add_steps(units):
        steps, done, first = [], {}, {}
        for u in units:
            pair = u % 2
            if pair not in first:
                first[pair] = u
                continue
            fresh = not any(p == pair for p, _, _ in steps)
            steps.append((pair, u, first[pair] if fresh else None))
            done[u] = len(steps)
            if fresh:
                done[first[pair]] = len(steps)
        return steps, done

    def last_add(steps, j):
        return max(i + 1 for i in range(j) if steps[i][0] == steps[j][0])

    (DSTEPS, DDONE), (PSTEPS, PDONE) = add_steps(DVE_U), add_steps(POOL_U)
    ND, NPOOL = len(DSTEPS), len(PSTEPS) + 2
    with ExitStack() as ctx:
        def sb(name, shape, dt):
            return ctx.enter_context(nc.sbuf_tensor(name, shape, dt))

        Kst = sb("Kst", [P, HEADS, N], F16)
        Qst = sb("Qst", [P, GROUPS, HG, NT], F16)
        V = sb("V", [P, MT, C], F32)
        prob = sb("prob", [P, PRING, 2, NT], F32)
        acc = sb("acc", [P, GROUPS, HG, NT], F32)
        accp = sb("accp", [P, GROUPS, HG, NT], F32)
        ones = sb("ones32", [P, HD], F32)
        rsum = sb("rsum", [P, NT], F32)
        wp = sb("wp", [P, CC, C], F32)
        O = X
        S = ctx.enter_context(nc.psum_tensor("S", [P, RING, 2, NT], F32))
        PO = ctx.enter_context(nc.psum_tensor("PO", [P, NT], F32))
        PS = ctx.enter_context(nc.psum_tensor("PS", [P, NT], F32))

        k_in = [sem(f"l0_k_in{g}") for g in range(GROUPS)]
        q_in = [sem(f"l0_q_in{g}") for g in range(GROUPS)]
        w_in = sem("l0_wproj_in")
        x_in = [sem(f"l0_x_again{t}") for t in range(TILES)]
        ones_ready = sem("l0_ones")
        vt_done = sem("l0_v_transposed")
        v_ready = sem("l0_v_ready")
        qk_done = sem("l0_scores")
        exp_done = sem("l0_exp")
        pv_done = sem("l0_pv")
        dve_add = sem("l0_dve_add")
        pool_add = sem("l0_pool_add")
        sums_done = sem("l0_sums")
        last_sums = sem("l0_last_sums")
        po_free = sem("l0_po_free")
        ps_free = sem("l0_ps_free")
        o_ready = sem("l0_o_ready")
        proj_done = sem("l0_proj")
        x_ready = sem("l0_x_ready")
        stats_done = sem("l0_stats")
        block = ctx.enter_context(nc.Block())

        @block.sync
        def _(sp):
            def load_q(g, off):
                for r in range(4):
                    sp.dma_start(Qst[r * HD:(r + 1) * HD, g, :, :],
                                 Qhl[r // 2, g * P:(g + 1) * P, ds(off, NT)].rearrange("(h d) n -> d h n", d=HD)).then_inc(q_in[g], 16)

            for g in range(GROUPS):
                for r in range(4):
                    sp.dma_start(Kst[r * HD:(r + 1) * HD, g * HG:(g + 1) * HG, :],
                                 Khl[r % 2, g * P:(g + 1) * P, :].rearrange("(h d) n -> d h n", d=HD)).then_inc(k_in[g], 16)
                load_q(g, 0)
            sp.dma_start(wp[:, :, :], w_proj.rearrange("(c p) n -> p c n", p=P)).then_inc(w_in, 16)
            with sp.Fori(1, TILES) as n:
                for g in range(GROUPS):
                    sp.wait_ge(qk_done, n * UI + ((g + 1) * UN - UI))
                    load_q(g, n * NT)
            sp.wait_ge(qk_done, (TILES - 1) * UI + UN)
            load_q(0, (TILES - 1) * NT)
            sp.wait_ge(pv_done, TILES * UI // 2)
            sp.wait_ge(dve_add, TILES * GROUPS * ND)
            sp.wait_ge(pool_add, TILES * GROUPS * NPOOL)
            sp.wait_ge(last_sums, TILES * GROUPS)
            for t in range(TILES):
                sp.dma_start(prob[:, t, :, :], x[:, t * NT:(t + 1) * NT].rearrange("(c p) n -> p c n", p=P)).then_inc(x_in[t], 16)

        @block.gpsimd
        def _(pool):
            nc.gpsimd.memset(ones[:, :], 1.0).then_inc(ones_ready, 1)

            def token_tile(n, first):
                for g in range(GROUPS):
                    for j, (pair, u, u0) in enumerate(PSTEPS):
                        dst = accp[:, g, 2 * pair:2 * pair + 2, :]
                        if j == 0 and not first:
                            pool.wait_ge(sums_done, n * GROUPS + (g + 1 - GROUPS))
                        if u0 is None:
                            pool.wait_ge(pool_add, n * (GROUPS * NPOOL) + (g * NPOOL + last_add(PSTEPS, j)))
                        pool.wait_ge(exp_done, n * UI + (g * UN + u + 1))
                        a = dst if u0 is None else prob[:, (g * UN + u0) % PRING, :, :]
                        nc.gpsimd.tensor_tensor(dst, a, prob[:, (g * UN + u) % PRING, :, :], ALU.add).then_inc(pool_add, 1)
                    pool.wait_ge(dve_add, n * (GROUPS * ND) + (g + 1) * ND)
                    pool.wait_ge(pool_add, n * (GROUPS * NPOOL) + (g * NPOOL + len(PSTEPS)))
                    for pair in range(2):
                        part = accp[:, g, 2 * pair:2 * pair + 2, :]
                        nc.gpsimd.tensor_tensor(part, part, acc[:, g, 2 * pair:2 * pair + 2, :], ALU.add).then_inc(pool_add, 1)

            token_tile(0, True)
            with pool.Fori(1, TILES) as n:
                token_tile(n, False)

        @block.scalar
        def _(act):
            def wait_summed(n, k):
                g, u = k // UN, k % UN
                if u in PE_U:
                    act.wait_ge(last_sums, n * GROUPS + (g + 1))
                elif u in DDONE:
                    act.wait_ge(dve_add, n * (GROUPS * ND) + (g * ND + DDONE[u]))
                else:
                    act.wait_ge(pool_add, n * (GROUPS * NPOOL) + (g * NPOOL + PDONE[u]))

            def token_tile(n, before):
                for k in range(UI):
                    act.wait_ge(qk_done, n * UI + (k + 1))
                    if k >= PRING:
                        act.wait_ge(pv_done, n * (UI // 2) + ((k - PRING) // 2 + 1))
                        wait_summed(n, k - PRING)
                    elif before is not None:
                        act.wait_ge(pv_done, n * (UI // 2) + (k - PRING) // 2 + 1)
                        wait_summed(before, k - PRING + UI)
                    nc.scalar.activation(prob[:, k % PRING, :, :], S[:, k % RING, :, :], ACT.Exp, scale=SPLIT2).then_inc(exp_done, 1)

            token_tile(0, None)
            with act.Fori(1, TILES) as n:
                token_tile(n, n - 1)

        @block.tensor
        def _(pe):
            for r in range(MT // 2):
                if r >= 2 * RING:
                    pe.wait_ge(v_ready, r - 2 * RING + 1)
                s = r % (2 * RING)
                for q in range(4):
                    j, c = 2 * r + q // 2, q % 2
                    last = nc.tensor.transpose(S[:, s // 2, s % 2, q * P:(q + 1) * P], X[:, c, j * P:(j + 1) * P], ident[:, :])
                last.then_inc(vt_done, 1)
            pe.wait_ge(v_ready, MT // 2)
            pe.wait_ge(ones_ready, 1)

            def scores(n, k, first):
                g, m, pair = k // UN, k % UN // 2, k % 2
                if k % UN == 0:
                    pe.wait_ge(q_in[g], (n + 1) * 64)
                    if first:
                        pe.wait_ge(k_in[g], 64)
                if k >= RING:
                    pe.wait_ge(exp_done, n * UI + (k - RING + 1))
                elif not first:
                    prev = max(u for u in range(UI - RING, UI) if u % RING == k)
                    pe.wait_ge(exp_done, n * UI + (prev + 1 - UI))
                for hh in range(2):
                    h = 2 * pair + hh
                    last = nc.tensor.matmul(S[:, k % RING, hh, :], Kst[:, g * HG + h, m * P:(m + 1) * P], Qst[:, g, h, :], start=True, stop=True)
                last.then_inc(qk_done, 1)

            def sums(n, g):
                pe.wait_ge(pool_add, n * (GROUPS * NPOOL) + (g + 1) * NPOOL)
                for h in range(HG):
                    last = nc.tensor.matmul(PS[h * HD:(h + 1) * HD, :], ones[:, :], accp[:, g, h, :], start=False, stop=True)
                last.then_inc(sums_done, 1)

            def token_tile(n, first):
                for k in range(UI):
                    g, m, pair = k // UN, k % UN // 2, k % 2
                    ahead = k + AHEAD
                    if ahead < UI:
                        scores(n, ahead, first)
                    else:
                        scores(n + 1, ahead - UI, False)
                    if pair == 0:
                        continue
                    pe.wait_ge(exp_done, n * UI + (k + 1))
                    if m == 0 and not (first and g == 0):
                        pe.wait_ge(po_free, n * GROUPS + g)
                    for h in range(HG):
                        u = k - 1 + h // 2
                        last = nc.tensor.matmul(PO[h * HD:(h + 1) * HD, :], V[:, m, (g * HG + h) * HD:(g * HG + h + 1) * HD],
                                                prob[:, u % PRING, h % 2, :], start=(m == 0), stop=(m == MT - 1))
                    last.then_inc(pv_done, 1)
                    if m == MT - 1:
                        if not (first and g == 0):
                            pe.wait_ge(ps_free, n * (GROUPS * PIECES) + g * PIECES)
                        for h in range(HG):
                            last = nc.tensor.matmul(PS[h * HD:(h + 1) * HD, :], ones[:, :], prob[:, (k - 1 + h // 2) % PRING, h % 2, :],
                                                    start=True, stop=False)
                        last.then_inc(last_sums, 1)
                    if k % UN == SUM_U:
                        if g:
                            sums(n, g - 1)
                        elif not first:
                            sums(n - 1, GROUPS - 1)

            for k in range(AHEAD):
                scores(0, k, True)
            token_tile(0, True)
            with pe.Fori(1, TILES) as n:
                token_tile(n, False)
            sums(TILES - 1, GROUPS - 1)
            pe.wait_ge(w_in, 16)
            pe.wait_ge(exp_done, TILES * UI)
            for t in range(TILES):
                pe.wait_ge(o_ready, (t + 1) * GROUPS * PIECES)
                for o in range(CC):
                    r = t * CC + o
                    s = r % (2 * RING)
                    if r >= 2 * RING:
                        pe.wait_ge(x_ready, r - 2 * RING + 1)
                    for c in range(CC):
                        last = nc.tensor.matmul(S[:, s // 2, s % 2, :], wp[:, c, o * P:(o + 1) * P], O[:, c, t * NT:(t + 1) * NT],
                                                start=(c == 0), stop=(c == CC - 1))
                last.then_inc(proj_done, 1)

        @block.vector
        def _(dve):
            for r in range(MT // 2):
                dve.wait_ge(vt_done, r + 1)
                s = r % (2 * RING)
                nc.vector.tensor_copy(V[:, 2 * r:2 * r + 2, :].rearrange("p j c -> p (j c)"), S[:, s // 2, s % 2, :]).then_inc(v_ready, 1)

            def copy_values(n, g):
                dve.wait_ge(pv_done, n * (UI // 2) + (g + 1) * MT)
                nc.vector.tensor_copy(O[:, g, ds(n * NT, NT)], PO[:, :]).then_inc(po_free, 1)

            def normalise_piece(n, g, j):
                dve.wait_ge(po_free, n * GROUPS + (g + 1))
                dve.wait_ge(sums_done, n * GROUPS + (g + 1))
                count = n * (GROUPS * PIECES) + (g * PIECES + j + 1)
                part = slice(j * PW, (j + 1) * PW)
                nc.vector.reciprocal(rsum[:, part], PS[:, part]).then_inc(ps_free, 1)
                dve.wait_ge(ps_free, count)
                out = O[:, g, ds(n * NT + j * PW, PW)]
                nc.vector.tensor_tensor(out, out, rsum[:, part], ALU.mult).then_inc(o_ready, 1)

            def token_tile(n, before):
                for g in range(GROUPS):
                    prev = (n, 0) if g else (before, 1)
                    pieces = list(zip(PIECE_U, range(PIECES))) if prev[0] is not None else []
                    for j, (pair, u, u0) in enumerate(DSTEPS):
                        while pieces and u >= pieces[0][0]:
                            normalise_piece(*prev, pieces.pop(0)[1])
                        dst = acc[:, g, 2 * pair:2 * pair + 2, :]
                        if j == 0 and before is not None:
                            dve.wait_ge(sums_done, n * GROUPS + (g + 1 - GROUPS))
                        if u0 is None:
                            dve.wait_ge(dve_add, n * (GROUPS * ND) + (g * ND + last_add(DSTEPS, j)))
                        dve.wait_ge(exp_done, n * UI + (g * UN + u + 1))
                        a = dst if u0 is None else prob[:, (g * UN + u0) % PRING, :, :]
                        nc.vector.tensor_tensor(dst, a, prob[:, (g * UN + u) % PRING, :, :], ALU.add).then_inc(dve_add, 1)
                    copy_values(n, g)

            token_tile(0, None)
            with dve.Fori(1, TILES) as n:
                token_tile(n, n - 1)
            for j in range(PIECES):
                normalise_piece(TILES - 1, GROUPS - 1, j)
            def next_stats(t):
                dve.wait_ge(x_ready, (t + 1) * CC)
                for c in range(CC):
                    tile_statistics(nc, X, stats, c, t).then_inc(stats_done, 1)

            for t in range(TILES):
                dve.wait_ge(x_in[t], 16)
                dve.wait_ge(proj_done, t + 1)
                for o in range(CC):
                    s = (t * CC + o) % (2 * RING)
                    nc.vector.tensor_tensor(X[:, o, t * NT:(t + 1) * NT], S[:, s // 2, s % 2, :], prob[:, t, o, :], ALU.add).then_inc(x_ready, 1)
                if t:
                    next_stats(t - 1)
            next_stats(TILES - 1)
            dve.wait_ge(stats_done, TILES * CC)


def layer1_codebook(nc, sem, X, Xs, Os, codes, codes_t, ident, group_avg, eps_col, stats):
    K = codes.shape[1]
    KB = K // NT
    MT = N // P
    RING = 4
    with ExitStack() as ctx:
        def sb(name, shape, dt):
            return ctx.enter_context(nc.sbuf_tensor(name, shape, dt))

        E2 = sb("E2", [P, CC, K], F32)
        Esq = sb("Esq", [P, CC, K], F32)
        nee = sb("nee", [P, K], F32)
        ones = sb("ones1", [P, P], F32)
        aggr = sb("aggr1", [P, CC, 2], F32)
        cols = sb("cols1", [P, 8, 2], F32)
        xt = sb("xt1", [P, RING, CC, P], F32)
        xsq = sb("xsq1", [P, RING, CC, P], F32)
        nxx = sb("nxx", [P, RING, 1], F32)
        nd = sb("nd", [P, RING, K], F32)
        best = sb("best", [P, RING, 8], F32)
        idx = sb("idx", [P, RING, 8], U32)
        quant = sb("quant", [P, RING, C], F32)
        ct = sb("ct", [P, RING, C], F32)
        zeros = sb("zeros1", [P, 2048], F32)
        D = ctx.enter_context(nc.psum_tensor("D1", [P, 2, KB, NT], F32))
        T = ctx.enter_context(nc.psum_tensor("T1", [P, 2, NT], F32))
        px = ctx.enter_context(nc.psum_tensor("px1", [P, 2, NT], F32))
        ps = px[:, 0, :]

        zeros_set = sem("l1_zeros_set")
        rows_zero = sem("l1_rows_zero")
        e_in = sem("l1_codes_in")
        ones_ready = sem("l1_ones")
        e_step = sem("l1_code_steps")
        ee_done = sem("l1_ee")
        nee_ready = sem("l1_nee")
        xt_ready = sem("l1_xt")
        sq_ready = sem("l1_xsq")
        d_done = sem("l1_products")
        nxx_ready = sem("l1_nxx")
        nd_ready = sem("l1_nd")
        best_ready = sem("l1_best")
        idx_ready = sem("l1_idx")
        q_in = [sem(f"l1_quant_in{b}") for b in range(RING)]
        qt_done = sem("l1_quant_t")
        ct_ready = sem("l1_ct")
        x_done = sem("l1_x")
        stats_done = sem("l1_stats")
        gn_vec, gn_pe, gn_act, gn_wait = group_norm_stats(nc, "gn1", sem, X, stats, aggr, group_avg, ps, cols, early=True)
        block = ctx.enter_context(nc.Block())

        @block.sync
        def _(sp):
            sp.dma_start(E2[:, :, :], codes.rearrange("(c p) k -> p c k", p=P)).then_inc(e_in, 16)
            sp.wait_ge(zeros_set, 1)
            per = zeros.shape[1]
            count = 0
            for rows in (Xs, Os):
                flat = rows.rearrange("(p r) c -> p (r c)", p=P)
                for o in range(0, flat.shape[1], per):
                    sp.dma_start(flat[:, o:o + per], zeros[:, :]).then_inc(rows_zero, 16)
                    count += 16
            sp.wait_ge(rows_zero, count)

        @block.gpsimd
        def _(pool):
            nc.gpsimd.memset(ones[:, :], 1.0).then_inc(ones_ready, 1)
            nc.gpsimd.memset(zeros[:, :], 0.0).then_inc(zeros_set, 1)

            def square(i):
                b = i % RING
                pool.wait_ge(xt_ready, i + 1)
                nc.gpsimd.tensor_tensor(xsq[:, b, :, :], xt[:, b, :, :], xt[:, b, :, :], ALU.mult).then_inc(sq_ready, 1)

            def add_codes(i):
                xi = X[:, :, i * P:(i + 1) * P]
                pool.wait_ge(ct_ready, i + 1)
                nc.gpsimd.tensor_tensor(xi, ct[:, i % RING, :].rearrange("p (c n) -> p c n", c=CC), xi, ALU.add).then_inc(x_done, 1)

            for i in range(RING - 1):
                square(i)
            for i in range(MT):
                if i + RING - 1 < MT:
                    square(i + RING - 1)
                if i >= RING:
                    pool.wait_ge(qt_done, i - RING + 1)
                pool.wait_ge(idx_ready, i + 1)
                nc.gpsimd.indirect_dma_start(out=quant[:, i % RING, :], out_offset=None, in_=codes_t,
                                             in_offset=bass.IndirectOffsetOnAxis(ap=idx[:, i % RING, 0:1], axis=0)).then_inc(q_in[i % RING], 16)
                if i >= RING:
                    add_codes(i - RING)
            for i in range(MT - RING, MT):
                add_codes(i)

        @block.scalar
        def _(act):
            gn_act(act, eps_col)
            act.wait_ge(ee_done, KB)
            nc.scalar.activation(nee[:, :], D[:, 0, :, :].rearrange("p k n -> p (k n)"), ACT.Copy, scale=-1.0).then_inc(nee_ready, 1)
            gn_wait(act)

            def norm(r, b, first):
                i = r * RING + b
                if not first:
                    act.wait_ge(d_done, r * RING + (b - RING + 1))
                for c in range(CC):
                    ins = nc.scalar.activation(xt[:, b, c, :], X[:, c, ds(r * (RING * P) + b * P, P)], ACT.Identity,
                                               scale=cols[:, 0, c:c + 1], bias=cols[:, 1, c:c + 1])
                ins.then_inc(xt_ready, 1)

            def token_norms(r, b, first):
                act.wait_ge(d_done, r * RING + (b + 1))
                if not first:
                    act.wait_ge(nd_ready, r * RING + (b - RING + 1))
                nc.scalar.activation(nxx[:, b, :], px[:, b % 2, 0:1], ACT.Copy, scale=-1.0).then_inc(nxx_ready, 1)

            for b in range(RING):
                norm(0, b, True)
            def copy_codes(r, b, first):
                act.wait_ge(qt_done, r * RING + (b + 1))
                if not first:
                    act.wait_ge(x_done, r * RING + (b - RING + 1))
                nc.scalar.activation(ct[:, b, :], T[:, b % 2, 0:C], ACT.Copy).then_inc(ct_ready, 1)

            for b in range(RING):
                token_norms(0, b, True)
                norm(1, b, False)
            for b in range(RING):
                token_norms(1, b, False)
                norm(2, b, False)
                copy_codes(0, b, True)
            with act.Fori(2, MT // RING - 1) as r:
                for b in range(RING):
                    token_norms(r, b, False)
                    norm(r + 1, b, False)
                    copy_codes(r - 1, b, False)
            for b in range(RING):
                token_norms(MT // RING - 1, b, False)
                copy_codes(MT // RING - 2, b, False)
            for b in range(RING):
                copy_codes(MT // RING - 1, b, False)

        @block.tensor
        def _(pe):
            gn_pe(pe)
            pe.wait_ge(ones_ready, 1)
            pe.wait_ge(e_step, 1)
            for k in range(KB):
                for c in range(CC):
                    last = nc.tensor.matmul(D[:, 0, k, :], ones[:, :], Esq[:, c, k * NT:(k + 1) * NT], start=(c == 0), stop=(c == CC - 1))
                last.then_inc(ee_done, 1)
            pe.wait_ge(nee_ready, 1)
            pe.wait_ge(e_step, 2)

            def products(r, b, early):
                pe.wait_ge(xt_ready, r * RING + (b + 1))
                pe.wait_ge(sq_ready, r * RING + (b + 1))
                if not early:
                    pe.wait_ge(nxx_ready, r * RING + (b - 1))
                    pe.wait_ge(nd_ready, r * RING + (b - 1))
                for c in range(CC):
                    nc.tensor.matmul(px[:, b % 2, 0:1], xsq[:, b, c, :], ones[:, 0:1], start=(c == 0), stop=(c == CC - 1))
                for k in range(KB):
                    part = slice(k * NT, (k + 1) * NT)
                    for c in range(CC):
                        last = nc.tensor.matmul(D[:, b % 2, k, :], xt[:, b, c, :], E2[:, c, part], start=(c == 0), stop=(c == CC - 1))
                last.then_inc(d_done, 1)

            def transpose(r, b, early):
                pe.wait_ge(q_in[b], r * 16 + 16)
                if not early:
                    pe.wait_ge(ct_ready, r * RING + (b - 1))
                for c in range(CC):
                    last = nc.tensor.transpose(T[:, b % 2, c * P:(c + 1) * P], quant[:, b, c * P:(c + 1) * P], ident)
                last.then_inc(qt_done, 1)

            for b in range(RING):
                products(0, b, b < 2)
            for b in range(RING):
                products(1, b, False)
                transpose(0, b, b < 2)
            with pe.Fori(2, MT // RING) as r:
                for b in range(RING):
                    products(r, b, False)
                    transpose(r - 1, b, False)
            for b in range(RING):
                transpose(MT // RING - 1, b, False)

        @block.vector
        def _(dve):
            gn_vec(dve)
            dve.wait_ge(e_in, 16)
            nc.vector.tensor_tensor(Esq[:, :, :], E2[:, :, :], E2[:, :, :], ALU.mult).then_inc(e_step, 1)
            dve.wait_ge(e_step, 1)
            nc.vector.tensor_scalar(out=E2[:, :, :], in0=E2[:, :, :], scalar1=2.0, scalar2=None, op0=ALU.mult).then_inc(e_step, 1)

            dve.wait_ge(nee_ready, 1)

            def distances(i):
                b = i % RING
                dve.wait_ge(d_done, i + 1)
                dve.wait_ge(nxx_ready, i + 1)
                if i >= RING:
                    dve.wait_ge(idx_ready, i - RING + 1)
                nc.vector.scalar_tensor_tensor(out=nd[:, b, :], in0=D[:, b % 2, :, :].rearrange("p k n -> p (k n)"), scalar=nxx[:, b, :],
                                               in1=nee[:, :], op0=ALU.add, op1=ALU.add).then_inc(nd_ready, 1)

            per = NT // P

            def done(t):
                return (t + 1) * per + RING + 2

            def next_stats(t):
                dve.wait_ge(x_done, (t + 1) * per)
                for c in range(CC):
                    tile_statistics(nc, X, stats, c, t).then_inc(stats_done, 1)

            distances(0)
            for i in range(MT):
                b = i % RING
                dve.wait_ge(nd_ready, i + 1)
                nc.vector.max(best[:, b, :], nd[:, b, :]).then_inc(best_ready, 1)
                if i + 1 < MT:
                    distances(i + 1)
                if i >= RING:
                    dve.wait_ge(q_in[b], 16 * (i // RING))
                dve.wait_ge(best_ready, i + 1)
                nc.vector.max_index(idx[:, b, :], best[:, b, :], nd[:, b, :]).then_inc(idx_ready, 1)
                if i >= done(0) and (i - done(0)) % per == 0:
                    next_stats((i - done(0)) // per)
            for t in range((MT - 1 - done(0)) // per + 1, TILES):
                next_stats(t)
            dve.wait_ge(stats_done, TILES * CC)


EXPERTS = 8
SLOTS = N // P + EXPERTS
WIN = 8
PAIRS = N // P


def by_window(ap):
    return ap.rearrange("p (r w c) -> p w r c", r=WIN, c=WIN)


def expert_weights(nc, ctx, sem, tag, w, bias):
    wsb = ctx.enter_context(nc.sbuf_tensor(tag + "w", [P, CC, w.shape[1]], F32))
    bsb = ctx.enter_context(nc.sbuf_tensor(tag + "b", [P, w.shape[1]], F32))
    w_in = sem(tag + "_w_in")

    def load(sp):
        for c in range(CC):
            sp.dma_start(wsb[:, c, :], w[c * P:(c + 1) * P, :]).then_inc(w_in, 16)
        sp.dma_start(bsb[:, :], bias.partition_broadcast(P)).then_inc(w_in, 16)
    return wsb, bsb, w_in, 16 * (CC + 1), load


def layer2_route(nc, sem, X, rw1, rb1, rw2, rb2, consts2, ident, group_avg, eps_col, stats, pos, pmax, expert, Xs, load_weights):
    HID = rw1.shape[1]
    with ExitStack() as ctx:
        def sb(name, shape, dt):
            return ctx.enter_context(nc.sbuf_tensor(name, shape, dt))

        xw = sb("xw", [P, CC, N], F32)
        XT = sb("XT", [P, PAIRS, C], F32)
        w1 = sb("rw1", [P, CC, HID], F32)
        b1 = sb("rb1", [P, 1], F32)
        w2 = sb("rw2", [P, EXPERTS], F32)
        b2 = sb("rb2", [1, EXPERTS], F32)
        cst = sb("cst2", [P, 2, P], F32)
        iota = sb("iota8", [P, PAIRS, EXPERTS], F32)
        tilec = sb("tilec", [P, SLOTS, EXPERTS], F32)
        hid = sb("hid", [P, 2, NT], F32)
        aggr = sb("aggr2", [P, CC, 2], F32)
        cols = sb("cols2", [P, 8, 2], F32)
        te = [sb(f"te{k}", [P, PAIRS, EXPERTS], F32) for k in range(4)]
        et = [sb(f"et{k}", [P, EXPERTS, PAIRS], F32) for k in range(3)]
        tk = [sb(f"tk{k}", [P, PAIRS], F32) for k in range(4)]
        ex = [sb(f"ex{k}", [P, EXPERTS], F32) for k in range(4)]
        exi = sb("exi", [P, 2, EXPERTS], I32)
        ones = sb("ones2", [P, PAIRS], F32)
        tcmp = sb("tcmp", [P, SLOTS, EXPERTS], F32)
        tsum = sb("tsum", [P, SLOTS], F32)
        psh = ctx.enter_context(nc.psum_tensor("psh", [P, 2, NT], F32))
        psl = ctx.enter_context(nc.psum_tensor("psl", [P, NT], F32))
        psx = ctx.enter_context(nc.psum_tensor("psx", [P, 3, NT], F32))
        psc = ctx.enter_context(nc.psum_tensor("psc2", [P, NT], F32))
        ps = ctx.enter_context(nc.psum_tensor("ps2", [P, NT], F32))

        w_in = sem("l2_w_in")
        xw_ready = sem("l2_xw")
        hid_done = sem("l2_hid")
        relu_done = sem("l2_relu")
        logits_done = sem("l2_logits")
        xt_done = sem("l2_xt")
        xt_ready = sem("l2_xt_ready")
        shift_ready = sem("l2_shift")
        exp_done = sem("l2_exp")
        onehot_ready = sem("l2_onehot")
        count_done = sem("l2_count")
        pos_ready = sem("l2_pos")
        chain_sem = sem("l2_chain")
        scattered = sem("l2_scattered")
        gn_vec, gn_pe, gn_act, _ = group_norm_stats(nc, "gn2", sem, X, stats, aggr, group_avg, ps, cols, early=True)
        block = ctx.enter_context(nc.Block())
        LOADS = 7

        @block.sync
        def _(sp):
            loads = [(w1[:, :, :], rw1.rearrange("(c p) m -> p c m", p=P)), (b1[:, :], rb1), (w2[:, :], rw2), (b2[:, :], rb2),
                     (cst[:, :, :], consts2["tri"]), (iota[:, :, :], consts2["iota"]), (tilec[:, :, :], consts2["tile"])]
            assert len(loads) == LOADS
            for dst, src in loads:
                sp.dma_start(dst, src).then_inc(w_in, 16)
            load_weights(sp)

        @block.gpsimd
        def _(pool):
            pool.wait_ge(xt_ready, PAIRS // 2)
            pool.wait_ge(pos_ready, 1)
            for i in range(PAIRS):
                nc.gpsimd.indirect_dma_start(out=Xs, out_offset=bass.IndirectOffsetOnAxis(ap=pos[:, i:i + 1], axis=0),
                                             in_=XT[:, i, :], in_offset=None).then_inc(scattered, 16)
            pool.wait_ge(scattered, 16 * PAIRS)

        @block.scalar
        def _(act):
            gn_act(act, eps_col)
            act.wait_ge(w_in, 16 * LOADS)

            def transposed(r):
                act.wait_ge(xt_done, r + 1)
                nc.scalar.activation(XT[:, 2 * r:2 * r + 2, :].rearrange("p j c -> p (j c)"), psx[:, r % 3, :], ACT.Copy).then_inc(xt_ready, 1)

            for t in range(TILES):
                act.wait_ge(hid_done, t + 1)
                if t >= 2:
                    act.wait_ge(logits_done, t - 1)
                nc.scalar.activation(hid[:, t % 2, :], psh[:, t % 2, :], ACT.Relu, bias=b1[:, 0:1]).then_inc(relu_done, 1)
                transposed(2 * t)
                transposed(2 * t + 1)
            act.wait_ge(shift_ready, 1)
            nc.scalar.activation(te[1][:, :, :], te[0][:, :, :], ACT.Exp).then_inc(exp_done, 1)

        @block.tensor
        def _(pe):
            gn_pe(pe)
            pe.wait_ge(w_in, 16 * LOADS)

            def hidden(t):
                pe.wait_ge(xw_ready, CC * (t + 1))
                if t >= 2:
                    pe.wait_ge(relu_done, t - 1)
                for c in range(CC):
                    last = nc.tensor.matmul(psh[:, t % 2, :], w1[:, c, :], xw[:, c, t * NT:(t + 1) * NT], start=(c == 0), stop=(c == CC - 1))
                last.then_inc(hid_done, 1)

            hidden(0)
            for t in range(TILES):
                if t + 1 < TILES:
                    hidden(t + 1)
                for r in (2 * t, 2 * t + 1):
                    if r >= 3:
                        pe.wait_ge(xt_ready, r - 2)
                    for q in range(4):
                        i, c = 2 * r + q // 2, q % 2
                        last = nc.tensor.transpose(psx[:, r % 3, q * P:(q + 1) * P], xw[:, c, i * P:(i + 1) * P], ident)
                    last.then_inc(xt_done, 1)
                pe.wait_ge(relu_done, t + 1)
                for q in range(NT // P):
                    i = t * (NT // P) + q
                    o = psl[:, i * EXPERTS:(i + 1) * EXPERTS]
                    nc.tensor.matmul(o, hid[:, t % 2, q * P:(q + 1) * P], w2[:, :], start=True, stop=False)
                    last = nc.tensor.matmul(o, cst[0:1, 1, :], b2[0:1, :], start=False, stop=True)
                last.then_inc(logits_done, 1)
            pe.wait_ge(onehot_ready, 1)
            half = PAIRS * EXPERTS
            rhs = te[3][:, :, :].rearrange("p i e -> p (i e)")
            for k in range(2):
                last = nc.tensor.matmul(psc[:, k * half:(k + 1) * half], cst[:, k, :], rhs, start=True, stop=True)
            last.then_inc(count_done, 1)

        @block.vector
        def _(dve):
            gn_vec(dve)
            for t in range(TILES):
                for c in range(CC):
                    nc.vector.tensor_scalar(out=xw[:, c, t * NT:(t + 1) * NT].rearrange("p (w r c) -> p w r c", r=WIN, c=WIN),
                                            in0=by_window(X[:, c, t * NT:(t + 1) * NT]),
                                            scalar1=cols[:, 0, c:c + 1], scalar2=cols[:, 1, c:c + 1],
                                            op0=ALU.mult, op1=ALU.add).then_inc(xw_ready, 1)
            chain = Chain(dve, chain_sem)

            def step(ins):
                chain.done(ins)
                chain.wait()

            def each(ap):
                return ap.unsqueeze(2).to_broadcast([P, PAIRS, EXPERTS])

            V = nc.vector
            dve.wait_ge(logits_done, TILES)
            logits = psl[:, 0:PAIRS * EXPERTS].rearrange("p (i e) -> p i e", e=EXPERTS)
            step(V.tensor_reduce(out=tk[0][:, :], in_=logits, axis=AX_X, op=ALU.max))
            V.tensor_tensor(te[0][:, :, :], logits, each(tk[0][:, :]), ALU.subtract).then_inc(shift_ready, 1)
            dve.wait_ge(exp_done, 1)
            step(V.tensor_reduce(out=tk[1][:, :], in_=te[1][:, :, :], axis=AX_X, op=ALU.add))
            step(V.reciprocal(tk[1][:, :], tk[1][:, :]))
            step(V.tensor_tensor(te[2][:, :, :], te[1][:, :, :], each(tk[1][:, :]), ALU.mult))
            step(V.tensor_reduce(out=pmax[:, :], in_=te[2][:, :, :], axis=AX_X, op=ALU.max))
            dve.wait_ge(w_in, 16 * LOADS)
            step(V.tensor_tensor(te[0][:, :, :], te[2][:, :, :], each(pmax[:, :]), ALU.is_equal))
            step(V.scalar_tensor_tensor(out=te[1][:, :, :].rearrange("p i e -> p (i e)"), in0=te[0][:, :, :].rearrange("p i e -> p (i e)"),
                                        scalar=-float(EXPERTS), in1=iota[:, :, :].rearrange("p i e -> p (i e)"), op0=ALU.mult, op1=ALU.add))
            step(V.tensor_reduce(out=tk[2][:, :], in_=te[1][:, :, :], axis=AX_X, op=ALU.min))
            V.tensor_tensor(te[3][:, :, :], te[1][:, :, :], each(tk[2][:, :]), ALU.is_equal).then_inc(onehot_ready, 1)
            step(V.memset(ones[:, :], 1.0))
            dve.wait_ge(count_done, 1)
            half = PAIRS * EXPERTS
            step(V.tensor_copy(et[0][:, :, :], psc[:, half:2 * half].rearrange("p (i e) -> p e i", e=EXPERTS)))
            for e in range(EXPERTS):
                chain.done(V.tensor_tensor_scan(out=et[1][:, e, :], data0=ones[:, 0:PAIRS], data1=et[0][:, e, :], initial=0.0,
                                                op0=ALU.mult, op1=ALU.add))
            chain.wait()
            step(V.tensor_tensor(et[2][:, :, :], et[1][:, :, :], et[0][:, :, :], ALU.subtract))
            step(V.tensor_scalar(out=exi[:, 0, :], in0=et[1][:, :, PAIRS - 1], scalar1=float(P - 1), scalar2=None, op0=ALU.add))
            step(V.tensor_scalar(out=exi[:, 1, :], in0=exi[:, 0, :], scalar1=P.bit_length() - 1, scalar2=None, op0=ALU.arith_shift_right))
            step(V.tensor_copy(ex[0][:, :], exi[:, 1, :]))
            step(V.tensor_tensor_scan(out=ex[1][:, :], data0=ones[:, 0:EXPERTS], data1=ex[0][:, :], initial=0.0, op0=ALU.mult, op1=ALU.add))
            step(V.tensor_tensor(ex[2][:, :], ex[1][:, :], ex[0][:, :], ALU.subtract))
            step(V.tensor_scalar(out=ex[3][:, :], in0=ex[2][:, :], scalar1=float(P), scalar2=-1.0, op0=ALU.mult, op1=ALU.add))
            step(V.tensor_tensor(et[0][:, :, :], et[2][:, :, :], ex[3][:, :].unsqueeze(2).to_broadcast([P, EXPERTS, PAIRS]), ALU.add))
            step(V.tensor_tensor(te[0][:, :, :], psc[:, 0:half].rearrange("p (i e) -> p i e", e=EXPERTS),
                                 et[0][:, :, :].rearrange("p e i -> p i e"), ALU.add))
            step(V.tensor_tensor(te[1][:, :, :], te[0][:, :, :], te[3][:, :, :], ALU.mult))
            step(V.tensor_reduce(out=tk[3][:, :], in_=te[1][:, :, :], axis=AX_X, op=ALU.add))
            V.tensor_copy(pos[:, :], tk[3][:, :]).then_inc(pos_ready, 1)
            step(V.tensor_tensor(tcmp[:, :, :], tilec[:, :, :], ex[1][:, :].unsqueeze(1).to_broadcast([P, SLOTS, EXPERTS]), ALU.is_ge))
            step(V.tensor_reduce(out=tsum[:, :], in_=tcmp[:, :, :], axis=AX_X, op=ALU.add))
            step(V.tensor_copy(expert[:, :], tsum[:, :]))


def layer2_sorted_linear(nc, sem, tag, src, dst, weights, expert, ident):
    M = dst.shape[1]
    HALVES = [(o, min(NT, M - o)) for o in range(0, M, NT)]
    XB = 8
    BUF = 2
    wsb, bsb, w_in, w_loaded, _ = weights
    with ExitStack() as ctx:
        def sb(name, shape, dt):
            return ctx.enter_context(nc.sbuf_tensor(tag + name, shape, dt))

        xs = sb("xs", [P, XB, C], F32)
        xsT = sb("xsT", [P, BUF, CC, P], F32)
        y = sb("y", [P, XB, M], F32)
        psT = ctx.enter_context(nc.psum_tensor(tag + "psT", [P, BUF, NT], F32))
        psY = ctx.enter_context(nc.psum_tensor(tag + "psY", [P, BUF, 2 * NT], F32))

        x_in = [sem(tag + f"_x_in{b}") for b in range(XB)]
        t_done = sem(tag + "_t")
        t_ready = sem(tag + "_t_ready")
        y_done = sem(tag + "_y")
        y_ready = sem(tag + "_y_ready")
        stored = [sem(tag + f"_stored{b}") for b in range(XB)]
        block = ctx.enter_context(nc.Block())
        ROUNDS = SLOTS // XB

        def rounds(engine, body):
            for b in range(XB):
                body(0, b, b)
            with engine.Fori(1, ROUNDS) as r:
                for b in range(XB):
                    body(r, b, r * XB + b)

        def again(j, n):
            return not isinstance(j, int) or j >= n

        @block.sync
        def _(sp):
            def load(b, row):
                sp.dma_start(xs[:, b, :], src[ds(row, P), :]).then_inc(x_in[b], 16)

            def store(b, j):
                sp.wait_ge(y_ready, j + 1)
                sp.dma_start(dst[ds(j * P, P), :], y[:, b, :]).then_inc(stored[b], 16)

            for b in range(XB):
                load(b, b * P)
            with sp.Fori(0, ROUNDS - 1) as r:
                for b in range(XB):
                    sp.wait_ge(t_done, r * XB + (b + 1))
                    load(b, r * (XB * P) + (XB + b) * P)
                    store(b, r * XB + b)
            for b in range(XB):
                store(b, SLOTS - XB + b)
            for b in range(XB):
                sp.wait_ge(stored[b], 16 * ROUNDS)

        @block.scalar
        def _(act):
            def body(r, b, j):
                act.wait_ge(t_done, j + 1)
                if again(j, BUF):
                    act.wait_ge(y_done, j - (BUF - 1))
                nc.scalar.activation(xsT[:, b % BUF, :, :].rearrange("p c n -> p (c n)"), psT[:, b % BUF, 0:C], ACT.Copy).then_inc(t_ready, 1)
            rounds(act, body)

        @block.tensor
        def _(pe):
            def transpose(r, b, j):
                pe.wait_ge(x_in[b], r * 16 + 16)
                if again(j, BUF):
                    pe.wait_ge(t_ready, j - (BUF - 1))
                for c in range(CC):
                    last = nc.tensor.transpose(psT[:, b % BUF, c * P:(c + 1) * P], xs[:, b, c * P:(c + 1) * P], ident)
                last.then_inc(t_done, 1)

            def multiply(b, j):
                off = nc.tensor.value_load(expert[0:1, ds(j, 1)], min_val=0, max_val=EXPERTS - 1) * M
                pe.wait_ge(t_ready, j + 1)
                if again(j, BUF):
                    pe.wait_ge(y_ready, j - (BUF - 1))
                for o, n in HALVES:
                    for c in range(CC):
                        last = nc.tensor.matmul(psY[:, b % BUF, o:o + n], xsT[:, b % BUF, c, :], wsb[:, c, ds(off + o, n)],
                                                start=(c == 0), stop=(c == CC - 1))
                last.then_inc(y_done, 1)

            transpose(0, 0, 0)
            transpose(0, 1, 1)
            pe.wait_ge(w_in, w_loaded)

            def body(r, b, j):
                multiply(b, j)
                after = b + BUF
                transpose(r + after // XB, after % XB, j + BUF)

            for b in range(XB):
                body(0, b, b)
            with pe.Fori(1, ROUNDS - 1) as r:
                for b in range(XB):
                    body(r, b, r * XB + b)
            for b in range(XB):
                j = SLOTS - XB + b
                if b + BUF < XB:
                    body(ROUNDS - 1, b, j)
                else:
                    multiply(b, j)

        @block.vector
        def _(dve):
            dve.wait_ge(w_in, w_loaded)

            def body(r, b, j):
                off = nc.vector.value_load(expert[0:1, ds(j, 1)], min_val=0, max_val=EXPERTS - 1) * M
                if again(j, XB):
                    dve.wait_ge(stored[b], r * 16)
                dve.wait_ge(y_done, j + 1)
                nc.vector.tensor_tensor(y[:, b, :], psY[:, b % BUF, 0:M], bsb[:, ds(off, M)], ALU.add).then_inc(y_ready, 1)
            rounds(dve, body)


def layer2_windows(nc, sem, pos, QKVs, Os, rope, ident, load_weights):
    SCALE = float(HD) ** -0.5
    HG = 4
    G = HEADS // HG
    WT = WIN * WIN
    VW = HD + 1
    RING = 6
    LAG = 6
    with ExitStack() as ctx:
        def sb(name, shape, dt):
            return ctx.enter_context(nc.sbuf_tensor(name, shape, dt))

        qkv = sb("qkv2", [P, RING, 3 * C], F32)
        tab = sb("tab2", [P, 2, 2 * C], F32)
        t1 = sb("t1", [P, 2, 2 * C], F32)
        t2 = sb("t2", [P, 2, 2 * C], F32)
        rqk = sb("rqk", [P, 2, 2 * C], F32)
        vx = sb("vx", [P, RING, HEADS, VW], F32)
        qT = sb("qT", [P, 2, G, P], F32)
        kT = sb("kT", [P, 2, G, HG, P], F32)
        mx = sb("mx", [P, 2, HEADS], F32)
        sh = sb("sh", [P, 2, HEADS, WT], F32)
        pb = sb("pb", [P, 2, HEADS, P], F32)
        pT = sb("pT", [P, 2, HEADS, P], F32)
        rs = sb("rs", [P, 2, HEADS], F32)
        ob = sb("ob", [P, RING, HEADS, HD], F32)
        psA = ctx.enter_context(nc.psum_tensor("psA", [P, NT], F32))
        psS = ctx.enter_context(nc.psum_tensor("psS", [P, 2, NT], F32))
        psP = ctx.enter_context(nc.psum_tensor("psP", [P, 2, 2, NT], F32))
        psO = ctx.enter_context(nc.psum_tensor("psO", [P, NT], F32))

        tab_in = sem("w2_tab_in")
        zeroed = sem("w2_zeroed")
        g_in = [sem(f"w2_gather{b}") for b in range(RING)]
        t1_done = sem("w2_t1")
        t2_done = sem("w2_t2")
        vx_ready = sem("w2_vx")
        r_ready = sem("w2_r")
        a_done = sem("w2_a")
        a_ready = sem("w2_a_ready")
        s_done = sem("w2_s")
        mx_done = sem("w2_mx")
        sh_ready = sem("w2_sh")
        e_ready = sem("w2_e")
        p_done = sem("w2_p")
        p_ready = sem("w2_p_ready")
        o_done = sem("w2_o")
        rs_done = sem("w2_rs")
        o_ready = sem("w2_o_ready")
        out_done = [sem(f"w2_out{b}") for b in range(RING)]
        block = ctx.enter_context(nc.Block())
        SLOT0, SLOT1 = 2 * RING + 2, PAIRS

        def slots(engine, body):
            def fixed(s):
                def tile(k):
                    i = s - k
                    return (i, i % RING, i // RING) if 0 <= i < PAIRS else None
                return tile
            for s in range(SLOT0):
                body(fixed(s))
            with engine.Fori(0, (SLOT1 - SLOT0) // RING) as r:
                for b in range(RING):
                    body(lambda k: (r * RING + (SLOT0 + b - k), (SLOT0 + b - k) % RING, r + (SLOT0 + b - k) // RING))
            for s in range(SLOT1, PAIRS + LAG):
                body(fixed(s))

        def again(i, n):
            return not isinstance(i, int) or i >= n

        @block.sync
        def _(sp):
            sp.dma_start(tab[:, :, :], rope).then_inc(tab_in, 16)
            load_weights(sp)

        @block.gpsimd
        def _(pool):
            nc.gpsimd.memset(pb[:, :, :, :].rearrange("p b h n -> p (b h n)"), 0.0).then_inc(zeroed, 1)
            nc.gpsimd.memset(kT[:, :, :, :, :].rearrange("p b g h n -> p (b g h n)"), 0.0).then_inc(zeroed, 1)
            nc.gpsimd.memset(vx[:, :, :, HD:VW].rearrange("p b h o -> p (b h o)"), 1.0).then_inc(zeroed, 1)
            pool.wait_ge(tab_in, 16)

            LATE = 1

            def gather(i):
                if i >= RING:
                    pool.wait_ge(t1_done, i - RING + 1)
                    pool.wait_ge(vx_ready, i - RING + 1)
                    pool.wait_ge(t2_done, 2 * (i - RING + 1))
                nc.gpsimd.indirect_dma_start(out=qkv[:, i % RING, :], out_offset=None, in_=QKVs,
                                             in_offset=bass.IndirectOffsetOnAxis(ap=pos[:, i:i + 1], axis=0)).then_inc(g_in[i % RING], 16)

            def scatter(i):
                pool.wait_ge(o_ready, i + 1)
                nc.gpsimd.indirect_dma_start(out=Os, out_offset=bass.IndirectOffsetOnAxis(ap=pos[:, i:i + 1], axis=0),
                                             in_=ob[:, i % RING, :, :].rearrange("p h d -> p (h d)"), in_offset=None).then_inc(out_done[i % RING], 16)

            def rotate(i):
                pool.wait_ge(g_in[i % RING], 16 * (i // RING + 1))
                if i >= 2:
                    pool.wait_ge(r_ready, i - 1)
                x = qkv[:, i % RING, 0:2 * C].rearrange("p (n two) -> p n two", two=2)
                s = tab[:, 1, :].rearrange("p (n two) -> p n two", two=2)
                o = t2[:, i % 2, :].rearrange("p (n two) -> p n two", two=2)
                nc.gpsimd.tensor_tensor(o[:, :, 0], x[:, :, 1], s[:, :, 0], ALU.mult).then_inc(t2_done, 1)
                nc.gpsimd.tensor_tensor(o[:, :, 1], x[:, :, 0], s[:, :, 1], ALU.mult).then_inc(t2_done, 1)

            for i in range(RING - 1):
                gather(i)
            rotate(0)
            for i in range(PAIRS + LAG + LATE):
                if i + 1 < PAIRS:
                    rotate(i + 1)
                if RING - 1 <= i + RING - 1 < PAIRS:
                    gather(i + RING - 1)
                if 0 <= i - LAG - LATE < PAIRS:
                    scatter(i - LAG - LATE)
            for b in range(RING):
                pool.wait_ge(out_done[b], 16 * len(range(b, PAIRS, RING)))

        @block.vector
        def _(dve):
            def rope1(i, b, r):
                dve.wait_ge(g_in[b], r * 16 + 16)
                nc.vector.tensor_tensor(t1[:, b % 2, :], qkv[:, b, 0:2 * C], tab[:, 0, :], ALU.mult).then_inc(t1_done, 1)

            def rope2(i, b, r):
                dve.wait_ge(t1_done, i + 1)
                if again(i, 2):
                    dve.wait_ge(a_done, i - 1)
                dve.wait_ge(t2_done, i * 2 + 2)
                nc.vector.tensor_tensor(rqk[:, b % 2, :], t1[:, b % 2, :], t2[:, b % 2, :], ALU.add).then_inc(r_ready, 1)

            def maximum(i, b, r):
                S = psS[:, b % 2, :].rearrange("p (h m) -> p h m", m=WT)
                dve.wait_ge(s_done, i + 1)
                nc.vector.tensor_reduce(out=mx[:, b % 2, :], in_=S, axis=AX_X, op=ALU.max).then_inc(mx_done, 1)

            def shift(i, b, r):
                S = psS[:, b % 2, :].rearrange("p (h m) -> p h m", m=WT)
                if again(i, 2):
                    dve.wait_ge(e_ready, i - 1)
                dve.wait_ge(mx_done, i + 1)
                nc.vector.tensor_tensor(sh[:, b % 2, :, :], S, mx[:, b % 2, :].unsqueeze(2).to_broadcast([P, HEADS, WT]), ALU.subtract).then_inc(sh_ready, 1)

            def invert(i, b, r):
                O = psO[:, 0:HEADS * VW].rearrange("p (h d) -> p h d", d=VW)
                dve.wait_ge(o_done, i + 1)
                nc.vector.reciprocal(rs[:, b % 2, :], O[:, :, HD]).then_inc(rs_done, 1)

            def normalise(i, b, r):
                O = psO[:, 0:HEADS * VW].rearrange("p (h d) -> p h d", d=VW)
                if again(i, RING):
                    dve.wait_ge(out_done[b], r * 16)
                dve.wait_ge(rs_done, i + 1)
                nc.vector.tensor_tensor(ob[:, b, :, :], O[:, :, 0:HD], rs[:, b % 2, :].unsqueeze(2).to_broadcast([P, HEADS, HD]), ALU.mult).then_inc(o_ready, 1)

            dve.wait_ge(tab_in, 16)

            def body(tile):
                for k, stage in ((0, rope1), (6, invert), (0, rope2), (6, normalise), (2, maximum), (2, shift)):
                    if tile(k) is not None:
                        stage(*tile(k))
            slots(dve, body)

        @block.scalar
        def _(act):
            def spread(i, b, r):
                act.wait_ge(a_done, i + 1)
                if again(i, 2):
                    act.wait_ge(s_done, i - 1)
                A = psA[:, :].rearrange("p (s n) -> p s n", n=P)
                nc.scalar.activation(qT[:, b % 2, :, :], A[:, 0:G, :], ACT.Copy)
                for h in range(HG):
                    on = slice(h * HD, (h + 1) * HD)
                    last = nc.scalar.activation(kT[on, b % 2, :, h, :], A[on, G:2 * G, :], ACT.Copy)
                last.then_inc(a_ready, 1)

            def place_v(i, b, r):
                act.wait_ge(g_in[b], r * 16 + 16)
                if again(i, RING):
                    act.wait_ge(o_done, i - (RING - 1))
                nc.scalar.activation(vx[:, b, :, 0:HD], qkv[:, b, 2 * C:3 * C].rearrange("p (h d) -> p h d", d=HD), ACT.Copy).then_inc(vx_ready, 1)

            def exponent(i, b, r):
                act.wait_ge(sh_ready, i + 1)
                if again(i, 2):
                    act.wait_ge(p_done, i - 1)
                for w in range(2):
                    on = slice(w * WT, (w + 1) * WT)
                    last = nc.scalar.activation(pb[on, b % 2, :, w * WT:(w + 1) * WT], sh[on, b % 2, :, :], ACT.Exp, scale=SCALE)
                last.then_inc(e_ready, 1)

            def evacuate(i, b, r):
                if again(i, 2):
                    act.wait_ge(o_done, i - 1)
                act.wait_ge(p_done, i + 1)
                nc.scalar.activation(pT[:, b % 2, :, :].rearrange("p h n -> p (h n)"), psP[:, b % 2, :, :].rearrange("p k n -> p (k n)"),
                                     ACT.Copy).then_inc(p_ready, 1)

            act.wait_ge(zeroed, 3)

            def body(tile):
                for k, stage in ((4, evacuate), (0, spread), (2, exponent), (0, place_v)):
                    if tile(k) is not None:
                        stage(*tile(k))
            slots(act, body)

        @block.tensor
        def _(pe):
            def transpose_qk(i, b, r):
                pe.wait_ge(r_ready, i + 1)
                if again(i, 1):
                    pe.wait_ge(a_ready, i)
                for q in range(2 * G):
                    last = nc.tensor.transpose(psA[:, q * P:(q + 1) * P], rqk[:, b % 2, q * P:(q + 1) * P], ident)
                last.then_inc(a_done, 1)

            def scores(i, b, r):
                pe.wait_ge(a_ready, i + 1)
                if again(i, 2):
                    pe.wait_ge(sh_ready, i - 1)
                for g in range(G):
                    for w in range(2):
                        on = slice(w * WT, (w + 1) * WT)
                        last = nc.tensor.matmul(psS[on, b % 2, g * HG * WT:(g + 1) * HG * WT], qT[:, b % 2, g, on], kT[:, b % 2, g, :, on],
                                                start=True, stop=True)
                last.then_inc(s_done, 1)

            def transpose_p(i, b, r):
                pe.wait_ge(e_ready, i + 1)
                if again(i, 2):
                    pe.wait_ge(p_ready, i - 1)
                for h in range(HEADS):
                    last = nc.tensor.transpose(psP[:, b % 2, h // HG, h % HG * P:(h % HG + 1) * P], pb[:, b % 2, h, :], ident)
                last.then_inc(p_done, 1)

            def values(i, b, r):
                pe.wait_ge(p_ready, i + 1)
                pe.wait_ge(vx_ready, i + 1)
                if again(i, 1):
                    pe.wait_ge(o_ready, i)
                for h in range(HEADS):
                    last = nc.tensor.matmul(psO[:, h * VW:(h + 1) * VW], pT[:, b % 2, h, :], vx[:, b, h, :], start=True, stop=True)
                last.then_inc(o_done, 1)

            pe.wait_ge(zeroed, 3)

            def body(tile):
                for k, stage in ((6, values), (4, transpose_p), (2, scores), (0, transpose_qk)):
                    if tile(k) is not None:
                        stage(*tile(k))
            slots(pe, body)


def layer2_combine(nc, sem, X, pos, pmax, Ps, ident, stats):
    RING = 4
    with ExitStack() as ctx:
        g = ctx.enter_context(nc.sbuf_tensor("g2", [P, RING, C], F32))
        gs = ctx.enter_context(nc.sbuf_tensor("gs2", [P, RING, C], F32))
        ps = ctx.enter_context(nc.psum_tensor("psg", [P, RING, NT], F32))
        g_in = [sem(f"c2_in{b}") for b in range(RING)]
        s_ready = sem("c2_scaled")
        t_done = sem("c2_t")
        x_done = sem("c2_x")
        stats_done = sem("c2_stats")
        block = ctx.enter_context(nc.Block())

        @block.gpsimd
        def _(pool):
            for i in range(PAIRS):
                if i >= RING:
                    pool.wait_ge(s_ready, i - RING + 1)
                nc.gpsimd.indirect_dma_start(out=g[:, i % RING, :], out_offset=None, in_=Ps,
                                             in_offset=bass.IndirectOffsetOnAxis(ap=pos[:, i:i + 1], axis=0)).then_inc(g_in[i % RING], 16)

        @block.scalar
        def _(act):
            for i in range(PAIRS):
                act.wait_ge(g_in[i % RING], 16 * (i // RING + 1))
                if i >= RING:
                    act.wait_ge(t_done, i - RING + 1)
                nc.scalar.activation(gs[:, i % RING, :], g[:, i % RING, :], ACT.Copy, scale=pmax[:, i:i + 1]).then_inc(s_ready, 1)

        @block.tensor
        def _(pe):
            for i in range(PAIRS):
                pe.wait_ge(s_ready, i + 1)
                if i >= RING:
                    pe.wait_ge(x_done, CC * (i - RING + 1))
                for c in range(CC):
                    last = nc.tensor.transpose(ps[:, i % RING, c * P:(c + 1) * P], gs[:, i % RING, c * P:(c + 1) * P], ident)
                last.then_inc(t_done, 1)

        @block.vector
        def _(dve):
            per = NT // P

            def next_stats(t):
                dve.wait_ge(x_done, (t + 1) * per * CC)
                for c in range(CC):
                    tile_statistics(nc, X, stats, c, t).then_inc(stats_done, 1)

            for i in range(PAIRS):
                dve.wait_ge(t_done, i + 1)
                for c in range(CC):
                    x = by_window(X[:, c, i // per * NT:(i // per + 1) * NT])[:, 2 * (i % per):2 * (i % per) + 2, :, :]
                    nc.vector.tensor_tensor(x, ps[:, i % RING, c * P:(c + 1) * P].rearrange("p (w r c) -> p w r c", r=WIN, c=WIN), x,
                                            ALU.add).then_inc(x_done, 1)
                if i % per == 0 and i:
                    next_stats(i // per - 1)
            next_stats(TILES - 1)
            dve.wait_ge(stats_done, TILES * CC)


def layer3_chain(nc, sem, X, w1, b1, w2, b2, w3row, w3col, b3, ident, group_avg, eps_col, stats, out):
    EX = w1.shape[1]
    ROUNDS = C // EX
    PW = W + 2
    HALF = TILES // 2
    with ExitStack() as ctx:
        def sb(name, shape, dt):
            return ctx.enter_context(nc.sbuf_tensor(name, shape, dt))

        xn = sb("xn3", [P, CC, N], F32)
        A = sb("A3", [P, CC, N], F32)
        B0 = sb("B0", [P, PW, PW], F32)
        B1 = sb("B1", [P, PW, PW], F32)
        B2 = sb("B2", [P, PW, PW], F32)
        S2 = sb("S2", [P, HALF, NT], F32)
        U = sb("U3", [P, HALF, NT], F32)
        w1s = sb("w1s", [P, CC, EX], F32)
        w2s = sb("w2s", [P, CC, 9, EX], F32)
        b12 = sb("b12", [P, 2], F32)
        w3r = sb("w3r", [P, C], F32)
        w3c = sb("w3c", [P, CC], F32)
        b3c = sb("b3c", [P, 1], F32)
        grow = sb("grow", [P, C], F32)
        step = sb("step3", [P, CC + 1, C], F32)
        MT3 = sb("MT3", [P, CC + 1, C], F32)
        ccol = sb("ccol", [P, CC], F32)
        one = sb("one3", [1, 1], F32)
        aggr = sb("aggr3", [P, CC, 2], F32)
        cols = sb("cols3", [P, 8, 2], F32)
        banks = [ctx.enter_context(nc.psum_tensor(f"bank3_{i}", [P, NT], F32)) for i in range(7)]
        ps = ctx.enter_context(nc.psum_tensor("ps3", [P, NT], F32))

        w_in = sem("l3_w_in")
        pads_zero = sem("l3_pads")
        xn_ready = sem("l3_xn")
        a0_ready = sem("l3_a0")
        y_ready = sem("l3_y")
        pair_done = sem("l3_pairs")
        a_ready = sem("l3_a")
        relu_done = sem("l3_relu")
        z_ready = sem("l3_z")
        u_ready = sem("l3_u")
        z_copied = sem("l3_z_copied")
        mat_step = sem("l3_mat")
        col_done = sem("l3_col")
        ccol_ready = sem("l3_ccol")
        last_relu = sem("l3_last_relu")
        m_done = sem("l3_m")
        o_ready = sem("l3_out_ready")
        x_out = sem("l3_x_out")
        gn_vec, gn_pe, gn_act, gn_wait = group_norm_stats(nc, "gn3", sem, X, stats, aggr, group_avg, ps, cols, early=True)
        block = ctx.enter_context(nc.Block())
        LOADS = 10
        MAT_STEPS = 11
        STAGES = [(B2, 1), (B0, 0), (B1, 0), (B0, 0), (B2, 1)]

        def lanes(h):
            return slice(h * EX, (h + 1) * EX)

        def rows(B, half, t):
            return B[lanes(half), 1 + t * TR:1 + (t + 1) * TR, 1:1 + W]

        def as_rows(ap):
            return ap.rearrange("p (h w) -> p h w", w=W)

        def pairs(stage, j):
            return (ROUNDS + stage) * HALF + j + 1

        @block.sync
        def _(sp):
            loads = [(w1s[:, :, :], w1.rearrange("(c p) m -> p c m", p=P))]
            loads += [(w2s[:, c, :, :], w2[:, c * P:(c + 1) * P, :].rearrange("t p m -> p t m")) for c in range(CC)]
            for h in range(2):
                loads += [(b12[lanes(h), 0:1], b1), (b12[lanes(h), 1:2], b2)]
            loads += [(w3r[:, :], w3row), (w3c[:, :], w3col), (b3c[:, :], b3)]
            assert len(loads) == LOADS
            for dst, src in loads:
                sp.dma_start(dst, src).then_inc(w_in, 16)
            for t in range(TILES):
                sp.wait_ge(o_ready, (t + 1) * CC)
                for c in range(CC):
                    sp.dma_start(out[c * P:(c + 1) * P, t * NT:(t + 1) * NT], X[:, c, t * NT:(t + 1) * NT]).then_inc(x_out, 16)
            sp.wait_ge(x_out, 16 * CC * TILES)

        @block.gpsimd
        def _(pool):
            for B in (B0, B1, B2):
                nc.gpsimd.memset(B[:, :, :].rearrange("p h w -> p (h w)"), 0.0).then_inc(pads_zero, 1)
            nc.gpsimd.memset(one[:, :], 1.0).then_inc(pads_zero, 1)
            for c in range(CC):
                for h in range(2):
                    part = slice(h * (N // 2), (h + 1) * (N // 2))
                    pool.wait_ge(xn_ready, CC * c + h + 1)
                    if c == 0 and h == 0:
                        pool.wait_ge(a0_ready, CC)
                    nc.gpsimd.tensor_tensor(X[:, c, part], X[:, c, part], xn[:, c, part], ALU.add).then_inc(y_ready, 1)
            for t in range(TILES):
                pool.wait_ge(z_ready, TILES + t + 1)
                pool.wait_ge(pair_done, pairs(1, min((t + 1) // 2, HALF - 1)))
                nc.gpsimd.tensor_copy(rows(B0, 0, t), rows(B1, 0, t)).then_inc(z_copied, 1)

        @block.scalar
        def _(act):
            gn_act(act, eps_col)
            gn_wait(act)
            act.wait_ge(w_in, 16 * LOADS)
            for c in range(CC):
                for h in range(2):
                    part = slice(h * (N // 2), (h + 1) * (N // 2))
                    nc.scalar.activation(xn[:, c, part], X[:, c, part], ACT.Identity, scale=cols[:, 0, c:c + 1],
                                         bias=cols[:, 1, c:c + 1]).then_inc(xn_ready, 1)
            for i in range(ROUNDS):
                for j in range(HALF):
                    act.wait_ge(pair_done, i * HALF + j + 1)
                    for h in range(2):
                        t = 2 * j + h
                        nc.scalar.activation(A[lanes(i % 2), i // 2, t * NT:(t + 1) * NT], banks[j][lanes(h), :], ACT.Identity,
                                             bias=b12[lanes(h), 0:1]).then_inc(a_ready, 1)
            for t in range(TILES):
                part = slice(t * NT, (t + 1) * NT)
                act.wait_ge(z_ready, 3 * TILES + t + 1)
                act.wait_ge(z_copied, t + 1)
                nc.scalar.activation(as_rows(A[:, 0, part]), B0[:, 1 + t * TR:1 + (t + 1) * TR, 1:1 + W], ACT.Relu).then_inc(last_relu, 1)
                nc.scalar.activation(as_rows(A[lanes(0), 1, part]), rows(B2, 0, t), ACT.Relu).then_inc(last_relu, 1)
            for t in range(TILES):
                part = slice(t * NT, (t + 1) * NT)
                act.wait_ge(z_ready, 4 * TILES + t + 1)
                nc.scalar.activation(A[lanes(1), 1, part], A[lanes(1), 1, part], ACT.Relu).then_inc(last_relu, 1)

        @block.tensor
        def _(pe):
            gn_pe(pe)
            pe.wait_ge(w_in, 16 * LOADS)
            pe.wait_ge(a0_ready, CC)
            for i in range(ROUNDS):
                for j in range(HALF):
                    if i:
                        pe.wait_ge(a_ready, (i - 1) * TILES + 2 * j + 2)
                    for c in range(CC):
                        for h in range(2):
                            t = 2 * j + h
                            last = nc.tensor.matmul(banks[j][lanes(h), :], w1s[:, c, :], A[:, c, t * NT:(t + 1) * NT],
                                                    start=(c == 0), stop=(c == CC - 1))
                    last.then_inc(pair_done, 1)
            pe.wait_ge(mat_step, MAT_STEPS)
            pe.wait_ge(pads_zero, 4)
            for c in range(CC):
                last = nc.tensor.matmul(ps[:, c:c + 1], MT3[0:1, CC, c * P:(c + 1) * P], one[0:1, 0:1], start=True, stop=True)
            last.then_inc(col_done, 1)
            pe.wait_ge(a_ready, ROUNDS * TILES)
            for s, (B, c) in enumerate(STAGES):
                for j in range(HALF):
                    reads = min(2 * j + 3, TILES)
                    if s < 2:
                        pe.wait_ge(relu_done, 3 * reads)
                    if s > 0:
                        pe.wait_ge(z_ready, (s - 1) * TILES + (reads if s > 1 else 2 * j + 2))
                    if s == 3:
                        pe.wait_ge(z_copied, reads)
                    for tap in range(9):
                        dy, dx = divmod(tap, 3)
                        for h in range(2):
                            t = 2 * j + h
                            last = nc.tensor.matmul(banks[j][lanes(h), :], w2s[:, c, tap, :],
                                                    B[:, t * TR + dy:t * TR + dy + TR, dx:dx + W],
                                                    start=(tap == 0), stop=(tap == 8))
                    last.then_inc(pair_done, 1)
            for t in range(TILES):
                pe.wait_ge(last_relu, 2 * TILES + t + 1)
                for o in range(CC):
                    r = t * CC + o
                    if r >= 3:
                        pe.wait_ge(o_ready, r - 2)
                    for c in range(CC):
                        last = nc.tensor.matmul(banks[4 + r % 3][:, :], MT3[:, c, o * P:(o + 1) * P], A[:, c, t * NT:(t + 1) * NT],
                                                start=(c == 0), stop=(c == CC - 1))
                    last.then_inc(m_done, 1)

        @block.vector
        def _(dve):
            gn_vec(dve)
            for c in range(CC):
                nc.vector.tensor_scalar(out=A[:, c, :], in0=X[:, c, :], scalar1=cols[:, 0, c:c + 1], scalar2=cols[:, 1, c:c + 1],
                                        op0=ALU.mult, op1=ALU.add).then_inc(a0_ready, 1)
            dve.wait_ge(w_in, 16 * LOADS)
            chain = Chain(dve, mat_step)
            chain.done(nc.vector.tensor_scalar(out=grow[:, :], in0=w3r[:, :], scalar1=1.0, scalar2=None, op0=ALU.add))
            chain.done(nc.vector.memset(step[:, :, :], 0.0))
            chain.wait()
            for c in range(CC):
                part = slice(c * P, (c + 1) * P)
                chain.done(nc.vector.scalar_tensor_tensor(out=step[:, c, part], in0=ident, scalar=-1.0, in1=w3r[:, part],
                                                          op0=ALU.mult, op1=ALU.mult))
            chain.done(nc.vector.tensor_scalar(out=step[:, CC, :], in0=w3r[:, :], scalar1=b3c[:, 0:1], scalar2=None, op0=ALU.mult))
            chain.done(nc.vector.tensor_copy(MT3[:, 0:CC, 0], w3c[:, :]))
            chain.done(nc.vector.memset(MT3[:, CC, 0:1], 0.0))
            chain.wait()
            for c in range(CC + 1):
                chain.done(nc.vector.tensor_tensor_scan(out=MT3[:, c, 1:C], data0=grow[:, 0:C - 1], data1=step[:, c, 0:C - 1],
                                                        initial=w3c[:, c:c + 1] if c < CC else 0.0, op0=ALU.mult, op1=ALU.add))
            chain.wait()
            chain.done(nc.vector.tensor_scalar(out=MT3[:, CC, :], in0=MT3[:, CC, :], scalar1=b3c[:, 0:1], scalar2=None, op0=ALU.add))
            assert chain.n == MAT_STEPS
            dve.wait_ge(pads_zero, 3)
            for t in range(TILES):
                part = slice(t * NT, (t + 1) * NT)
                dve.wait_ge(a_ready, (ROUNDS - 1) * TILES + t + 1)
                for dst, src in ((B0[:, 1 + t * TR:1 + (t + 1) * TR, 1:1 + W], A[:, 0, part]),
                                 (B2[:, 1 + t * TR:1 + (t + 1) * TR, 1:1 + W], A[:, 1, part]),
                                 (rows(B1, 1, t), A[lanes(1), 0, part])):
                    nc.vector.tensor_scalar(out=dst, in0=as_rows(src), scalar1=0.0, scalar2=None, op0=ALU.max).then_inc(relu_done, 1)
            dve.wait_ge(col_done, 1)
            nc.vector.tensor_copy(ccol[:, :], ps[:, 0:CC]).then_inc(ccol_ready, 1)

            def biased(dst, t, share):
                j, h = divmod(t, 2)
                nc.vector.scalar_tensor_tensor(out=dst, in0=as_rows(banks[j][lanes(h), :]), scalar=b12[lanes(h), 1:2],
                                               in1=as_rows(share[lanes(h), j, :]), op0=ALU.add, op1=ALU.add).then_inc(z_ready, 1)

            for s in range(len(STAGES)):
                for t in range(TILES):
                    j, h = divmod(t, 2)
                    dve.wait_ge(pair_done, pairs(s, j))
                    if s == 0:
                        nc.vector.tensor_copy(S2[lanes(h), j, :], banks[j][lanes(h), :]).then_inc(z_ready, 1)
                    elif s == 1:
                        dve.wait_ge(z_ready, t + 1)
                        biased(rows(B1, 0, t), t, S2)
                    elif s == 2:
                        biased(rows(B0, 1, t), t, S2)
                    elif s == 3:
                        nc.vector.tensor_copy(U[lanes(h), j, :], banks[j][lanes(h), :]).then_inc(u_ready, 1)
                        biased(rows(B2, 0, t), t, S2)
                    else:
                        dve.wait_ge(u_ready, t + 1)
                        biased(as_rows(A[lanes(1), 1, t * NT:(t + 1) * NT]), t, U)
            dve.wait_ge(y_ready, 2 * CC)
            dve.wait_ge(ccol_ready, 1)
            for t in range(TILES):
                for o in range(CC):
                    r = t * CC + o
                    xt = X[:, o, t * NT:(t + 1) * NT]
                    dve.wait_ge(m_done, r + 1)
                    nc.vector.scalar_tensor_tensor(out=xt, in0=banks[4 + r % 3][:, :], scalar=ccol[:, o:o + 1], in1=xt,
                                                   op0=ALU.add, op1=ALU.add).then_inc(o_ready, 1)


def build(nc, a, out):
    with ExitStack() as ctx:
        def sem(name):
            return nc.alloc_semaphore(name=name)

        X = ctx.enter_context(nc.sbuf_tensor("X", [P, CC, N], F32))
        consts = ctx.enter_context(nc.sbuf_tensor("consts", [P, 3, P], F32))
        pos = ctx.enter_context(nc.sbuf_tensor("pos", [P, PAIRS], U32))
        pmax = ctx.enter_context(nc.sbuf_tensor("pmax", [P, PAIRS], F32))
        expert = ctx.enter_context(nc.sbuf_tensor("expert", [P, SLOTS], U32))
        stats = ctx.enter_context(nc.sbuf_tensor("stats", [P, CC, TILES, 6], F32))
        eps = ctx.enter_context(nc.sbuf_tensor("eps", [P, 1], F32))
        Qhl = nc.dram_tensor("q_parts", [2, C, N], F16).ap()
        Xs = nc.dram_tensor("tokens_by_expert", [SLOTS * P, C], F32).ap()
        QKVs = nc.dram_tensor("qkv_by_expert", [SLOTS * P, 3 * C], F32).ap()
        Os = nc.dram_tensor("attended_by_expert", [SLOTS * P, C], F32).ap()
        Ps = nc.dram_tensor("projected_by_expert", [SLOTS * P, C], F32).ap()
        Khl = nc.dram_tensor("k_parts", [2, C, N], F16).ap()
        consts_in = sem("consts_in")
        eps_set = sem("eps_set")
        with nc.Block() as block:
            @block.sync
            def _(sp):
                sp.dma_start(consts[:, :, :], a["consts"]).then_inc(consts_in, 16)
                sp.wait_ge(consts_in, 16)

            @block.vector
            def _(dve):
                nc.vector.memset(eps[:, :], GN_EPS).then_inc(eps_set, 1)
                dve.wait_ge(eps_set, 1)
        ident, ones_head, group_avg = consts[:, 0, :], consts[:, 1, :], consts[:, 2, :]
        with nc.cleanup_on_exit():
            layer0_conv(nc, sem, X, a["x"], (a["L0_conv_W1"], a["L0_conv_W3"], a["L0_conv_W5"]), a["L0_conv_Wdw"],
                        a["temp"], ones_head, group_avg, eps[:, 0:1], stats, Qhl, Khl, consts_in)
        with nc.cleanup_on_exit():
            layer0_attention(nc, sem, X, a["x"], Qhl, Khl, a["L0_conv_Wproj"], ident, stats)
        with nc.cleanup_on_exit():
            layer1_codebook(nc, sem, X, Xs, Os, a["codes"], a["codes_t"], ident, group_avg, eps[:, 0:1], stats)
        with nc.cleanup_on_exit(), ExitStack() as stage:
            weights = expert_weights(nc, stage, sem, "qkv", a["qkv_w"], a["qkv_b"])
            layer2_route(nc, sem, X, a["rw1"], a["rb1"], a["rw2"], a["rb2"], a, ident, group_avg, eps[:, 0:1], stats,
                         pos, pmax, expert, Xs, weights[-1])
            layer2_sorted_linear(nc, sem, "qkv", Xs, QKVs, weights, expert, ident)
        with nc.cleanup_on_exit(), ExitStack() as stage:
            weights = expert_weights(nc, stage, sem, "proj", a["proj_w"], a["proj_b"])
            layer2_windows(nc, sem, pos, QKVs, Os, a["rope"], ident, weights[-1])
            layer2_sorted_linear(nc, sem, "proj", Os, Ps, weights, expert, ident)
        with nc.cleanup_on_exit():
            layer2_combine(nc, sem, X, pos, pmax, Ps, ident, stats)
            layer3_chain(nc, sem, X, a["w1"], a["b1"], a["w2"], a["b2"], a["w3row"], a["w3col"], a["b3"], ident, group_avg, eps[:, 0:1], stats, out)


def kernel(**inputs):
    import numpy as np
    import concourse.bacc as bacc
    from concourse.bass_utils import run_bass_kernel_spmd

    a = {name: np.asarray(value) for name, value in inputs.items()}
    arrays = {
        "x": a["x"].reshape(N, C).T,
        "L0_conv_W1": a["L0_conv_W1"].reshape(C, C, 1).transpose(1, 2, 0),
        "L0_conv_W3": a["L0_conv_W3"].reshape(C, C, 9).transpose(1, 2, 0),
        "L0_conv_W5": a["L0_conv_W5"].reshape(C, C, 25).transpose(1, 2, 0),
        "L0_conv_Wdw": a["L0_conv_Wdw"].reshape(3 * C, 9),
        "L0_conv_Wproj": a["L0_conv_Wproj"].reshape(C, C).T,
        "temp": np.repeat(a["L0_conv_temperature"].reshape(HEADS), HD).reshape(CC, P).T,
        "rw1": a["L2_conv_router_w1"].T,
        "rb1": a["L2_conv_router_b1"].reshape(-1, 1),
        "rw2": a["L2_conv_router_w2"].T,
        "rb2": a["L2_conv_router_b2"].reshape(1, -1),
        "qkv_w": a["L2_conv_qkv_w"].reshape(EXPERTS * 3 * C, C).T,
        "qkv_b": a["L2_conv_qkv_b"].reshape(-1),
        "proj_w": a["L2_conv_proj_w"].reshape(EXPERTS * C, C).T,
        "proj_b": a["L2_conv_proj_b"].reshape(-1),
        "w1": a["L3_conv_w1"].reshape(C, -1),
        "b1": a["L3_conv_b1"].reshape(-1, 1),
        "w2": a["L3_conv_w2"].reshape(9, C, -1),
        "b2": a["L3_conv_b2"].reshape(-1, 1),
        "w3row": np.broadcast_to(a["L3_conv_w3"].reshape(1, C), (P, C)),
        "w3col": a["L3_conv_w3"].reshape(CC, P).T,
        "b3": np.broadcast_to(a["L3_conv_b3"].reshape(1, 1), (P, 1)),
        "codes": a["L1_conv_embeddings"],
        "codes_t": a["L1_conv_embeddings"].T,
    }
    p = np.arange(P)
    same = lambda w: (p[:, None] // w == p[None, :] // w)
    arrays["consts"] = np.stack([np.eye(P), same(HD), same(C // 32) / (C // 32)], axis=1).astype(np.float32)
    arrays["tri"] = np.stack([p[:, None] <= p[None, :], np.ones((P, P))], axis=1).astype(np.float32)
    arrays["iota"] = np.broadcast_to(np.arange(EXPERTS, dtype=np.float32) + EXPERTS, (P, PAIRS, EXPERTS))
    tile = np.where(np.arange(EXPERTS) < EXPERTS - 1, np.arange(SLOTS)[:, None], -1)
    arrays["tile"] = np.broadcast_to(tile.astype(np.float32), (P, SLOTS, EXPERTS))
    half = HD // 2
    inv = (1.0 / 10000.0 ** (np.arange(0, half, 2, dtype=np.float32) / np.float32(half))).astype(np.float32)
    row, col = p // WIN % WIN, p % WIN
    ang = np.concatenate([row[:, None].astype(np.float32) * inv, col[:, None].astype(np.float32) * inv], axis=1)
    cos = np.repeat(np.cos(ang), 2, axis=1)
    sin = np.repeat(np.sin(ang), 2, axis=1) * np.where(np.arange(HD) % 2, 1, -1)
    arrays["rope"] = np.stack([np.tile(cos, 2 * HEADS), np.tile(sin, 2 * HEADS)], axis=1).astype(np.float32)
    arrays = {name: np.ascontiguousarray(value) for name, value in arrays.items()}
    nc = bacc.Bacc("TRN2", target_bir_lowering=False, num_devices=1)
    args = {name: nc.dram_tensor(name + "_dram", v.shape, mybir.dt.from_np(v.dtype), kind="ExternalInput").ap()
            for name, v in arrays.items()}
    out = nc.dram_tensor("out_dram", (C, N), F32, kind="ExternalOutput").ap()
    build(nc, args, out)
    r = run_bass_kernel_spmd(nc, [{name + "_dram": v for name, v in arrays.items()}], core_ids=[0])
    return r.results[0]["out_dram"].T.reshape(1, H, W, C)
```
